# Optimizing a Trainium2 kernel written in Bass

```python
import numpy as np
import jax
import jax.numpy as jnp

def _softmax(x, axis=-1):
    return jax.nn.softmax(x, axis=axis)

def _gelu(x):
    return jax.nn.gelu(x, approximate=True)

def _silu(x):
    return jax.nn.silu(x)

def _sigmoid(x):
    return jax.nn.sigmoid(x)

def _layernorm(x, axis=-1, eps=1e-05):
    m = jnp.mean(x, axis=axis, keepdims=True)
    v = jnp.var(x, axis=axis, keepdims=True)
    return (x - m) / jnp.sqrt(v + eps)

def _scatter_add(tgt, idx, src, axis=0):
    return tgt.at[idx].add(src)

def _segment_sum(src, seg, n):
    return jax.ops.segment_sum(src, seg, n)
kernel_name = 'mk_seq_postln_d2_jaxref_r8_6c1e16'

def setup_inputs(seed: int=0):
    np.random.seed(seed)
    _w = jnp.asarray

    def _L0_attn_setup():
        import jax, jax.numpy as jnp
        import numpy as np
        import math
        D_MODEL = 256
        D_STATE = 16
        EXPAND = 2
        D_INNER = D_MODEL * EXPAND
        DT_RANK = math.ceil(D_MODEL / 16)
        BATCH, SEQ_LEN = (2, 64)
        key = jax.random.key(seed)
        ks = jax.random.split(key, 6)
        x = jax.random.normal(ks[0], (BATCH, SEQ_LEN, D_INNER), dtype=jnp.float32)
        A_log = jnp.log(jax.random.uniform(ks[1], (D_INNER, D_STATE), minval=0.5, maxval=16.0, dtype=jnp.float32))
        D = jnp.ones((D_INNER,), dtype=jnp.float32)
        x_proj_w = 0.02 * jax.random.normal(ks[2], (DT_RANK + 2 * D_STATE, D_INNER), dtype=jnp.float32)
        dt_init_std = DT_RANK ** (-0.5)
        dt_proj_w = jax.random.uniform(ks[3], (D_INNER, DT_RANK), minval=-dt_init_std, maxval=dt_init_std, dtype=jnp.float32)
        dt = jnp.exp(jax.random.uniform(ks[4], (D_INNER,), dtype=jnp.float32) * (math.log(0.1) - math.log(0.001)) + math.log(0.001))
        dt = jnp.clip(dt, 0.0001, None)
        dt_proj_b = dt + jnp.log(-jnp.expm1(-dt))
        return {'x': x, 'A_log': A_log, 'D': D, 'x_proj_w': x_proj_w, 'dt_proj_w': dt_proj_w, 'dt_proj_b': dt_proj_b}
    _L0_attn_in = _L0_attn_setup()

    def _L0_ffn_setup():
        import jax, jax.numpy as jnp
        import numpy as np
        DIM = 512
        INTER = 128
        E = 16
        GROUPS = 4
        LIM = 2
        K = 2
        SHARED_INTER = 2 * INTER
        SCALE = 1.0
        key = jax.random.key(seed)
        ks = jax.random.split(key, 16)

        def n(k, shape, s=0.02):
            return jax.random.normal(k, shape, jnp.float32) * s
        return {'x': jax.random.normal(ks[0], (1, 256, DIM), jnp.float32), 'router_w': n(ks[1], (DIM, E)), 'router_b': n(ks[2], (E,)), 'router_bias': n(ks[3], (E,), 1.0), 'ew1': n(ks[4], (E, DIM, INTER)), 'eb1': n(ks[5], (E, INTER)), 'ew2': n(ks[6], (E, DIM, INTER)), 'eb2': n(ks[7], (E, INTER)), 'ew3': n(ks[8], (E, INTER, DIM)), 'eb3': n(ks[9], (E, DIM)), 'sw1': n(ks[10], (DIM, SHARED_INTER)), 'sb1': n(ks[11], (SHARED_INTER,)), 'sw2': n(ks[12], (DIM, SHARED_INTER)), 'sb2': n(ks[13], (SHARED_INTER,)), 'sw3': n(ks[14], (SHARED_INTER, DIM)), 'sb3': n(ks[15], (DIM,))}
    _L0_ffn_in = _L0_ffn_setup()

    def _L1_attn_setup():
        import jax, jax.numpy as jnp
        import numpy as np
        HIDDEN = 512
        HEADS = 32
        D_K = HIDDEN // HEADS
        key = jax.random.key(seed)
        ks = jax.random.split(key, 5)
        scale = 1.0 / np.sqrt(HIDDEN)
        x = jax.random.normal(ks[0], (2, 256, HIDDEN), dtype=jnp.float32)
        w_q = jax.random.uniform(ks[1], (HIDDEN, HIDDEN), jnp.float32, -scale, scale)
        w_k = jax.random.uniform(ks[2], (HIDDEN, HIDDEN), jnp.float32, -scale, scale)
        w_v = jax.random.uniform(ks[3], (HIDDEN, HIDDEN), jnp.float32, -scale, scale)
        w_o = jax.random.uniform(ks[4], (HIDDEN, HIDDEN), jnp.float32, -scale, scale)
        return {'x': x, 'w_q': w_q, 'w_k': w_k, 'w_v': w_v, 'w_o': w_o}
    _L1_attn_in = _L1_attn_setup()

    def _L1_ffn_setup():
        import jax, jax.numpy as jnp
        import numpy as np
        BS = 128
        FP8_MAX = 448.0

        def act_quant(x):
            T, K = x.shape
            xb = x.reshape(T, K // BS, BS)
            amax = jnp.max(jnp.abs(xb), axis=-1)
            scale = amax / FP8_MAX + 1e-12
            xq = (xb / scale[:, :, None]).reshape(T, K)
            return (xq, scale)

        def linear_dsv3(x, wq, w_scale):
            T, K = x.shape
            N = wq.shape[0]
            xq, xs = act_quant(x)
            xdq = (xq.reshape(T, K // BS, BS) * xs[:, :, None]).reshape(T, K)
            wdq = (wq.reshape(N // BS, BS, K // BS, BS) * w_scale[:, None, :, None]).reshape(N, K)
            return xdq @ wdq.T
        key = jax.random.key(seed)
        ks = jax.random.split(key, 4)
        DIM, INTER = (512, 1792)

        def make_qweight(k, n, m):
            w = jax.random.normal(k, (n, m), dtype=jnp.float32) * 0.02
            wb = w.reshape(n // BS, BS, m // BS, BS)
            amax = jnp.max(jnp.abs(wb), axis=(1, 3))
            scale = amax / FP8_MAX + 1e-12
            wq = (wb / scale[:, None, :, None]).reshape(n, m)
            return (wq, scale)
        x = jax.random.normal(ks[0], (2, 128, DIM), dtype=jnp.float32)
        w1, w1_scale = make_qweight(ks[1], INTER, DIM)
        w3, w3_scale = make_qweight(ks[2], INTER, DIM)
        w2, w2_scale = make_qweight(ks[3], DIM, INTER)
        return {'x': x, 'w1': w1, 'w1_scale': w1_scale, 'w3': w3, 'w3_scale': w3_scale, 'w2': w2, 'w2_scale': w2_scale}
    _L1_ffn_in = _L1_ffn_setup()
    _d = {'L0_attn_x': _L0_attn_in['x'], 'L0_attn_A_log': _L0_attn_in['A_log'], 'L0_attn_D': _L0_attn_in['D'], 'L0_attn_x_proj_w': _L0_attn_in['x_proj_w'], 'L0_attn_dt_proj_w': _L0_attn_in['dt_proj_w'], 'L0_attn_dt_proj_b': _L0_attn_in['dt_proj_b'], 'L0_ffn_router_w': _L0_ffn_in['router_w'], 'L0_ffn_router_b': _L0_ffn_in['router_b'], 'L0_ffn_router_bias': _L0_ffn_in['router_bias'], 'L0_ffn_ew1': _L0_ffn_in['ew1'], 'L0_ffn_eb1': _L0_ffn_in['eb1'], 'L0_ffn_ew2': _L0_ffn_in['ew2'], 'L0_ffn_eb2': _L0_ffn_in['eb2'], 'L0_ffn_ew3': _L0_ffn_in['ew3'], 'L0_ffn_eb3': _L0_ffn_in['eb3'], 'L0_ffn_sw1': _L0_ffn_in['sw1'], 'L0_ffn_sb1': _L0_ffn_in['sb1'], 'L0_ffn_sw2': _L0_ffn_in['sw2'], 'L0_ffn_sb2': _L0_ffn_in['sb2'], 'L0_ffn_sw3': _L0_ffn_in['sw3'], 'L0_ffn_sb3': _L0_ffn_in['sb3'], 'L1_attn_w_q': _L1_attn_in['w_q'], 'L1_attn_w_k': _L1_attn_in['w_k'], 'L1_attn_w_v': _L1_attn_in['w_v'], 'L1_attn_w_o': _L1_attn_in['w_o'], 'L1_ffn_w1': _L1_ffn_in['w1'], 'L1_ffn_w1_scale': _L1_ffn_in['w1_scale'], 'L1_ffn_w3': _L1_ffn_in['w3'], 'L1_ffn_w3_scale': _L1_ffn_in['w3_scale'], 'L1_ffn_w2': _L1_ffn_in['w2'], 'L1_ffn_w2_scale': _L1_ffn_in['w2_scale']}
    _x0 = _d['L0_attn_x']
    _d['L0_attn_x'] = jax.random.normal(jax.random.fold_in(jax.random.key(seed), 1), (4, 512, 512), dtype=_x0.dtype)
    del _x0
    return _d

def reference(L0_attn_x, L0_attn_A_log, L0_attn_D, L0_attn_x_proj_w, L0_attn_dt_proj_w, L0_attn_dt_proj_b, L0_ffn_router_w, L0_ffn_router_b, L0_ffn_router_bias, L0_ffn_ew1, L0_ffn_eb1, L0_ffn_ew2, L0_ffn_eb2, L0_ffn_ew3, L0_ffn_eb3, L0_ffn_sw1, L0_ffn_sb1, L0_ffn_sw2, L0_ffn_sb2, L0_ffn_sw3, L0_ffn_sb3, L1_attn_w_q, L1_attn_w_k, L1_attn_w_v, L1_attn_w_o, L1_ffn_w1, L1_ffn_w1_scale, L1_ffn_w3, L1_ffn_w3_scale, L1_ffn_w2, L1_ffn_w2_scale):

    def _L0_attn_ref(x, A_log, D, x_proj_w, dt_proj_w, dt_proj_b):
        import jax, jax.numpy as jnp
        import numpy as np
        import math
        D_MODEL = 256
        D_STATE = 16
        EXPAND = 2
        D_INNER = D_MODEL * EXPAND
        DT_RANK = math.ceil(D_MODEL / 16)
        BATCH, SEQ_LEN = (2, 64)
        A = -jnp.exp(A_log)
        xp = jnp.einsum('bld,rd->blr', x, x_proj_w)
        dt_in = xp[..., :DT_RANK]
        B = xp[..., DT_RANK:DT_RANK + D_STATE]
        C = xp[..., DT_RANK + D_STATE:]
        dt = jax.nn.softplus(jnp.einsum('blr,dr->bld', dt_in, dt_proj_w) + dt_proj_b)
        dA = jnp.exp(dt[..., None] * A)
        dBx = dt[..., None] * B[:, :, None, :] * x[..., None]

        def step(h, inp):
            dA_t, dBx_t, C_t = inp
            h = dA_t * h + dBx_t
            y = jnp.einsum('bdn,bn->bd', h, C_t)
            return (h, y)
        h0 = jnp.zeros((x.shape[0], D_INNER, D_STATE), dtype=x.dtype)
        _, ys = jax.lax.scan(step, h0, (jnp.moveaxis(dA, 1, 0), jnp.moveaxis(dBx, 1, 0), jnp.moveaxis(C, 1, 0)))
        y = jnp.moveaxis(ys, 0, 1) + D * x
        return y

    def _L0_ffn_ref(x, router_w, router_b, router_bias, ew1, eb1, ew2, eb2, ew3, eb3, sw1, sb1, sw2, sb2, sw3, sb3):
        import jax, jax.numpy as jnp
        import numpy as np
        DIM = 512
        INTER = 128
        E = 16
        GROUPS = 4
        LIM = 2
        K = 2
        SHARED_INTER = 2 * INTER
        SCALE = 1.0
        shape = x.shape
        xt = x.reshape(-1, DIM)
        T = xt.shape[0]
        logits = xt @ router_w + router_b
        scores = jax.nn.softmax(logits.astype(jnp.float32), axis=-1) + router_bias
        g = scores.reshape(T, GROUPS, E // GROUPS)
        _, gidx = jax.lax.top_k(g.max(axis=-1), LIM)
        keep = jnp.zeros((T, GROUPS), bool).at[jnp.arange(T)[:, None], gidx].set(True)
        masked = jnp.where(keep[:, :, None], g, -jnp.inf).reshape(T, E)
        _, idx = jax.lax.top_k(masked, K)
        vals = (jnp.take_along_axis(scores, idx, axis=1) * SCALE).astype(x.dtype)
        gate = jnp.zeros((T, E), x.dtype).at[jnp.arange(T)[:, None], idx].add(vals)

        def step(y, p):
            w1, b1, w2, b2, w3, b3, ge = p
            h = jax.nn.silu(xt @ w1 + b1) * (xt @ w2 + b2)
            return (y + ge[:, None] * (h @ w3 + b3), None)
        y, _ = jax.lax.scan(step, jnp.zeros_like(xt), (ew1, eb1, ew2, eb2, ew3, eb3, gate.T))
        z = jax.nn.silu(xt @ sw1 + sb1) * (xt @ sw2 + sb2) @ sw3 + sb3
        return (y + z).reshape(shape)

    def _L1_attn_ref(x, w_q, w_k, w_v, w_o):
        import jax, jax.numpy as jnp
        import numpy as np
        HIDDEN = 512
        HEADS = 32
        D_K = HIDDEN // HEADS
        B, S, _ = x.shape

        def proj(w):
            y = jnp.einsum('bsd,ed->bse', x, w)
            return y.reshape(B, S, HEADS, D_K).transpose(0, 2, 1, 3)
        q, k, v = (proj(w_q), proj(w_k), proj(w_v))
        scores = jnp.einsum('bhqd,bhkd->bhqk', q, k) / jnp.sqrt(jnp.float32(D_K))
        attn = jax.nn.softmax(scores, axis=-1)
        out = jnp.einsum('bhqk,bhkd->bhqd', attn, v)
        out = out.transpose(0, 2, 1, 3).reshape(B, S, HIDDEN)
        return jnp.einsum('bse,oe->bso', out, w_o)

    def _L1_ffn_ref(x, w1, w1_scale, w3, w3_scale, w2, w2_scale):
        import jax, jax.numpy as jnp
        import numpy as np
        BS = 128
        FP8_MAX = 448.0

        def act_quant(x):
            T, K = x.shape
            xb = x.reshape(T, K // BS, BS)
            amax = jnp.max(jnp.abs(xb), axis=-1)
            scale = amax / FP8_MAX + 1e-12
            xq = (xb / scale[:, :, None]).reshape(T, K)
            return (xq, scale)

        def linear_dsv3(x, wq, w_scale):
            T, K = x.shape
            N = wq.shape[0]
            xq, xs = act_quant(x)
            xdq = (xq.reshape(T, K // BS, BS) * xs[:, :, None]).reshape(T, K)
            wdq = (wq.reshape(N // BS, BS, K // BS, BS) * w_scale[:, None, :, None]).reshape(N, K)
            return xdq @ wdq.T
        B, S, D = x.shape
        xf = x.reshape(-1, D)
        g = linear_dsv3(xf, w1, w1_scale)
        u = linear_dsv3(xf, w3, w3_scale)
        h = jax.nn.silu(g) * u
        y = linear_dsv3(h, w2, w2_scale)
        return y.reshape(B, S, D)
    x = L0_attn_x
    x = _layernorm(x + _L0_attn_ref(x, L0_attn_A_log, L0_attn_D, L0_attn_x_proj_w, L0_attn_dt_proj_w, L0_attn_dt_proj_b), axis=-1)
    x = _layernorm(x + _L0_ffn_ref(x, L0_ffn_router_w, L0_ffn_router_b, L0_ffn_router_bias, L0_ffn_ew1, L0_ffn_eb1, L0_ffn_ew2, L0_ffn_eb2, L0_ffn_ew3, L0_ffn_eb3, L0_ffn_sw1, L0_ffn_sb1, L0_ffn_sw2, L0_ffn_sb2, L0_ffn_sw3, L0_ffn_sb3), axis=-1)
    x = _layernorm(x + _L1_attn_ref(x, L1_attn_w_q, L1_attn_w_k, L1_attn_w_v, L1_attn_w_o), axis=-1)
    x = _layernorm(x + _L1_ffn_ref(x, L1_ffn_w1, L1_ffn_w1_scale, L1_ffn_w3, L1_ffn_w3_scale, L1_ffn_w2, L1_ffn_w2_scale), axis=-1)
    return x

_drawn_inputs = setup_inputs


def setup_inputs(seed=0):
    import zlib

    import numpy as np

    out = dict(_drawn_inputs(seed))
    spreads = {'L0_attn_D': (1.0, 0.2)}
    factors = {'L0_attn_A_log': 18.99,
     'L0_attn_dt_proj_w': 35.809,
     'L0_attn_dt_proj_b': 14.301,
     'L0_ffn_router_w': 8.0,
     'L0_ffn_router_b': 22.232,
     'L0_ffn_eb1': 8.0,
     'L0_ffn_eb2': 8.0,
     'L0_ffn_sb1': 8.0,
     'L0_ffn_sb2': 8.0,
     'L0_ffn_sb3': 2.707,
     'L1_attn_w_q': 6.918,
     'L1_attn_w_k': 6.24,
     'L1_ffn_w1_scale': 6.955,
     'L1_ffn_w3_scale': 6.82,
     'L1_ffn_w2_scale': 8.0,
     'L0_attn_x_proj_w': 4.026}
    for name, (base, spread) in spreads.items():
        noise = np.random.default_rng([zlib.crc32(name.encode()), seed]).standard_normal(out[name].shape)
        drawn = base * np.exp(spread * noise) if base else spread * noise
        out[name] = jnp.asarray(drawn.astype(out[name].dtype))
    for name, factor in factors.items():
        out[name] = (out[name] * factor).astype(out[name].dtype)
    return out
```

```python
from contextlib import ExitStack


import concourse.bass as bass
from concourse import mybir

F32 = mybir.dt.float32
F32R = mybir.dt.float32r
ALU = mybir.AluOpType
ACT = mybir.ActivationFunctionType
AX = mybir.AxisListType

P = 128
BATCH, SEQ, DIM = 4, 512, 512
TOK = BATCH * SEQ
KC = DIM // P
TILES = TOK // P
NB = 512
BLOCKS = TOK // NB
PER_BLOCK = NB // P
STATE, RANK = 16, 16
EXPERTS, GROUPS, INTER = 16, 4, 128
MLPS = EXPERTS + 2
HEADS, DK = 32, 16
GHEADS = P // DK
UNITS = BATCH * KC
VPAD = 32
FFN_INTER = 1792
FBLOCKS = FFN_INTER // P
FPAIRS = FBLOCKS // 2
EPS = 1e-5
FP8_MAX = 448.0
BIG = 3.0e38


class Chain:

    def __init__(self, eng, sem):
        self.eng, self.sem, self.base, self.n = eng, sem, 0, 0

    def step(self, ins):
        ins.then_inc(self.sem, 1)
        self.n += 1

    def settle(self):
        self.eng.wait_ge(self.sem, self.base + self.n)

    def enter(self, i, per):
        self.start, self.per = self.base + self.n, per
        self.base, self.n = self.start + i * per, 0

    def leave(self, times):
        assert self.n == self.per, (self.n, self.per)
        self.base, self.n = self.start + times * self.per, 0


def scoped(nc, ctx, tag):
    def sb(name, shape, dt=F32):
        return ctx.enter_context(nc.sbuf_tensor(f"{tag}_{name}", shape, dt))

    def ps(name, shape):
        return ctx.enter_context(nc.psum_tensor(f"{tag}_{name}", shape, F32))

    def sem(name):
        return ctx.enter_context(nc.semaphore(f"{tag}_{name}"))

    return sb, ps, sem


def wait_apart(eng, sem, value):
    eng.wait_ge(sem, value)
    eng.nop(nofuse=True)


def three(pe, out, lh, ll, rh, rl, first, last):
    pe.matmul(out, lh, rh, start=first, stop=False)
    pe.matmul(out, lh, rl, start=False, stop=False)
    return pe.matmul(out, ll, rh, start=False, stop=last)


def ssm_inputs(nc, a, g):
    with ExitStack() as ctx:
        sb, ps, sem = scoped(nc, ctx, "pre")
        wx = sb("wx", [P, KC, RANK + 2 * STATE])
        wdt = sb("wdt", [RANK, DIM])
        dtb = sb("dtb", [P, KC])
        alog = sb("alog", [P, KC, STATE])
        dtin = sb("dtin", [RANK, NB])
        brow = sb("brow", [STATE, 2, NB])
        z = sb("z", [P, 2, NB])
        mag = sb("mag", [P, 2, NB])
        e = sb("e", [P, 2, NB])
        ln = sb("ln", [P, 2, NB])
        d = sb("d", [P, 2, NB])
        d1 = sb("d1", [P, 2, NB])
        l1 = sb("l1", [P, 2, NB])
        q = sb("q", [P, 2, NB])
        q2 = sb("q2", [P, 2, NB])
        pp = ps("pp", [P, 3, NB])
        pz = ps("pz", [P, 2, NB])
        loaded, x_in = sem("loaded"), [sem(f"x_in{b}") for b in range(BATCH)]
        rows_ready, rows_copied = sem("rows_ready"), sem("rows_copied")
        z_ready, z_read = sem("z_ready"), sem("z_read")
        act_chain, dve_chain = sem("act_chain"), sem("dve_chain")
        ln_ready, dt_ready, b_stored = sem("ln_ready"), sem("dt_ready"), [sem("b_stored0"), sem("b_stored1")]
        u_ready = sem("u_ready")
        block = ctx.enter_context(nc.Block())

        @block.sync
        def _(sp):
            sp.dma_start(wx[:], a["xprojT"].rearrange("(c p) r -> p c r", p=P)).then_inc(loaded, 16)
            sp.dma_start(wdt[:], a["dtprojT"]).then_inc(loaded, 16)
            sp.dma_start(dtb[:], a["dtb"]).then_inc(loaded, 16)
            sp.dma_start(alog[:], a["alog"].rearrange("(c p) n -> p c n", p=P)).then_inc(loaded, 16)
            sp.dma_start(g.D1[:], a["dcoef"]).then_inc(loaded, 16)
            for b in range(BATCH):
                sp.dma_start(g.XT[:, :, b * NB:(b + 1) * NB],
                             a["xT"].rearrange("(c p) t -> p c t", p=P)[:, :, b * NB:(b + 1) * NB]).then_inc(x_in[b], 16)
            for b in range(BATCH):
                sp.wait_ge(rows_copied, 3 * b + 2)
                sp.dma_start(g.brow_dram[:, b, :], brow[:, b % 2, :]).then_inc(b_stored[b % 2], 16)
            for s in range(2):
                sp.wait_ge(b_stored[s], 16 * BATCH // 2)

        @block.tensor
        def _(pe):
            for b in range(BATCH):
                pe.wait_ge(loaded, 80)
                pe.wait_ge(x_in[b], 16)
                if b:
                    pe.wait_ge(rows_copied, 3 * b)
                for k in range(3):
                    for c in range(KC):
                        mm = pe.matmul(pp[0:RANK, k, :], wx[:, c, k * RANK:(k + 1) * RANK],
                                       g.XT[:, c, b * NB:(b + 1) * NB], start=(c == 0), stop=(c == KC - 1))
                    mm.then_inc(rows_ready, 1)
                pe.wait_ge(rows_copied, 3 * b + 1)
                for c in range(KC):
                    i = b * KC + c
                    if i >= 2:
                        pe.wait_ge(z_read, i - 1)
                    pe.matmul(pz[:, i % 2, :], wdt[:, c * P:(c + 1) * P], dtin[:], start=True,
                              stop=True).then_inc(z_ready, 1)

        @block.scalar
        def _(act):
            own = Chain(act, act_chain)
            act.wait_ge(loaded, 80)
            own.step(nc.scalar.activation(g.A[:], alog[:], ACT.Exp))
            for b in range(BATCH):
                act.wait_ge(rows_ready, 3 * b + 1)
                if b:
                    act.wait_ge(z_ready, KC * b)
                nc.scalar.activation(dtin[:], pp[0:RANK, 0, :], ACT.Copy).then_inc(rows_copied, 1)
                act.wait_ge(rows_ready, 3 * b + 2)
                if b >= 2:
                    act.wait_ge(b_stored[b % 2], 16 * (b // 2))
                nc.scalar.activation(brow[:, b % 2, :], pp[0:STATE, 1, :], ACT.Copy).then_inc(rows_copied, 1)
                act.wait_ge(rows_ready, 3 * b + 3)
                nc.scalar.activation(g.CT[:, b * NB:(b + 1) * NB], pp[0:STATE, 2, :], ACT.Copy).then_inc(rows_copied, 1)
                for c in range(KC):
                    i = b * KC + c
                    s = i % 2
                    act.wait_ge(z_ready, i + 1)
                    if i >= 2:
                        act.wait_ge(dt_ready, i - 1)
                    own.step(nc.scalar.activation(z[:, s, :], pz[:, s, :], ACT.Identity, bias=dtb[:, c:c + 1]))
                    own.settle()
                    z_read_ins = nc.scalar.activation(mag[:, s, :], z[:, s, :], ACT.Abs)
                    z_read_ins.then_inc(z_read, 1)
                    act.wait_ge(z_read, i + 1)
                    own.step(nc.scalar.activation(e[:, s, :], mag[:, s, :], ACT.Exp, scale=-1.0))
                    own.settle()
                    nc.scalar.activation(ln[:, s, :], e[:, s, :], ACT.Ln, bias=1.0).then_inc(ln_ready, 1)

        @block.vector
        def _(dve):
            own = Chain(dve, dve_chain)
            dve.wait_ge(loaded, 80)
            own.step(nc.vector.tensor_scalar(g.D1[:], g.D1[:], 1.0, None, ALU.add))
            dve.wait_ge(act_chain, 1)
            own.step(nc.vector.tensor_scalar(g.A[:], g.A[:], -1.0, None, ALU.mult))
            for i in range(BATCH * KC):
                b, c, s = i // KC, i % KC, i % 2
                dve.wait_ge(ln_ready, i + 1)
                own.step(nc.vector.tensor_scalar(d[:, s, :], e[:, s, :], 1.0, -1.0, ALU.add, ALU.add))
                own.settle()
                own.step(nc.vector.scalar_tensor_tensor(out=d1[:, s, :], in0=d[:, s, :], scalar=0.0, in1=d[:, s, :],
                                                        op0=ALU.is_equal, op1=ALU.add))
                own.step(nc.vector.scalar_tensor_tensor(out=l1[:, s, :], in0=d[:, s, :], scalar=0.0, in1=ln[:, s, :],
                                                        op0=ALU.is_equal, op1=ALU.add))
                own.settle()
                own.step(nc.vector.reciprocal(q[:, s, :], d1[:, s, :]))
                own.settle()
                own.step(nc.vector.tensor_tensor(q2[:, s, :], q[:, s, :], l1[:, s, :], ALU.mult))
                own.settle()
                own.step(nc.vector.tensor_tensor(l1[:, s, :], q2[:, s, :], e[:, s, :], ALU.mult))
                own.settle()
                nc.vector.scalar_tensor_tensor(out=g.DT[:, c, b * NB:(b + 1) * NB], in0=z[:, s, :], scalar=0.0,
                                               in1=l1[:, s, :], op0=ALU.max, op1=ALU.add).then_inc(dt_ready, 1)

        @block.gpsimd
        def _(pool):
            nc.gpsimd.memset(g.sel[:], 0.0).then_inc(u_ready, 1)
            nc.gpsimd.memset(g.ident[:], 0.0).then_inc(u_ready, 1)
            pool.wait_ge(u_ready, 2)
            nc.gpsimd.affine_select(out=g.sel[:], in_=g.sel[:], compare_op=ALU.not_equal, fill=1.0, base=0,
                                    pattern=[[-1, STATE], [0, P]], channel_multiplier=1).then_inc(u_ready, 1)
            nc.gpsimd.affine_select(out=g.ident[:], in_=g.ident[:], compare_op=ALU.not_equal, fill=1.0, base=0,
                                    pattern=[[-1, P]], channel_multiplier=1).then_inc(u_ready, 1)
            for i in range(BATCH * KC):
                b, c = i // KC, i % KC
                pool.wait_ge(dt_ready, i + 1)
                pool.wait_ge(x_in[b], 16)
                cols = slice(b * NB, (b + 1) * NB)
                nc.gpsimd.tensor_tensor(g.U[:, c, cols], g.DT[:, c, cols], g.XT[:, c, cols], ALU.mult).then_inc(u_ready, 1)


def ssm_scan(nc, a, g):
    with ExitStack() as ctx:
        sb, ps, sem = scoped(nc, ctx, "scan")
        RING = 4
        STEPS = STATE * KC
        bbc = sb("bbc", [P, RING, NB])
        dbx = sb("dbx", [P, RING, NB])
        h = sb("h", [P, 2, NB])
        hc = sb("hc", [P, 2, NB])
        da = ps("da", [P, 2, NB])
        cbc = ps("cbc", [P, 2, NB])
        y = ps("y", [P, KC, NB])
        b_in = [sem(f"b_in{k}") for k in range(RING)]
        dbx_ready, dbx_0 = sem("dbx_ready"), STATE
        h_ready, h_0 = sem("h_ready"), RING
        hc_ready, hc_0 = sem("hc_ready"), 2 * KC
        y_used_hc, y_used_0 = sem("y_used_hc"), 2
        y_read = sem("y_read")
        da_ready, c_ready = sem("da_ready"), sem("c_ready")
        block = ctx.enter_context(nc.Block())

        @block.sync
        def _(sp):
            with sp.Fori(0, BATCH) as b:
                for n in range(STATE):
                    sp.wait_ge(dbx_ready, b * STEPS + KC * (n - RING + 1) + dbx_0)
                    sp.dma_start(bbc[:, n % RING, :], g.brow_dram[n, b].partition_broadcast(P)).then_inc(b_in[n % RING], 16)

        @block.gpsimd
        def _(pool):
            pool.sem_inc(dbx_ready, dbx_0)
            with pool.Fori(0, BATCH) as b:
                for n in range(STATE):
                    pool.wait_ge(b_in[n % RING], b * (16 * STATE // RING) + 16 * (n // RING + 1))
                    for c in range(KC):
                        i = n * KC + c
                        wait_apart(pool, h_ready, b * STEPS + i - RING + 1 + h_0)
                        nc.gpsimd.tensor_tensor(dbx[:, i % RING, :], g.U[:, c, bass.ts(b, NB)], bbc[:, n % RING, :],
                                                ALU.mult).then_inc(dbx_ready, 1)

        @block.scalar
        def _(act):
            with act.Fori(0, BATCH) as b:
                for n in range(STATE):
                    for c in range(KC):
                        i = n * KC + c
                        wait_apart(act, h_ready, b * STEPS + i - 1 + h_0)
                        nc.scalar.activation(da[:, i % 2, :], g.DT[:, c, bass.ts(b, NB)], ACT.Exp,
                                             scale=g.A[:, c, n:n + 1]).then_inc(da_ready, 1)

        @block.vector
        def _(dve):
            dve.sem_inc(h_ready, h_0)
            dve.sem_inc(hc_ready, hc_0)
            dve.sem_inc(y_read, KC)

            def weigh(b, i):
                dve.wait_ge(h_ready, b * STEPS + i + 1 + h_0)
                dve.wait_ge(c_ready, b * STATE + i // KC + 1)
                dve.wait_ge(y_used_hc, b * STEPS + i - 1 + y_used_0)
                nc.vector.tensor_tensor(hc[:, i % 2, :], cbc[:, (i // KC) % 2, :], h[:, i % 2, :],
                                        ALU.mult).then_inc(hc_ready, 1)

            with dve.Fori(0, BATCH) as b:
                for i in range(STEPS):
                    dve.wait_ge(da_ready, b * STEPS + i + 1)
                    dve.wait_ge(dbx_ready, b * STEPS + i + 1 + dbx_0)
                    dve.wait_ge(hc_ready, b * STEPS + i - 1 + hc_0)
                    nc.vector.tensor_tensor_scan(h[:, i % 2, :], da[:, i % 2, :], dbx[:, i % RING, :], 0.0,
                                                 ALU.mult, ALU.add).then_inc(h_ready, 1)
                    if i:
                        weigh(b, i - 1)
                weigh(b, STEPS - 1)
                for c in range(KC):
                    dve.wait_ge(y_used_hc, b * STEPS + STEPS - KC + c + 1 + y_used_0)
                    xs = g.XT[:, c, bass.ts(b, NB)]
                    nc.vector.scalar_tensor_tensor(out=xs, in0=xs, scalar=g.D1[:, c:c + 1], in1=y[:, c, :],
                                                   op0=ALU.mult, op1=ALU.add).then_inc(y_read, 1)

        @block.tensor
        def _(pe):
            pe.sem_inc(y_used_hc, y_used_0)
            with pe.Fori(0, BATCH) as b:
                for n in range(STATE + 1):
                    if n < STATE:
                        wait_apart(pe, hc_ready, b * STEPS + KC * (n - 1) + hc_0)
                        pe.matmul(cbc[:, n % 2, :], g.sel[:, n, :], g.CT[:, bass.ts(b, NB)], start=True,
                                  stop=True).then_inc(c_ready, 1)
                    if n == 0:
                        continue
                    for c in range(KC):
                        m = n - 1
                        i = m * KC + c
                        if m == 0:
                            pe.wait_ge(y_read, b * KC + c + 1)
                        pe.wait_ge(hc_ready, b * STEPS + i + 1 + hc_0)
                        mm = pe.matmul(y[:, c, :], g.ident[:], hc[:, i % 2, :], start=(m == 0), stop=(m == STATE - 1))
                        mm.then_inc(y_used_hc, 1)


def normalise(nc, g, tag, by_feature, out=None, quantise=False):
    with ExitStack() as ctx:
        sb, ps, sem = scoped(nc, ctx, tag)
        stats = sb("stats", [P, TILES, 6])
        mv = sb("mv", [P, TILES, 2])
        std = sb("std", [P, TILES])
        rstd = sb("rstd", [P, TILES])
        eps = sb("eps", [P, 1])
        if quantise:
            amax, scale, inv = (sb(n, [P, TILES, KC]) for n in ("amax", "scale", "inv"))
            xq = sb("xq", [P, 2, DIM])
        pr = [ps(f"pr{k}", [P, DIM]) for k in range(2)] if by_feature else None
        pt = [ps(f"pt{k}", [P, KC, P]) for k in range(2)] if out is None else None
        x_ready, dve_chain = sem("x_ready"), sem("dve_chain")
        if by_feature:
            turned = sem("turned")
        if out is None:
            x_turned, hi_ready, lo_ready = sem("x_turned"), sem("hi_ready"), sem("lo_ready")
        else:
            stored = sem("stored")
        var_ready, std_ready, eps_ready = sem("var_ready"), sem("std_ready"), sem("eps_ready")
        if quantise:
            xq_ready, y_copied = sem("xq_ready"), sem("y_copied")
        block = ctx.enter_context(nc.Block())

        @block.tensor
        def _(pe):
            for t in range(TILES + 1):
                if by_feature and t < TILES:
                    if t >= 2:
                        pe.wait_ge(x_ready, t - 1)
                    for c in range(KC):
                        mm = pe.transpose(pr[t % 2][:, c * P:(c + 1) * P], g.XT[:, c, t * P:(t + 1) * P], g.ident[:])
                    mm.then_inc(turned, 1)
                if t and out is None:
                    m = t - 1
                    pe.wait_ge(xq_ready if quantise else x_ready, m + 1)
                    if m >= 2:
                        pe.wait_ge(lo_ready, m - 1)
                    for c in range(KC):
                        cols = slice(c * P, (c + 1) * P)
                        mm = pe.transpose(pt[m % 2][:, c, :], xq[:, m % 2, cols] if quantise else g.X[:, m, cols],
                                          g.ident[:])
                    mm.then_inc(x_turned, 1)

        @block.vector
        def _(dve):
            own = Chain(dve, dve_chain)
            nc.vector.memset(eps[:], EPS).then_inc(eps_ready, 1)

            def low_part(m):
                dve.wait_ge(hi_ready, m + 1)
                cols = slice(m * P, (m + 1) * P)
                nc.vector.tensor_tensor(g.XL[:, :, cols], pt[m % 2][:], g.XH[:, :, cols].bitcast(F32),
                                        ALU.subtract).then_inc(lo_ready, 1)

            def quantised(m):
                dve.wait_ge(x_ready, m + 1)
                own.step(nc.vector.tensor_reduce(amax[:, m, :], g.X[:, m, :].rearrange("p (c k) -> p c k", k=P), AX.X,
                                                 ALU.max, apply_absolute_value=True))
                own.settle()
                own.step(nc.vector.tensor_scalar(scale[:, m, :], amax[:, m, :], 1.0 / FP8_MAX, 1e-12, ALU.mult, ALU.add))
                own.settle()
                own.step(nc.vector.reciprocal(inv[:, m, :], scale[:, m, :]))
                own.settle()
                if m >= 2:
                    dve.wait_ge(x_turned, m - 1)
                for c in range(KC):
                    cols = slice(c * P, (c + 1) * P)
                    ins = nc.vector.tensor_scalar(xq[:, m % 2, cols], g.X[:, m, cols], inv[:, m, c:c + 1],
                                                  scale[:, m, c:c + 1], ALU.mult, ALU.mult)
                    if c < KC - 1:
                        own.step(ins)
                ins.then_inc(xq_ready, 1)

            def source(t):
                return pr[t % 2][:] if by_feature else g.Y[:, t, :]

            for t in range(TILES + 2):
                if t < TILES:
                    if by_feature:
                        dve.wait_ge(turned, t + 1)
                    own.step(nc.vector.bn_stats(stats[:, t, :], source(t)))
                    own.settle()
                    nc.vector.bn_aggr(mv[:, t, :], stats[:, t, :]).then_inc(var_ready, 1)
                if 1 <= t <= TILES:
                    m = t - 1
                    dve.wait_ge(std_ready, m + 1)
                    own.step(nc.vector.reciprocal(rstd[:, m:m + 1], std[:, m:m + 1]))
                    own.settle()
                    nc.vector.tensor_scalar(g.X[:, m, :], source(m), mv[:, m, 0:1], rstd[:, m:m + 1], ALU.subtract,
                                            ALU.mult).then_inc(x_ready, 1)
                    if quantise:
                        quantised(m)
                if t >= 2 and out is None:
                    low_part(t - 2)

        @block.scalar
        def _(act):
            act.wait_ge(eps_ready, 1)
            for t in range(TILES + 2):
                if t < TILES:
                    act.wait_ge(var_ready, t + 1)
                    nc.scalar.activation(std[:, t:t + 1], mv[:, t, 1:2], ACT.Sqrt, bias=eps[:, 0:1]).then_inc(std_ready, 1)
                if quantise and 1 <= t <= TILES:
                    act.wait_ge(x_ready, t)
                    nc.scalar.activation(g.Y[:, t - 1, :], g.X[:, t - 1, :], ACT.Copy).then_inc(y_copied, 1)
                if t >= 2 and out is None:
                    m = t - 2
                    act.wait_ge(x_turned, m + 1)
                    nc.scalar.activation(g.XH[:, :, m * P:(m + 1) * P], pt[m % 2][:], ACT.Copy).then_inc(hi_ready, 1)

        @block.sync
        def _(sp):
            if out is not None:
                rows = out.rearrange("(t p) d -> p t d", p=P)
                for t in range(0, TILES, 2):
                    sp.wait_ge(x_ready, t + 2)
                    sp.dma_start(rows[:, t:t + 2, :], g.X[:, t:t + 2, :]).then_inc(stored, 16)
                sp.wait_ge(stored, 16 * TILES // 2)


def route(nc, a, g):
    with ExitStack() as ctx:
        sb, ps, sem = scoped(nc, ctx, "route")
        rw = sb("rw", [P, KC, EXPERTS])
        rh = sb("rh", [P, KC, EXPERTS], F32R)
        rl = sb("rl", [P, KC, EXPERTS], F32R)
        rb = sb("rb", [P, EXPERTS])
        rbias = sb("rbias", [P, EXPERTS])
        order = sb("order", [P, EXPERTS])
        b3 = sb("b3", [MLPS, DIM])
        full = [P, TILES, EXPERTS]
        grouped = [P, TILES, GROUPS]
        lg, lg2, ex, pr_, sc = (sb(n, full) for n in ("lg", "lg2", "ex", "pr", "sc"))
        ms, ms2, ms3, eq, key, e1, e2, esum = (sb(n, full) for n in ("ms", "ms2", "ms3", "eq", "key", "e1", "e2", "es"))
        gm, gm2, geq, gkey, g1, g2, keep, low = (sb(n, grouped) for n in
                                                 ("gm", "gm2", "geq", "gkey", "g1", "g2", "keep", "low"))
        one, two, three_ = (sb(n, [P, TILES]) for n in ("one", "two", "three"))
        gT = sb("gT", [MLPS, TOK])
        pl = ps("pl", full)
        pg = [ps(f"pg{k}", [P, NB]) for k in range(2)]
        py = [ps(f"py{k}", [P, DIM]) for k in range(2)]
        loaded, logits, exped, gated = sem("loaded"), sem("logits"), sem("exped"), sem("gated")
        turned, copied, y_ready, y_added = sem("turned"), sem("copied"), sem("y_ready"), sem("y_added")
        dve_chain, split = sem("dve_chain"), sem("split")
        block = ctx.enter_context(nc.Block())

        @block.sync
        def _(sp):
            sp.dma_start(rw[:], a["router_w"].rearrange("(c p) e -> p c e", p=P)).then_inc(loaded, 16)
            sp.dma_start(rb[:], a["router_b"].partition_broadcast(P)).then_inc(loaded, 16)
            sp.dma_start(rbias[:], a["router_bias"].partition_broadcast(P)).then_inc(loaded, 16)
            sp.dma_start(order[:], a["order"].partition_broadcast(P)).then_inc(loaded, 16)
            sp.dma_start(b3[:], a["b3"]).then_inc(loaded, 16)

        @block.tensor
        def _(pe):
            pe.wait_ge(split, 2)
            for t in range(TILES):
                cols = slice(t * P, (t + 1) * P)
                for c in range(KC):
                    for x in (g.XH, g.XL):
                        for w in (rh, rl):
                            first = c == 0 and x is g.XH and w is rh
                            last = c == KC - 1 and x is g.XL and w is rl
                            mm = pe.matmul(pl[:, t, :], x[:, c, cols], w[:, c, :], start=first, stop=last)
            mm.then_inc(logits, 1)
            pe.wait_ge(gated, 1)
            for b in range(BLOCKS):
                if b >= 2:
                    pe.wait_ge(copied, b - 1)
                for j in range(PER_BLOCK):
                    t = b * PER_BLOCK + j
                    mm = pe.transpose(pg[b % 2][0:MLPS, j * P:(j + 1) * P], g.gate[:, :, t], g.ident[:])
                mm.then_inc(turned, 1)
            for t in range(TILES):
                pe.wait_ge(copied, t // PER_BLOCK + 1)
                if t >= 2:
                    pe.wait_ge(y_added, t - 1)
                pe.matmul(py[t % 2][:], gT[:, t * P:(t + 1) * P], b3[:], start=True, stop=True).then_inc(y_ready, 1)

        @block.scalar
        def _(act):
            act.wait_ge(dve_chain, 3 + 2)
            nc.scalar.activation(ex[:], lg2[:], ACT.Exp).then_inc(exped, 1)
            for b in range(BLOCKS):
                act.wait_ge(turned, b + 1)
                nc.scalar.activation(gT[:, b * NB:(b + 1) * NB], pg[b % 2][0:MLPS, :], ACT.Copy).then_inc(copied, 1)

        @block.vector
        def _(dve):
            own = Chain(dve, dve_chain)

            def along(x, n):
                return x.unsqueeze(2).to_broadcast([P, TILES, n])

            def do(ins):
                own.step(ins)
                own.settle()

            def pick(sel, v, n, eq_, key_):
                do(nc.vector.tensor_reduce(one[:], v, AX.X, ALU.max))
                do(nc.vector.tensor_tensor(eq_, v, along(one[:], n), ALU.is_equal))
                do(nc.vector.tensor_tensor(key_, eq_, order[:, 0:n].unsqueeze(1).to_broadcast([P, TILES, n]), ALU.mult))
                do(nc.vector.tensor_reduce(two[:], key_, AX.X, ALU.max))
                do(nc.vector.tensor_tensor(sel, key_, along(two[:], n), ALU.is_equal))

            def by_group(x):
                return x[:].rearrange("p t (g k) -> p (t g) k", g=GROUPS)

            def per_group(x):
                return x[:].rearrange("p t g -> p (t g)").unsqueeze(2).to_broadcast([P, TILES * GROUPS, EXPERTS // GROUPS])

            dve.wait_ge(loaded, 80)
            own.step(nc.vector.memset(g.gate[:, EXPERTS:MLPS, :], 1.0))
            nc.vector.tensor_copy(rh[:], rw[:]).then_inc(split, 1)
            dve.wait_ge(split, 1)
            nc.vector.tensor_tensor(rl[:], rw[:], rh[:].bitcast(F32), ALU.subtract).then_inc(split, 1)
            dve.wait_ge(logits, 1)
            do(nc.vector.tensor_tensor(lg[:], pl[:], rb[:].unsqueeze(1).to_broadcast(full), ALU.add))
            do(nc.vector.tensor_reduce(three_[:], lg[:], AX.X, ALU.max))
            do(nc.vector.tensor_tensor(lg2[:], lg[:], along(three_[:], EXPERTS), ALU.subtract))
            own.step(nc.vector.memset(esum[:], 0.0))
            dve.wait_ge(exped, 1)
            do(nc.vector.tensor_reduce(one[:], ex[:], AX.X, ALU.add))
            do(nc.vector.reciprocal(two[:], one[:]))
            do(nc.vector.tensor_tensor(pr_[:], ex[:], along(two[:], EXPERTS), ALU.mult))
            do(nc.vector.tensor_tensor(sc[:], pr_[:], rbias[:].unsqueeze(1).to_broadcast(full), ALU.add))
            do(nc.vector.tensor_reduce(gm[:].rearrange("p t g -> p (t g)"), by_group(sc), AX.X, ALU.max))
            pick(g1[:], gm[:], GROUPS, geq[:], gkey[:])
            do(nc.vector.scalar_tensor_tensor(out=gm2[:], in0=g1[:], scalar=-BIG, in1=gm[:], op0=ALU.mult, op1=ALU.add))
            pick(g2[:], gm2[:], GROUPS, geq[:], gkey[:])
            do(nc.vector.tensor_tensor(keep[:], g1[:], g2[:], ALU.add))
            do(nc.vector.tensor_scalar(low[:], keep[:], -1.0, BIG, ALU.add, ALU.mult))
            do(nc.vector.tensor_tensor(by_group(ms), by_group(sc), per_group(keep), ALU.mult))
            do(nc.vector.tensor_tensor(by_group(ms2), by_group(ms), per_group(low), ALU.add))
            pick(e1[:], ms2[:], EXPERTS, eq[:], key[:])
            do(nc.vector.scalar_tensor_tensor(out=ms3[:], in0=e1[:], scalar=-BIG / 2, in1=ms2[:], op0=ALU.mult,
                                              op1=ALU.add))
            do(nc.vector.tensor_scalar(ms3[:], ms3[:], -BIG, None, ALU.max))
            pick(e2[:], ms3[:], EXPERTS, eq[:], key[:])
            do(nc.vector.tensor_tensor(esum[:], e1[:], e2[:], ALU.add))
            nc.vector.tensor_tensor(g.gate[:, 0:EXPERTS, :].rearrange("p e t -> p t e"), esum[:], sc[:],
                                    ALU.mult).then_inc(gated, 1)
            for t in range(TILES):
                dve.wait_ge(y_ready, t + 1)
                nc.vector.tensor_tensor(g.Y[:, t, :], py[t % 2][:], g.X[:, t, :], ALU.add).then_inc(y_added, 1)


def experts(nc, a, g):
    with ExitStack() as ctx:
        sb, ps, sem = scoped(nc, ctx, "moe")
        WN = 2 * KC * INTER + DIM
        bias = sb("bias", [P, MLPS, 2])
        raw = [sb(f"raw{s}", [P, WN]) for s in range(2)]
        wh = [sb(f"wh{s}", [P, WN], F32R) for s in range(2)]
        wl = [sb(f"wl{s}", [P, WN], F32R) for s in range(2)]
        silu = sb("silu", [P, 2, NB])
        h = sb("h", [P, 2, NB])
        hh = sb("hh", [P, 2, NB], F32R)
        hl = sb("hl", [P, 2, NB], F32R)
        pg = [ps(f"pg{k}", [P, NB]) for k in range(2)]
        pu = [ps(f"pu{k}", [P, NB]) for k in range(2)]
        py = [ps(f"py{k}", [P, DIM]) for k in range(PER_BLOCK)]
        w_in, b_in, pool_chain = [sem("w_in0"), sem("w_in1")], sem("b_in"), sem("pool_chain")
        g_ready, u_ready, s_ready, hh_ready = sem("g_ready"), sem("u_ready"), sem("s_ready"), sem("hh_ready")
        split_ready, split_0 = sem("split_ready"), 2
        h_ready, h_0 = sem("h_ready"), 2
        hl_ready, hl_0 = sem("hl_ready"), 2
        y_ready, y_0 = sem("y_ready"), 2 * TILES
        y_added, added_0 = sem("y_added"), TILES
        block = ctx.enter_context(nc.Block())

        @block.sync
        def _(sp):
            sp.dma_start(bias[:], a["b12"]).then_inc(b_in, 16)
            with sp.Fori(0, MLPS // 2) as i:
                for s in range(2):
                    sp.wait_ge(split_ready, 2 * i + s - 1 + split_0)
                    sp.dma_start(raw[s][:], a["w123"][2 * i + s]).then_inc(w_in[s], 16)

        @block.gpsimd
        def _(pool):
            pool.sem_inc(split_ready, split_0)
            with pool.Fori(0, MLPS // 2) as i:
                for s in range(2):
                    pool.wait_ge(w_in[s], 16 * i + 16)
                    wait_apart(pool, y_ready, (2 * i + s - 1) * TILES + y_0)
                    nc.gpsimd.tensor_scalar(wh[s][:], raw[s][:], 1.0, 0.0, ALU.mult, ALU.add).then_inc(pool_chain, 1)
                    pool.wait_ge(pool_chain, 2 * i + s + 1)
                    nc.gpsimd.tensor_tensor(wl[s][:], raw[s][:], wh[s][:].bitcast(F32), ALU.subtract).then_inc(split_ready, 1)

        @block.tensor
        def _(pe):
            pe.sem_inc(y_ready, y_0)
            with pe.Fori(0, MLPS // 2) as i:
                for s in range(2):
                    e = 2 * i + s

                    def up(tb):
                        q = BLOCKS * e + tb
                        cols = slice(tb * NB, (tb + 1) * NB)
                        pe.wait_ge(h_ready, q - 1 + h_0)
                        for out, at, ready in ((pg, 0, g_ready), (pu, KC * INTER, u_ready)):
                            for c in range(KC):
                                w = slice(at + c * INTER, at + (c + 1) * INTER)
                                mm = three(pe, out[tb % 2][:], wh[s][:, w], wl[s][:, w], g.XH[:, c, cols],
                                           g.XL[:, c, cols], c == 0, c == KC - 1)
                            mm.then_inc(ready, 1)

                    def down(tb):
                        q = BLOCKS * e + tb
                        pe.wait_ge(hl_ready, q + 1 + hl_0)
                        w = slice(2 * KC * INTER, WN)
                        for j in range(PER_BLOCK):
                            cols = slice(j * P, (j + 1) * P)
                            pe.wait_ge(y_added, PER_BLOCK * (q - 1) + j + 1 + added_0)
                            three(pe, py[j][:], hh[:, tb % 2, cols], hl[:, tb % 2, cols], wh[s][:, w], wl[s][:, w],
                                  True, True).then_inc(y_ready, 1)

                    pe.wait_ge(split_ready, e + 1 + split_0)
                    up(0)
                    for tb in range(1, BLOCKS):
                        up(tb)
                        down(tb - 1)
                    down(BLOCKS - 1)

        @block.scalar
        def _(act):
            act.wait_ge(b_in, 16)
            with act.Fori(0, MLPS // 2) as i:
                for s in range(2):
                    for tb in range(BLOCKS):
                        q = BLOCKS * (2 * i + s) + tb
                        act.wait_ge(g_ready, q + 1)
                        wait_apart(act, h_ready, q - 1 + h_0)
                        nc.scalar.activation(silu[:, tb % 2, :], pg[tb % 2][:], ACT.Silu,
                                             bias=bias[:, bass.ds(2 * i + s, 1), 0]).then_inc(s_ready, 1)
                        act.wait_ge(h_ready, q + 1 + h_0)
                        act.wait_ge(y_ready, PER_BLOCK * (q - 1) + y_0)
                        nc.scalar.activation(hh[:, tb % 2, :], h[:, tb % 2, :], ACT.Copy).then_inc(hh_ready, 1)

        @block.vector
        def _(dve):
            dve.sem_inc(h_ready, h_0)
            dve.sem_inc(hl_ready, hl_0)
            dve.sem_inc(y_added, added_0)
            dve.wait_ge(b_in, 16)
            with dve.Fori(0, MLPS // 2) as i:
                for s in range(2):
                    e = 2 * i + s

                    def hidden(tb):
                        q = BLOCKS * e + tb
                        dve.wait_ge(u_ready, q + 1)
                        dve.wait_ge(s_ready, q + 1)
                        dve.wait_ge(hl_ready, q - 1 + hl_0)
                        nc.vector.scalar_tensor_tensor(out=h[:, tb % 2, :], in0=pu[tb % 2][:],
                                                       scalar=bias[:, bass.ds(e, 1), 1], in1=silu[:, tb % 2, :],
                                                       op0=ALU.add, op1=ALU.mult).then_inc(h_ready, 1)
                        dve.wait_ge(hh_ready, q + 1)
                        nc.vector.tensor_tensor(hl[:, tb % 2, :], h[:, tb % 2, :], hh[:, tb % 2, :].bitcast(F32),
                                                ALU.subtract).then_inc(hl_ready, 1)

                    def add(tb):
                        for j in range(PER_BLOCK):
                            t = PER_BLOCK * tb + j
                            dve.wait_ge(y_ready, TILES * e + t + 1 + y_0)
                            dve.wait_ge(y_added, TILES * (e - 1) + t + 1 + added_0)
                            nc.vector.scalar_tensor_tensor(out=g.Y[:, t, :], in0=py[j][:],
                                                           scalar=g.gate[:, bass.ds(e, 1), t], in1=g.Y[:, t, :],
                                                           op0=ALU.mult, op1=ALU.add).then_inc(y_added, 1)

                    hidden(0)
                    for tb in range(1, BLOCKS):
                        hidden(tb)
                        add(tb - 1)
                    add(BLOCKS - 1)


def project(nc, a, g):
    with ExitStack() as ctx:
        sb, ps, sem = scoped(nc, ctx, "proj")
        raw = [g.sums[:, k * KC * DIM:(k + 1) * KC * DIM] for k in range(3)]
        wh = [sb(f"wh{k}", [P, KC * DIM], F32R) for k in range(3)]
        wl = [sb(f"wl{k}", [P, KC * DIM], F32R) for k in range(3)]
        hi = sb("hi", [P, 2, NB], F32R)
        lo = sb("lo", [P, 2, NB], F32R)
        v = sb("v", [P, 2, HEADS, VPAD])
        po = [ps(f"po{k}", [P, NB]) for k in range(4)]
        w_in = [sem(f"w_in{k}") for k in range(3)]
        w_hi, w_split, pads, product = sem("w_hi"), sem("w_split"), sem("pads"), sem("product")
        w_first, hi_ready, lo_ready, v_ready = sem("w_first"), sem("hi_ready"), sem("lo_ready"), sem("v_ready")
        stored, v_stored = [sem("stored0"), sem("stored1")], [sem("v_stored0"), sem("v_stored1")]
        QK = 2 * KC * BLOCKS
        block = ctx.enter_context(nc.Block())

        @block.sync
        def _(sp):
            for k in range(3):
                sp.dma_start(raw[k].rearrange("p (c e) -> p c e", c=KC),
                             a["wqkvT"][k].rearrange("(c p) e -> p c e", p=P)).then_inc(w_in[k], 16)
            for q in range(QK):
                which, unit = q // (KC * BLOCKS), (q % BLOCKS) * KC + (q // BLOCKS) % KC
                sp.wait_ge(hi_ready, q + 1)
                sp.dma_start(g.qk_dram[which, 0, unit], hi[:, q % 2, :].bitcast(F32)).then_inc(stored[q % 2], 16)
                sp.wait_ge(lo_ready, q + 1)
                sp.dma_start(g.qk_dram[which, 1, unit], lo[:, q % 2, :].bitcast(F32)).then_inc(stored[q % 2], 16)
            for t in range(TILES):
                sp.wait_ge(v_ready, t + 1)
                sp.dma_start(g.v_dram[t], v[:, t % 2].rearrange("p h d -> p (h d)")).then_inc(v_stored[t % 2], 16)
            for k in range(2):
                sp.wait_ge(stored[k], 16 * QK)
                sp.wait_ge(v_stored[k], 16 * TILES // 2)

        @block.gpsimd
        def _(pool):
            nc.gpsimd.memset(v[:], 0.0).then_inc(pads, 1)
            pool.wait_ge(pads, 1)
            nc.gpsimd.memset(v[:, :, :, DK:DK + 1], 1.0).then_inc(pads, 1)
            for k in (1, 2):
                pool.wait_ge(w_in[k], 16)
                nc.gpsimd.tensor_scalar(wh[k][:], raw[k], 1.0, 0.0, ALU.mult, ALU.add).then_inc(w_hi, 1)
                pool.wait_ge(w_hi, k)
                nc.gpsimd.tensor_tensor(wl[k][:], raw[k], wh[k][:].bitcast(F32), ALU.subtract).then_inc(w_split, 1)

        @block.tensor
        def _(pe):
            def bank_free(n):
                if n >= QK + 4:
                    pe.wait_ge(v_ready, n - QK - 3)
                elif n >= 4:
                    pe.wait_ge(lo_ready, n - 3)

            for q in range(QK):
                which, c_out, b = q // (KC * BLOCKS), (q // BLOCKS) % KC, q % BLOCKS
                if q == 0:
                    pe.wait_ge(w_first, 2)
                if q == QK // 2:
                    pe.wait_ge(w_split, 1)
                bank_free(q)
                for c in range(KC):
                    w = slice(c * DIM + c_out * P, c * DIM + (c_out + 1) * P)
                    mm = three(pe, po[q % 4][:], wh[which][:, w], wl[which][:, w], g.XH[:, c, b * NB:(b + 1) * NB],
                               g.XL[:, c, b * NB:(b + 1) * NB], c == 0, c == KC - 1)
                mm.then_inc(product, 1)
            pe.wait_ge(w_split, 2)
            for t in range(TILES):
                bank_free(QK + t)
                for c in range(KC):
                    w = slice(c * DIM, (c + 1) * DIM)
                    cols = slice(t * P, (t + 1) * P)
                    mm = three(pe, po[t % 4][:], g.XH[:, c, cols], g.XL[:, c, cols], wh[2][:, w], wl[2][:, w],
                               c == 0, c == KC - 1)
                mm.then_inc(product, 1)

        @block.scalar
        def _(act):
            act.wait_ge(w_in[0], 16)
            nc.scalar.activation(wh[0][:], raw[0], ACT.Copy).then_inc(w_first, 1)
            for q in range(QK):
                act.wait_ge(product, q + 1)
                if q >= 2:
                    act.wait_ge(stored[q % 2], 32 * (q // 2))
                nc.scalar.activation(hi[:, q % 2, :], po[q % 4][:], ACT.Copy).then_inc(hi_ready, 1)
            act.wait_ge(pads, 2)
            for t in range(TILES):
                act.wait_ge(product, QK + t + 1)
                if t >= 2:
                    act.wait_ge(v_stored[t % 2], 16 * (t // 2))
                nc.scalar.activation(v[:, t % 2, :, 0:DK], po[t % 4][:].rearrange("p (h d) -> p h d", d=DK),
                                     ACT.Copy).then_inc(v_ready, 1)

        @block.vector
        def _(dve):
            dve.wait_ge(w_first, 1)
            nc.vector.tensor_tensor(wl[0][:], raw[0], wh[0][:].bitcast(F32), ALU.subtract).then_inc(w_first, 1)
            for q in range(QK):
                dve.wait_ge(hi_ready, q + 1)
                nc.vector.tensor_tensor(lo[:, q % 2, :], po[q % 4][:], hi[:, q % 2, :].bitcast(F32),
                                        ALU.subtract).then_inc(lo_ready, 1)


def attend(nc, a, g):
    with ExitStack() as ctx:
        sb, ps, sem = scoped(nc, ctx, "att")
        SET = 4
        SETS = HEADS // SET
        RING = 4
        STEPS = 4
        LEAD = 7
        PER_B = SETS * STEPS
        MROW = 96
        qs = [sb(f"qs{k}", [P, SET, NB], F32R) for k in range(RING)]
        ks = [sb(f"ks{k}", [P, SET, NB], F32R) for k in range(RING)]
        v = [sb(f"v{k}", [P, STEPS, SET * VPAD]) for k in range(RING)]
        prob = [sb(f"prob{k}", [P, SET, NB]) for k in range(2)]
        top = [sb(f"top{k}", [P, STEPS, SET]) for k in range(2)]
        mh = [sb(f"mh{k}", [SET, NB], F32R) for k in range(2)]
        ml = [sb(f"ml{k}", [SET, NB], F32R) for k in range(2)]
        o_sb = [sb(f"o_sb{k}", [P, NB]) for k in range(2)]
        rec = sb("rec", [P, STEPS, SET])
        p_first = [ps(f"first{k}", [P, NB]) for k in range(2)]
        p_second = ps("second", [P, SET, NB])
        p_out = ps("out", [P, NB])
        p_turn = ps("turn", [P, NB])
        loaded = [sem(f"loaded{k}") for k in range(RING)]
        v_in = [sem(f"v_in{k}") for k in range(RING)]
        m_in = [sem(f"m_in{k}") for k in range(RING)]
        q_pads, k_pads, first_ready, second_ready, max_turned = sem("q_pads"), sem("k_pads"), sem("first_ready"), sem("second_ready"), sem("max_turned")
        mh_ready, ml_ready, dve_chain = sem("mh_ready"), sem("ml_ready"), sem("dve_chain")
        exp_done, exp_0 = sem("exp_done"), 2
        pv_done, pv_0 = sem("pv_done"), RING * STEPS
        max_done, max_0 = sem("max_done"), 2
        turned_m, turned_0 = sem("turned_m"), 2
        o_copied, copied_0 = sem("o_copied"), 1
        o_turned, o_turned_0 = sem("o_turned"), 2
        o_done, o_done_0 = sem("o_done"), 2
        block = ctx.enter_context(nc.Block())

        def load(sp, b, w):
            slot = w % RING
            sp.wait_ge(pv_done, PER_B * b + STEPS * (w - RING) + STEPS + pv_0)
            unit, half = b * KC + w // 2, w % 2
            for dst, which, parts in ((qs, 0, (0, 0, 1, 1)), (ks, 1, (0, 1, 0, 1))):
                for r, part in enumerate(parts):
                    src = g.qk_dram[which, part, bass.ds(unit, 1), half * SET * DK:(half + 1) * SET * DK, :]
                    sp.dma_start(dst[slot][r * DK:(r + 1) * DK, :, :].bitcast(F32),
                                 src.rearrange("u (h d) t -> d (u h) t", d=DK)).then_inc(loaded[slot], 16)
            cols = slice(SET * VPAD * (w % SETS), SET * VPAD * (w % SETS + 1))
            sp.dma_start(v[slot][:], g.v_dram[bass.ds((b + w // SETS) * STEPS, STEPS), :, cols].rearrange("t p c -> p t c")
                         ).then_inc(v_in[slot], 16)

        def load_max(sp, b, w):
            sp.wait_ge(ml_ready, SETS * b + w + 1)
            for r, src in ((0, mh), (1, ml)):
                rows = slice(MROW + r * SET, MROW + (r + 1) * SET)
                sp.dma_start(qs[w % RING][rows, :, :].bitcast(F32),
                             src[w % 2][:].bitcast(F32).unsqueeze(1).to_broadcast([SET, SET, NB])
                             ).then_inc(m_in[w % RING], 16)

        @block.sync
        def _(sp):
            for w in range(3):
                load(sp, 0, w)
            sp.wait_ge(q_pads, RING)
            load_max(sp, 0, 0)

            def batch(b, last):
                for s in range(SETS):
                    if not (last and s + 3 >= SETS):
                        load(sp, b, s + 3)
                    if not (last and s + 1 >= SETS):
                        load_max(sp, b, s + 1)

            with sp.Fori(0, BATCH - 1) as b:
                batch(b, False)
            batch(BATCH - 1, True)

        @block.gpsimd
        def _(pool):
            for k in range(RING):
                nc.gpsimd.memset(ks[k][64:P, :, :].bitcast(F32), 0.0).then_inc(k_pads, 1)
                pool.wait_ge(k_pads, 3 * k + 1)
                rows = ks[k][MROW:MROW + 2 * SET, :, :]
                for part in range(2):
                    nc.gpsimd.affine_select(out=rows, in_=rows.bitcast(F32), compare_op=ALU.not_equal, fill=1.0, base=-part * SET,
                                            pattern=[[-1, SET], [0, NB]], channel_multiplier=1).then_inc(k_pads, 1)
                    pool.wait_ge(k_pads, 3 * k + 2 + part)

        @block.tensor
        def _(pe):
            pe.sem_inc(pv_done, pv_0)
            pe.sem_inc(turned_m, turned_0)
            pe.sem_inc(o_turned, o_turned_0)

            def first(b, step, item):
                w, n = step // STEPS, (step % STEPS) * 4 + item
                head, qt = n // 4, n % 4
                if n == 0:
                    if isinstance(b, int) and b == 0 and w < RING:
                        pe.wait_ge(q_pads, w + 1)
                        pe.wait_ge(k_pads, 3 * w + 3)
                    pe.wait_ge(loaded[w % RING], 128 * (SETS // RING) * b + 128 * (w // RING + 1))
                m = 4 * step + item
                pe.wait_ge(max_done, 4 * PER_B * b + m - 1 + max_0)
                pe.matmul(p_first[m % 2][:], qs[w % RING][0:MROW, head, qt * P:(qt + 1) * P],
                          ks[w % RING][0:MROW, head, :], start=True, stop=True).then_inc(first_ready, 1)

            def turn_max(b, w):
                pe.wait_ge(max_done, 4 * PER_B * b + 4 * STEPS * (w + 1) + max_0)
                if not (isinstance(b, int) and b == 0 and w == 0):
                    pe.wait_ge(o_done, SETS * b + w - 2 + o_done_0)
                for qt in range(4):
                    mm = pe.transpose(p_turn[0:SET, qt * P:(qt + 1) * P], top[w % 2][:, qt, :], g.ident[:])
                mm.then_inc(turned_m, 1)

            def second(b, step, pair):
                s, kt = step // STEPS, step % STEPS
                if kt == 0 and pair == 0:
                    pe.wait_ge(m_in[s % RING], 32 * (SETS // RING) * b + 32 * (s // RING + 1))
                pe.wait_ge(exp_done, 2 * (PER_B * b + step - 1) + pair + 1 + exp_0)
                for j in range(2 * pair, 2 * pair + 2):
                    mm = pe.matmul(p_second[:, j, :], ks[s % RING][:, j, kt * P:(kt + 1) * P], qs[s % RING][:, j, :],
                                   start=True, stop=True)
                mm.then_inc(second_ready, 1)

            def weigh(b, step):
                s, kt = step // STEPS, step % STEPS
                if kt == 0:
                    pe.wait_ge(v_in[s % RING], 16 * (SETS // RING) * b + 16 * (s // RING + 1))
                    pe.wait_ge(o_copied, SETS * b + s + copied_0)
                pe.wait_ge(exp_done, 2 * (PER_B * b + step) + 2 + exp_0)
                for j in range(SET):
                    mm = pe.matmul(p_out[VPAD * j:VPAD * (j + 1), :], v[s % RING][:, kt, VPAD * j:VPAD * (j + 1)],
                                   prob[step % 2][:, j, :], start=(kt == 0), stop=(kt == STEPS - 1))
                mm.then_inc(pv_done, 1)

            def turn_out(b, s, maxima):
                pe.wait_ge(o_copied, SETS * b + s + 1 + copied_0)
                if maxima:
                    pe.wait_ge(ml_ready, SETS * b + s + 3)
                else:
                    pe.wait_ge(o_done, SETS * b + s + o_done_0)
                for qt in range(4):
                    mm = pe.transpose(p_turn[:, qt * P:(qt + 1) * P], o_sb[s % 2][:, qt * P:(qt + 1) * P], g.ident[:])
                mm.then_inc(o_turned, 1)

            for step in range(LEAD):
                for item in range(4):
                    first(0, step, item)
                if step == STEPS:
                    turn_max(0, 0)

            def batch(b, begin, last):
                for step in range(PER_B):
                    ahead = not (last and step + LEAD >= PER_B)
                    s, kt = step // STEPS, step % STEPS
                    second(b, step, 0)
                    if ahead:
                        first(b, step + LEAD, 0)
                    second(b, step, 1)
                    if ahead:
                        first(b, step + LEAD, 1)
                    if not (begin and step == 0):
                        weigh(b, step - 1)
                    if ahead:
                        first(b, step + LEAD, 2)
                        first(b, step + LEAD, 3)
                    maxima = not (last and s + 1 >= SETS)
                    if kt == 1 and maxima:
                        turn_max(b, s + 1)
                    if kt == 2 and not (begin and s == 0):
                        turn_out(b, s - 1, maxima)

            batch(0, True, False)
            with pe.Fori(1, BATCH - 1) as b:
                batch(b, False, False)
            batch(BATCH - 1, False, True)
            weigh(BATCH - 1, PER_B - 1)
            turn_out(BATCH - 1, SETS - 1, False)

        @block.scalar
        def _(act):
            act.sem_inc(exp_done, exp_0)
            act.sem_inc(o_copied, copied_0)

            def exps(b, step, pair):
                act.wait_ge(second_ready, 2 * (PER_B * b + step) + pair + 1)
                act.wait_ge(pv_done, PER_B * b + step - 1 + pv_0)
                js = slice(2 * pair, 2 * pair + 2)
                nc.scalar.activation(prob[step % 2][:, js, :], p_second[:, js, :], ACT.Exp,
                                     scale=DK ** -0.5).then_inc(exp_done, 1)

            def high_max(b, w):
                act.wait_ge(turned_m, SETS * b + w + 1 + turned_0)
                nc.scalar.activation(mh[w % 2][:], p_turn[0:SET, :], ACT.Copy, scale=-1.0).then_inc(mh_ready, 1)

            def copy_out(b, s):
                act.wait_ge(pv_done, PER_B * b + STEPS * (s + 1) + pv_0)
                act.wait_ge(o_turned, SETS * b + s - 1 + o_turned_0)
                nc.scalar.activation(o_sb[s % 2][:], p_out[:], ACT.Copy).then_inc(o_copied, 1)

            high_max(0, 0)

            def batch(b, begin, last):
                for step in range(PER_B):
                    s, kt = step // STEPS, step % STEPS
                    exps(b, step, 0)
                    if kt == 2 and not (last and s + 1 >= SETS):
                        high_max(b, s + 1)
                    exps(b, step, 1)
                    if kt == 0 and not (begin and s == 0):
                        copy_out(b, s - 1)

            batch(0, True, False)
            with act.Fori(1, BATCH - 1) as b:
                batch(b, False, False)
            batch(BATCH - 1, False, True)
            copy_out(BATCH - 1, SETS - 1)

        @block.vector
        def _(dve):
            dve.sem_inc(max_done, max_0)
            dve.sem_inc(o_done, o_done_0)
            for k in range(RING):
                nc.vector.memset(qs[k][64:P, :, :].bitcast(F32), 0.0).then_inc(q_pads, 1)

            def maximum(b, step, item):
                w, n = step // STEPS, (step % STEPS) * 4 + item
                head, qt = n // 4, n % 4
                m = 4 * step + item
                if n == 0:
                    dve.wait_ge(turned_m, SETS * b + w - 1 + turned_0)
                dve.wait_ge(first_ready, 4 * PER_B * b + m + 1)
                nc.vector.tensor_reduce(top[w % 2][:, qt, head:head + 1], p_first[m % 2][:], AX.X,
                                        ALU.max).then_inc(max_done, 1)

            def low_max(b, w):
                dve.wait_ge(mh_ready, SETS * b + w + 1)
                nc.vector.scalar_tensor_tensor(out=ml[w % 2][:], in0=p_turn[0:SET, :], scalar=-1.0,
                                               in1=mh[w % 2][:].bitcast(F32), op0=ALU.mult,
                                               op1=ALU.subtract).then_inc(ml_ready, 1)

            def divide(b, s):
                dve.wait_ge(o_turned, SETS * b + s + 1 + o_turned_0)
                o = p_turn[:].rearrange("p (t h d) -> p t h d", t=STEPS, h=SET)
                nc.vector.reciprocal(rec[:].unsqueeze(3), o[:, :, :, DK:DK + 1]).then_inc(dve_chain, 1)
                dve.wait_ge(dve_chain, SETS * b + s + 1)
                tile = (b + s // SETS) * PER_BLOCK
                at = (s % SETS) * SET * DK
                dst = g.Y[:, bass.ds(tile, PER_BLOCK), at:at + SET * DK].rearrange("p t (h d) -> p t h d", d=DK)
                nc.vector.tensor_tensor(dst, o[:, :, :, 0:DK], rec[:].unsqueeze(3).to_broadcast([P, STEPS, SET, DK]),
                                        ALU.mult).then_inc(o_done, 1)

            for step in range(LEAD):
                for item in range(4):
                    maximum(0, step, item)
                if step == STEPS:
                    low_max(0, 0)

            def batch(b, begin, last):
                for step in range(PER_B):
                    s, kt = step // STEPS, step % STEPS
                    ahead = not (last and step + LEAD >= PER_B)
                    for item in range(4):
                        if ahead:
                            maximum(b, step + LEAD, item)
                        if item == 1 and kt == 2 and not (last and s + 1 >= SETS):
                            low_max(b, s + 1)
                        if item == 1 and kt == 3 and not (begin and s == 0):
                            divide(b, s - 1)

            batch(0, True, False)
            with dve.Fori(1, BATCH - 1) as b:
                batch(b, False, False)
            batch(BATCH - 1, False, True)
            divide(BATCH - 1, SETS - 1)


def attention_out(nc, a, g):
    with ExitStack() as ctx:
        sb, ps, sem = scoped(nc, ctx, "wo")
        raw = sb("raw", [P, KC * DIM])
        wh = sb("wh", [P, KC * DIM], F32R)
        wl = sb("wl", [P, KC * DIM], F32R)
        th = sb("th", [P, 2, KC, P], F32R)
        tl = sb("tl", [P, 2, KC, P], F32R)
        pt = [ps(f"pt{k}", [P, KC, P]) for k in range(2)]
        po = [ps(f"po{k}", [P, DIM]) for k in range(2)]
        w_in, w_split = sem("w_in"), sem("w_split")
        turned, hi_ready, lo_ready, product, added = (sem("turned"), sem("hi_ready"), sem("lo_ready"), sem("product"),
                                                      sem("added"))
        block = ctx.enter_context(nc.Block())

        @block.sync
        def _(sp):
            sp.dma_start(raw[:].rearrange("p (c e) -> p c e", c=KC),
                         a["woT"].rearrange("(c p) e -> p c e", p=P)).then_inc(w_in, 16)

        @block.tensor
        def _(pe):
            for t in range(TILES + 1):
                if t < TILES:
                    if t >= 2:
                        pe.wait_ge(lo_ready, t - 1)
                    for c in range(KC):
                        mm = pe.transpose(pt[t % 2][:, c, :], g.Y[:, t, c * P:(c + 1) * P], g.ident[:])
                    mm.then_inc(turned, 1)
                if t:
                    m = t - 1
                    if m == 0:
                        pe.wait_ge(w_split, 2)
                    if m >= 2:
                        pe.wait_ge(added, m - 1)
                    pe.wait_ge(lo_ready, m + 1)
                    for c in range(KC):
                        w = slice(c * DIM, (c + 1) * DIM)
                        mm = three(pe, po[m % 2][:], th[:, m % 2, c, :], tl[:, m % 2, c, :], wh[:, w], wl[:, w],
                                   c == 0, c == KC - 1)
                    mm.then_inc(product, 1)

        @block.scalar
        def _(act):
            act.wait_ge(w_in, 16)
            nc.scalar.activation(wh[:], raw[:], ACT.Copy).then_inc(w_split, 1)
            for t in range(TILES):
                act.wait_ge(turned, t + 1)
                if t >= 2:
                    act.wait_ge(product, t - 1)
                nc.scalar.activation(th[:, t % 2], pt[t % 2][:], ACT.Copy).then_inc(hi_ready, 1)

        @block.vector
        def _(dve):
            dve.wait_ge(w_split, 1)
            nc.vector.tensor_tensor(wl[:], raw[:], wh[:].bitcast(F32), ALU.subtract).then_inc(w_split, 1)
            for t in range(TILES + 1):
                if t < TILES:
                    dve.wait_ge(hi_ready, t + 1)
                    nc.vector.tensor_tensor(tl[:, t % 2], pt[t % 2][:], th[:, t % 2].bitcast(F32),
                                            ALU.subtract).then_inc(lo_ready, 1)
                if t:
                    m = t - 1
                    dve.wait_ge(product, m + 1)
                    nc.vector.tensor_tensor(g.Y[:, m, :], po[m % 2][:], g.X[:, m, :], ALU.add).then_inc(added, 1)


def quantised_mlp(nc, a, g):
    with ExitStack() as ctx:
        sb, ps, sem = scoped(nc, ctx, "ffn")
        PAIR = 2 * P
        W13 = KC * 2 * PAIR
        WN = W13 + 2 * DIM
        scales = sb("scales", [P, FPAIRS, WN // P])
        raw = sb("raw", [P, WN])
        wh = [sb(f"wh{s}", [P, WN], F32R) for s in range(2)]
        wl = [sb(f"wl{s}", [P, WN], F32R) for s in range(2)]
        silu = sb("silu", [P, 2, PAIR])
        h = sb("h", [P, PAIR])
        hq = sb("hq", [P, 2, PAIR])
        amax = sb("amax", [P, 2])
        scale = sb("scale", [P, 2])
        inv = sb("inv", [P, 2])
        hh = sb("hh", [P, 2, 2, P], F32R)
        hl = sb("hl", [P, 2, 2, P], F32R)
        pg = [ps(f"pg{k}", [P, 2 * PAIR]) for k in range(2)]
        pt = [ps(f"pt{k}", [P, 2, P]) for k in range(2)]
        py = [ps(f"py{k}", [P, DIM]) for k in range(2)]
        w_in, sc_in, pool_chain, dve_chain = sem("w_in"), sem("sc_in"), sem("pool_chain"), sem("dve_chain")
        g_ready, s_ready, hh_ready = sem("g_ready"), sem("s_ready"), sem("hh_ready")
        split_ready, split_0 = sem("split_ready"), 1
        u_used, used_0 = sem("u_used"), 2
        turned, turned_0 = sem("turned"), 2
        hq_ready, hq_0 = sem("hq_ready"), 2
        hl_ready, hl_0 = sem("hl_ready"), 2
        y_ready, y_0 = sem("y_ready"), 2 * TILES
        y_added, added_0 = sem("y_added"), TILES
        block = ctx.enter_context(nc.Block())

        def pairs(eng, body):
            with eng.Fori(0, FPAIRS // 2) as i:
                for s in range(2):
                    body(2 * i + s, s)
            body(FPAIRS - 1, 0)

        @block.sync
        def _(sp):
            sp.dma_start(scales[:], a["scales"].partition_broadcast(P)).then_inc(sc_in, 16)

            def fetch(p, s):
                sp.wait_ge(split_ready, p + split_0)
                sp.dma_start(raw[:], a["w132"][p]).then_inc(w_in, 16)

            pairs(sp, fetch)

        @block.gpsimd
        def _(pool):
            pool.sem_inc(split_ready, split_0)
            pool.wait_ge(sc_in, 16)

            def split(p, s):
                wait_apart(pool, w_in, 16 * p + 16)
                blocks = raw[:].rearrange("p (n k) -> p n k", k=P)
                sc = scales[:, bass.ds(p, 1), :].rearrange("p a n -> p (a n)").unsqueeze(2).to_broadcast([P, WN // P, P])
                nc.gpsimd.tensor_tensor(blocks, blocks, sc, ALU.mult).then_inc(pool_chain, 1)
                pool.wait_ge(pool_chain, 2 * p + 1)
                wait_apart(pool, y_ready, (p - 1) * TILES + y_0)
                nc.gpsimd.tensor_scalar(wh[s][:], raw[:], 1.0, 0.0, ALU.mult, ALU.add).then_inc(pool_chain, 1)
                pool.wait_ge(pool_chain, 2 * p + 2)
                nc.gpsimd.tensor_tensor(wl[s][:], raw[:], wh[s][:].bitcast(F32), ALU.subtract).then_inc(split_ready, 1)

            pairs(pool, split)

        @block.tensor
        def _(pe):
            pe.sem_inc(y_ready, y_0)
            pe.sem_inc(turned, turned_0)

            def pair(p, s):
                def up(t):
                    pe.wait_ge(u_used, TILES * p + t - 1 + used_0)
                    for c in range(KC):
                        w = slice(c * 2 * PAIR, (c + 1) * 2 * PAIR)
                        cols = slice(t * P, (t + 1) * P)
                        mm = three(pe, pg[t % 2][:], g.XH[:, c, cols], g.XL[:, c, cols], wh[s][:, w], wl[s][:, w],
                                   c == 0, c == KC - 1)
                    mm.then_inc(g_ready, 1)

                def turn(t):
                    pe.wait_ge(hq_ready, TILES * p + t + 1 + hq_0)
                    pe.wait_ge(hl_ready, TILES * p + t - 1 + hl_0)
                    for i in range(2):
                        mm = pe.transpose(pt[t % 2][:, i, :], hq[:, t % 2, i * P:(i + 1) * P], g.ident[:])
                    mm.then_inc(turned, 1)

                def down(t):
                    pe.wait_ge(hl_ready, TILES * p + t + 1 + hl_0)
                    pe.wait_ge(y_added, TILES * p + t - 1 + added_0)
                    for i in range(2):
                        w = slice(W13 + i * DIM, W13 + (i + 1) * DIM)
                        mm = three(pe, py[t % 2][:], hh[:, t % 2, i, :], hl[:, t % 2, i, :], wh[s][:, w], wl[s][:, w],
                                   i == 0, i == 1)
                    mm.then_inc(y_ready, 1)

                pe.wait_ge(split_ready, p + 1 + split_0)
                for t in range(TILES + 2):
                    if t < TILES:
                        up(t)
                    if 1 <= t <= TILES:
                        turn(t - 1)
                    if t >= 2:
                        down(t - 2)

            pairs(pe, pair)

        @block.scalar
        def _(act):
            def pair(p, s):
                for t in range(TILES + 1):
                    if t < TILES:
                        act.wait_ge(g_ready, TILES * p + t + 1)
                        act.wait_ge(u_used, TILES * p + t - 1 + used_0)
                        nc.scalar.activation(silu[:, t % 2, :], pg[t % 2][:, 0:PAIR], ACT.Silu).then_inc(s_ready, 1)
                    if t:
                        m = t - 1
                        act.wait_ge(turned, TILES * p + m + 1 + turned_0)
                        act.wait_ge(y_ready, TILES * p + m - 1 + y_0)
                        nc.scalar.activation(hh[:, m % 2], pt[m % 2][:], ACT.Copy).then_inc(hh_ready, 1)

            pairs(act, pair)

        @block.vector
        def _(dve):
            own = Chain(dve, dve_chain)
            dve.sem_inc(u_used, used_0)
            dve.sem_inc(hq_ready, hq_0)
            dve.sem_inc(hl_ready, hl_0)
            dve.sem_inc(y_added, added_0)
            PER_TILE = 4

            def pair(p, s):
                def hidden(t):
                    n = TILES * p + t
                    own.base, own.n = PER_TILE * n, 0
                    dve.wait_ge(s_ready, n + 1)
                    dve.wait_ge(hq_ready, n + hq_0)
                    nc.vector.tensor_tensor(h[:], pg[t % 2][:, PAIR:2 * PAIR], silu[:, t % 2, :],
                                            ALU.mult).then_inc(u_used, 1)
                    dve.wait_ge(u_used, n + 1 + used_0)
                    own.step(nc.vector.tensor_reduce(amax[:], h[:].rearrange("p (i k) -> p i k", k=P), AX.X, ALU.max,
                                                     apply_absolute_value=True))
                    own.settle()
                    own.step(nc.vector.tensor_scalar(scale[:], amax[:], 1.0 / FP8_MAX, 1e-12, ALU.mult, ALU.add))
                    own.settle()
                    own.step(nc.vector.reciprocal(inv[:], scale[:]))
                    own.settle()
                    dve.wait_ge(turned, n - 1 + turned_0)
                    own.step(nc.vector.tensor_scalar(hq[:, t % 2, 0:P], h[:, 0:P], inv[:, 0:1], scale[:, 0:1],
                                                     ALU.mult, ALU.mult))
                    nc.vector.tensor_scalar(hq[:, t % 2, P:PAIR], h[:, P:PAIR], inv[:, 1:2], scale[:, 1:2],
                                            ALU.mult, ALU.mult).then_inc(hq_ready, 1)

                def low(t):
                    dve.wait_ge(hh_ready, TILES * p + t + 1)
                    nc.vector.tensor_tensor(hl[:, t % 2], pt[t % 2][:], hh[:, t % 2].bitcast(F32),
                                            ALU.subtract).then_inc(hl_ready, 1)

                def add(t):
                    dve.wait_ge(y_ready, TILES * p + t + 1 + y_0)
                    dve.wait_ge(y_added, TILES * (p - 1) + t + 1 + added_0)
                    nc.vector.tensor_tensor(g.Y[:, t, :], py[t % 2][:], g.Y[:, t, :], ALU.add).then_inc(y_added, 1)

                for t in range(TILES + 2):
                    if t < TILES:
                        hidden(t)
                    if 1 <= t <= TILES:
                        low(t - 1)
                    if t >= 2:
                        add(t - 2)

            pairs(dve, pair)


class Shared:
    pass


def program(nc, a, out):
    g = Shared()
    g.brow_dram = nc.dram_tensor("brow_dram", [STATE, BATCH, NB], F32, kind="Internal").ap()
    g.qk_dram = nc.dram_tensor("qk_dram", [2, 2, UNITS, P, NB], F32, kind="Internal").ap()
    g.v_dram = nc.dram_tensor("v_dram", [TILES, P, HEADS * VPAD], F32, kind="Internal").ap()
    with ExitStack() as ctx:
        sb, _, sem = scoped(nc, ctx, "all")
        g.ident = sb("ident", [P, P])
        g.gate = sb("gate", [P, MLPS, TILES])
        sums = sb("sums", [P, KC * TOK])
        g.sums = sums
        g.XT = sums[:].rearrange("p (c t) -> p c t", c=KC)
        g.Y = sums[:].rearrange("p (t d) -> p t d", t=TILES)
        g.X = sb("X", [P, TILES, DIM])
        with ExitStack() as ssm:
            sb, _, _ = scoped(nc, ssm, "ssm")
            g.sel = sb("sel", [STATE, STATE, P])
            g.A = sb("A", [P, KC, STATE])
            g.D1 = sb("D1", [P, KC])
            g.DT = sb("DT", [P, KC, TOK])
            g.U = sb("U", [P, KC, TOK])
            g.CT = sb("CT", [STATE, TOK])
            ssm_inputs(nc, a, g)
            ssm_scan(nc, a, g)
        with ExitStack() as later:
            sb, _, _ = scoped(nc, later, "later")
            g.XH = sb("XH", [P, KC, TOK], F32R)
            g.XL = sb("XL", [P, KC, TOK], F32R)
            normalise(nc, g, "ln1", True)
            route(nc, a, g)
            experts(nc, a, g)
            normalise(nc, g, "ln2", False)
            project(nc, a, g)
        attend(nc, a, g)
        attention_out(nc, a, g)
        with ExitStack() as later:
            sb, _, _ = scoped(nc, later, "last")
            g.XH = sb("XH", [P, KC, TOK], F32R)
            g.XL = sb("XL", [P, KC, TOK], F32R)
            normalise(nc, g, "ln3", False, quantise=True)
            quantised_mlp(nc, a, g)
        normalise(nc, g, "ln4", False, out)


def laid_out(x):
    import numpy as np

    def dense(v):
        return np.ascontiguousarray(v)

    def columns(v):
        return dense(v.reshape(-1, P).T)

    def halves(w):
        return w.reshape(DIM, 2, INTER).transpose(1, 0, 2)

    def folded(w):
        return w.reshape(MLPS, KC, P, INTER).transpose(0, 2, 1, 3).reshape(MLPS, P, KC * INTER)

    def by_pair(w):
        return w.T.reshape(KC, P, FPAIRS, 2 * P)

    w1 = np.concatenate([x["L0_ffn_ew1"], halves(x["L0_ffn_sw1"])])
    w2 = np.concatenate([x["L0_ffn_ew2"], halves(x["L0_ffn_sw2"])])
    w3 = np.concatenate([x["L0_ffn_ew3"], x["L0_ffn_sw3"].reshape(2, INTER, DIM)])
    b1 = np.concatenate([x["L0_ffn_eb1"], x["L0_ffn_sb1"].reshape(2, INTER)])
    b2 = np.concatenate([x["L0_ffn_eb2"], x["L0_ffn_sb2"].reshape(2, INTER)])
    b3 = np.concatenate([x["L0_ffn_eb3"], x["L0_ffn_sb3"].reshape(1, DIM), np.zeros((1, DIM), np.float32)])
    w13 = np.stack([by_pair(x["L1_ffn_w1"]), by_pair(x["L1_ffn_w3"])], 3)
    w13 = w13.transpose(2, 1, 0, 3, 4).reshape(FPAIRS, P, KC * 4 * P)
    down = x["L1_ffn_w2"].T.reshape(FPAIRS, 2, P, DIM).transpose(0, 2, 1, 3).reshape(FPAIRS, P, 2 * DIM)
    s1, s3 = (x[n].reshape(FPAIRS, 2, KC) for n in ("L1_ffn_w1_scale", "L1_ffn_w3_scale"))
    s13 = np.stack([s1, s3], 1).transpose(0, 3, 1, 2).reshape(FPAIRS, 4 * KC)
    s2 = x["L1_ffn_w2_scale"].T.reshape(FPAIRS, 2 * KC)
    return {
        "xT": dense(x["L0_attn_x"].reshape(TOK, DIM).T),
        "xprojT": dense(x["L0_attn_x_proj_w"].T),
        "dtprojT": dense(x["L0_attn_dt_proj_w"].T),
        "dtb": columns(x["L0_attn_dt_proj_b"]),
        "alog": dense(x["L0_attn_A_log"]),
        "dcoef": columns(x["L0_attn_D"]),
        "router_w": dense(x["L0_ffn_router_w"]),
        "router_b": dense(x["L0_ffn_router_b"]),
        "router_bias": dense(x["L0_ffn_router_bias"]),
        "order": np.arange(EXPERTS, 0, -1, dtype=np.float32),
        "w123": dense(np.concatenate([folded(w1), folded(w2), w3], axis=2)),
        "b12": dense(np.stack([b1, b2], -1).transpose(1, 0, 2)),
        "b3": b3,
        "wqkvT": dense(np.stack([x[f"L1_attn_w_{n}"].T for n in "qkv"])),
        "woT": dense(x["L1_attn_w_o"].T),
        "w132": dense(np.concatenate([w13, down], axis=2)),
        "scales": dense(np.concatenate([s13, s2], axis=1)),
    }


def kernel(**inputs):
    import numpy as np
    import concourse.bacc as bacc
    from concourse.bass_utils import run_bass_kernel_spmd

    nc = bacc.Bacc("TRN2", target_bir_lowering=False, num_devices=1)
    arrays = laid_out({n: np.asarray(v) for n, v in inputs.items()})
    aps = {n: nc.dram_tensor(f"in_{n}", v.shape, mybir.dt.from_np(v.dtype), kind="ExternalInput").ap()
           for n, v in arrays.items()}
    out = nc.dram_tensor("out_x", (TOK, DIM), F32, kind="ExternalOutput").ap()
    program(nc, aps, out)
    result = run_bass_kernel_spmd(nc, [{f"in_{n}": v for n, v in arrays.items()}], core_ids=[0])
    return result.results[0]["out_x"].reshape(BATCH, SEQ, DIM)
```

```python
from contextlib import ExitStack


import concourse.bass as bass
from concourse import mybir

F32 = mybir.dt.float32
F32R = mybir.dt.float32r
ALU = mybir.AluOpType
ACT = mybir.ActivationFunctionType
AX = mybir.AxisListType

P = 128
BATCH, SEQ, DIM = 4, 512, 512
TOK = BATCH * SEQ
KC = DIM // P
TILES = TOK // P
NB = 512
BLOCKS = TOK // NB
PER_BLOCK = NB // P
STATE, RANK = 16, 16
EXPERTS, GROUPS, INTER = 16, 4, 128
MLPS = EXPERTS + 2
TOP = 2
TURN = 4
SORTED = -(-(TOP * TILES + EXPERTS - 1) // TURN) * TURN
WUP = 2 * KC * INTER
WN = WUP + DIM
HEADS, DK = 32, 16
GHEADS = P // DK
UNITS = BATCH * KC
VPAD = 32
FFN_INTER = 1792
FBLOCKS = FFN_INTER // P
FPAIRS = FBLOCKS // 2
EPS = 1e-5
FP8_MAX = 448.0
BIG = 3.0e38


class Chain:

    def __init__(self, eng, sem):
        self.eng, self.sem, self.base, self.n = eng, sem, 0, 0

    def step(self, ins):
        ins.then_inc(self.sem, 1)
        self.n += 1

    def settle(self):
        self.eng.wait_ge(self.sem, self.base + self.n)

    def enter(self, i, per):
        self.start, self.per = self.base + self.n, per
        self.base, self.n = self.start + i * per, 0

    def leave(self, times):
        assert self.n == self.per, (self.n, self.per)
        self.base, self.n = self.start + times * self.per, 0


def clear(nc, sems):
    numbers = sorted(s.num for s in sems)
    with nc.Block() as block:
        @block.gpsimd
        def _(pool):
            first = numbers[0]
            for n, after in zip(numbers, numbers[1:] + [None]):
                if after != n + 1:
                    pool.sem_clear(range(first, n + 1))
                    first = after


def scoped(nc, ctx, tag, reused=False):
    sems = []
    if reused:
        ctx.callback(clear, nc, sems)

    def sb(name, shape, dt=F32):
        return ctx.enter_context(nc.sbuf_tensor(f"{tag}_{name}", shape, dt))

    def ps(name, shape):
        return ctx.enter_context(nc.psum_tensor(f"{tag}_{name}", shape, F32))

    def sem(name):
        sems.append(ctx.enter_context(nc.semaphore(f"{tag}_{name}")))
        return sems[-1]

    return sb, ps, sem


def wait_apart(eng, sem, value):
    eng.wait_ge(sem, value)
    eng.nop(nofuse=True)


def three(pe, out, lh, ll, rh, rl, first, last):
    pe.matmul(out, lh, rh, start=first, stop=False)
    pe.matmul(out, lh, rl, start=False, stop=False)
    return pe.matmul(out, ll, rh, start=False, stop=last)


def ssm_inputs(nc, a, g):
    with ExitStack() as ctx:
        sb, ps, sem = scoped(nc, ctx, "pre", reused=True)
        wx = sb("wx", [P, KC, RANK + 2 * STATE])
        wdt = sb("wdt", [RANK, DIM])
        dtb = sb("dtb", [P, KC])
        alog = sb("alog", [P, KC, STATE])
        dtin = sb("dtin", [RANK, NB])
        brow = sb("brow", [STATE, 2, NB])
        z = sb("z", [P, 2, NB])
        mag = sb("mag", [P, 2, NB])
        e = sb("e", [P, 2, NB])
        ln = sb("ln", [P, 2, NB])
        d = sb("d", [P, 2, NB])
        d1 = sb("d1", [P, 2, NB])
        l1 = sb("l1", [P, 2, NB])
        q = sb("q", [P, 2, NB])
        q2 = sb("q2", [P, 2, NB])
        pp = ps("pp", [P, 3, NB])
        pz = ps("pz", [P, 2, NB])
        loaded, x_in = sem("loaded"), [sem(f"x_in{b}") for b in range(BATCH)]
        rows_ready, rows_copied = sem("rows_ready"), sem("rows_copied")
        z_ready, z_read = sem("z_ready"), sem("z_read")
        act_chain, dve_chain = sem("act_chain"), sem("dve_chain")
        ln_ready, dt_ready, b_stored = sem("ln_ready"), sem("dt_ready"), [sem("b_stored0"), sem("b_stored1")]
        u_ready, zeroed, cleared = sem("u_ready"), sem("zeroed"), sem("cleared")
        zero = sb("zero", [P, DIM])
        CLEARS = SORTED // BATCH
        block = ctx.enter_context(nc.Block())

        @block.sync
        def _(sp):
            sp.dma_start(wx[:], a["xprojT"].rearrange("(c p) r -> p c r", p=P)).then_inc(loaded, 16)
            sp.dma_start(wdt[:], a["dtprojT"]).then_inc(loaded, 16)
            sp.dma_start(dtb[:], a["dtb"]).then_inc(loaded, 16)
            sp.dma_start(alog[:], a["alog"].rearrange("(c p) n -> p c n", p=P)).then_inc(loaded, 16)
            sp.dma_start(g.D1[:], a["dcoef"]).then_inc(loaded, 16)
            for b in range(BATCH):
                sp.dma_start(g.XT[:, :, b * NB:(b + 1) * NB],
                             a["xT"].rearrange("(c p) t -> p c t", p=P)[:, :, b * NB:(b + 1) * NB]).then_inc(x_in[b], 16)
            sp.wait_ge(zeroed, 1)
            for b in range(BATCH):
                rows = g.sorted_x.rearrange("(t p) d -> p t d", p=P)[:, b * CLEARS:(b + 1) * CLEARS, :]
                sp.dma_start(rows, zero[:].unsqueeze(1).to_broadcast([P, CLEARS, DIM])).then_inc(cleared, 16)
                sp.wait_ge(rows_copied, 3 * b + 2)
                sp.dma_start(g.brow_dram[:, b, :], brow[:, b % 2, :]).then_inc(b_stored[b % 2], 16)
            for s in range(2):
                sp.wait_ge(b_stored[s], 16 * BATCH // 2)
            sp.wait_ge(cleared, 16 * BATCH)

        @block.tensor
        def _(pe):
            for b in range(BATCH):
                pe.wait_ge(loaded, 80)
                pe.wait_ge(x_in[b], 16)
                if b:
                    pe.wait_ge(rows_copied, 3 * b)
                for k in range(3):
                    for c in range(KC):
                        mm = pe.matmul(pp[0:RANK, k, :], wx[:, c, k * RANK:(k + 1) * RANK],
                                       g.XT[:, c, b * NB:(b + 1) * NB], start=(c == 0), stop=(c == KC - 1))
                    mm.then_inc(rows_ready, 1)
                pe.wait_ge(rows_copied, 3 * b + 1)
                for c in range(KC):
                    i = b * KC + c
                    if i >= 2:
                        pe.wait_ge(z_read, i - 1)
                    pe.matmul(pz[:, i % 2, :], wdt[:, c * P:(c + 1) * P], dtin[:], start=True,
                              stop=True).then_inc(z_ready, 1)

        @block.scalar
        def _(act):
            own = Chain(act, act_chain)
            act.wait_ge(loaded, 80)
            own.step(nc.scalar.activation(g.A[:], alog[:], ACT.Exp))
            for b in range(BATCH):
                act.wait_ge(rows_ready, 3 * b + 1)
                if b:
                    act.wait_ge(z_ready, KC * b)
                nc.scalar.activation(dtin[:], pp[0:RANK, 0, :], ACT.Copy).then_inc(rows_copied, 1)
                act.wait_ge(rows_ready, 3 * b + 2)
                if b >= 2:
                    act.wait_ge(b_stored[b % 2], 16 * (b // 2))
                nc.scalar.activation(brow[:, b % 2, :], pp[0:STATE, 1, :], ACT.Copy).then_inc(rows_copied, 1)
                act.wait_ge(rows_ready, 3 * b + 3)
                nc.scalar.activation(g.CT[:, b * NB:(b + 1) * NB], pp[0:STATE, 2, :], ACT.Copy).then_inc(rows_copied, 1)
                for c in range(KC):
                    i = b * KC + c
                    s = i % 2
                    act.wait_ge(z_ready, i + 1)
                    if i >= 2:
                        act.wait_ge(dt_ready, i - 1)
                    own.step(nc.scalar.activation(z[:, s, :], pz[:, s, :], ACT.Identity, bias=dtb[:, c:c + 1]))
                    own.settle()
                    z_read_ins = nc.scalar.activation(mag[:, s, :], z[:, s, :], ACT.Abs)
                    z_read_ins.then_inc(z_read, 1)
                    act.wait_ge(z_read, i + 1)
                    own.step(nc.scalar.activation(e[:, s, :], mag[:, s, :], ACT.Exp, scale=-1.0))
                    own.settle()
                    nc.scalar.activation(ln[:, s, :], e[:, s, :], ACT.Ln, bias=1.0).then_inc(ln_ready, 1)

        @block.vector
        def _(dve):
            own = Chain(dve, dve_chain)
            dve.wait_ge(loaded, 80)
            own.step(nc.vector.tensor_scalar(g.D1[:], g.D1[:], 1.0, None, ALU.add))
            dve.wait_ge(act_chain, 1)
            own.step(nc.vector.tensor_scalar(g.A[:], g.A[:], -1.0, None, ALU.mult))
            for i in range(BATCH * KC):
                b, c, s = i // KC, i % KC, i % 2
                dve.wait_ge(ln_ready, i + 1)
                own.step(nc.vector.tensor_scalar(d[:, s, :], e[:, s, :], 1.0, -1.0, ALU.add, ALU.add))
                own.settle()
                own.step(nc.vector.scalar_tensor_tensor(out=d1[:, s, :], in0=d[:, s, :], scalar=0.0, in1=d[:, s, :],
                                                        op0=ALU.is_equal, op1=ALU.add))
                own.step(nc.vector.scalar_tensor_tensor(out=l1[:, s, :], in0=d[:, s, :], scalar=0.0, in1=ln[:, s, :],
                                                        op0=ALU.is_equal, op1=ALU.add))
                own.settle()
                own.step(nc.vector.reciprocal(q[:, s, :], d1[:, s, :]))
                own.settle()
                own.step(nc.vector.tensor_tensor(q2[:, s, :], q[:, s, :], l1[:, s, :], ALU.mult))
                own.settle()
                own.step(nc.vector.tensor_tensor(l1[:, s, :], q2[:, s, :], e[:, s, :], ALU.mult))
                own.settle()
                nc.vector.scalar_tensor_tensor(out=g.DT[:, c, b * NB:(b + 1) * NB], in0=z[:, s, :], scalar=0.0,
                                               in1=l1[:, s, :], op0=ALU.max, op1=ALU.add).then_inc(dt_ready, 1)

        @block.gpsimd
        def _(pool):
            nc.gpsimd.memset(zero[:], 0.0).then_inc(zeroed, 1)
            nc.gpsimd.memset(g.sel[:], 0.0).then_inc(u_ready, 1)
            nc.gpsimd.memset(g.ident[:], 0.0).then_inc(u_ready, 1)
            pool.wait_ge(u_ready, 2)
            nc.gpsimd.affine_select(out=g.sel[:], in_=g.sel[:], compare_op=ALU.not_equal, fill=1.0, base=0,
                                    pattern=[[-1, STATE], [0, P]], channel_multiplier=1).then_inc(u_ready, 1)
            nc.gpsimd.affine_select(out=g.ident[:], in_=g.ident[:], compare_op=ALU.not_equal, fill=1.0, base=0,
                                    pattern=[[-1, P]], channel_multiplier=1).then_inc(u_ready, 1)
            for i in range(BATCH * KC):
                b, c = i // KC, i % KC
                pool.wait_ge(dt_ready, i + 1)
                pool.wait_ge(x_in[b], 16)
                cols = slice(b * NB, (b + 1) * NB)
                nc.gpsimd.tensor_tensor(g.U[:, c, cols], g.DT[:, c, cols], g.XT[:, c, cols], ALU.mult).then_inc(u_ready, 1)


def ssm_scan(nc, a, g):
    with ExitStack() as ctx:
        sb, ps, sem = scoped(nc, ctx, "scan", reused=True)
        RING = 4
        STEPS = STATE * KC
        bbc = sb("bbc", [P, RING, NB])
        dbx = sb("dbx", [P, RING, NB])
        h = sb("h", [P, 2, NB])
        hc = sb("hc", [P, 2, NB])
        da = ps("da", [P, 2, NB])
        cbc = ps("cbc", [P, 2, NB])
        y = ps("y", [P, KC, NB])
        b_in = [sem(f"b_in{k}") for k in range(RING)]
        dbx_ready, dbx_0 = sem("dbx_ready"), STATE
        h_ready, h_0 = sem("h_ready"), RING
        hc_ready, hc_0 = sem("hc_ready"), 2 * KC
        y_used_hc, y_used_0 = sem("y_used_hc"), 2
        y_read = sem("y_read")
        da_ready, c_ready = sem("da_ready"), sem("c_ready")
        block = ctx.enter_context(nc.Block())

        @block.sync
        def _(sp):
            with sp.Fori(0, BATCH) as b:
                for n in range(STATE):
                    sp.wait_ge(dbx_ready, b * STEPS + KC * (n - RING + 1) + dbx_0)
                    sp.dma_start(bbc[:, n % RING, :], g.brow_dram[n, b].partition_broadcast(P)).then_inc(b_in[n % RING], 16)

        @block.gpsimd
        def _(pool):
            pool.sem_inc(dbx_ready, dbx_0)
            with pool.Fori(0, BATCH) as b:
                for n in range(STATE):
                    pool.wait_ge(b_in[n % RING], b * (16 * STATE // RING) + 16 * (n // RING + 1))
                    for c in range(KC):
                        i = n * KC + c
                        wait_apart(pool, h_ready, b * STEPS + i - RING + 1 + h_0)
                        nc.gpsimd.tensor_tensor(dbx[:, i % RING, :], g.U[:, c, bass.ts(b, NB)], bbc[:, n % RING, :],
                                                ALU.mult).then_inc(dbx_ready, 1)

        @block.scalar
        def _(act):
            with act.Fori(0, BATCH) as b:
                for n in range(STATE):
                    for c in range(KC):
                        i = n * KC + c
                        wait_apart(act, h_ready, b * STEPS + i - 1 + h_0)
                        nc.scalar.activation(da[:, i % 2, :], g.DT[:, c, bass.ts(b, NB)], ACT.Exp,
                                             scale=g.A[:, c, n:n + 1]).then_inc(da_ready, 1)

        @block.vector
        def _(dve):
            dve.sem_inc(h_ready, h_0)
            dve.sem_inc(hc_ready, hc_0)
            dve.sem_inc(y_read, KC)

            def weigh(b, i):
                dve.wait_ge(h_ready, b * STEPS + i + 1 + h_0)
                dve.wait_ge(c_ready, b * STATE + i // KC + 1)
                dve.wait_ge(y_used_hc, b * STEPS + i - 1 + y_used_0)
                nc.vector.tensor_tensor(hc[:, i % 2, :], cbc[:, (i // KC) % 2, :], h[:, i % 2, :],
                                        ALU.mult).then_inc(hc_ready, 1)

            with dve.Fori(0, BATCH) as b:
                for i in range(STEPS):
                    dve.wait_ge(da_ready, b * STEPS + i + 1)
                    dve.wait_ge(dbx_ready, b * STEPS + i + 1 + dbx_0)
                    dve.wait_ge(hc_ready, b * STEPS + i - 1 + hc_0)
                    nc.vector.tensor_tensor_scan(h[:, i % 2, :], da[:, i % 2, :], dbx[:, i % RING, :], 0.0,
                                                 ALU.mult, ALU.add).then_inc(h_ready, 1)
                    if i:
                        weigh(b, i - 1)
                weigh(b, STEPS - 1)
                for c in range(KC):
                    dve.wait_ge(y_used_hc, b * STEPS + STEPS - KC + c + 1 + y_used_0)
                    xs = g.XT[:, c, bass.ts(b, NB)]
                    nc.vector.scalar_tensor_tensor(out=xs, in0=xs, scalar=g.D1[:, c:c + 1], in1=y[:, c, :],
                                                   op0=ALU.mult, op1=ALU.add).then_inc(y_read, 1)

        @block.tensor
        def _(pe):
            pe.sem_inc(y_used_hc, y_used_0)
            with pe.Fori(0, BATCH) as b:
                for n in range(STATE + 1):
                    if n < STATE:
                        wait_apart(pe, hc_ready, b * STEPS + KC * (n - 1) + hc_0)
                        pe.matmul(cbc[:, n % 2, :], g.sel[:, n, :], g.CT[:, bass.ts(b, NB)], start=True,
                                  stop=True).then_inc(c_ready, 1)
                    if n == 0:
                        continue
                    for c in range(KC):
                        m = n - 1
                        i = m * KC + c
                        if m == 0:
                            pe.wait_ge(y_read, b * KC + c + 1)
                        pe.wait_ge(hc_ready, b * STEPS + i + 1 + hc_0)
                        mm = pe.matmul(y[:, c, :], g.ident[:], hc[:, i % 2, :], start=(m == 0), stop=(m == STATE - 1))
                        mm.then_inc(y_used_hc, 1)


def normalise(nc, g, tag, by_feature, out=None, quantise=False, gather=False):
    with ExitStack() as ctx:
        sb, ps, sem = scoped(nc, ctx, tag)
        stats = sb("stats", [P, TILES, 6])
        mv = sb("mv", [P, TILES, 2])
        std = sb("std", [P, TILES])
        rstd = sb("rstd", [P, TILES])
        eps = sb("eps", [P, 1])
        if quantise:
            amax, scale, inv = (sb(n, [P, TILES, KC]) for n in ("amax", "scale", "inv"))
            xq = sb("xq", [P, 2, DIM])
        pr = [ps(f"pr{k}", [P, DIM]) for k in range(2)] if by_feature else None
        pt = [ps(f"pt{k}", [P, KC, P]) for k in range(2)] if out is None else None
        x_ready, dve_chain = sem("x_ready"), sem("dve_chain")
        if by_feature:
            turned = sem("turned")
        if gather:
            GRING = 4
            rows = sb("rows", [P, GRING, TOP, DIM])
            gathered, added = [sem(f"gathered{k}") for k in range(GRING)], sem("added")
        if out is None:
            x_turned, hi_ready, lo_ready = sem("x_turned"), sem("hi_ready"), sem("lo_ready")
        else:
            stored = sem("stored")
        var_ready, std_ready, eps_ready = sem("var_ready"), sem("std_ready"), sem("eps_ready")
        if quantise:
            xq_ready, y_copied = sem("xq_ready"), sem("y_copied")
        block = ctx.enter_context(nc.Block())

        if gather:
            @block.gpsimd
            def _(pool):
                for t in range(TILES):
                    if t >= GRING:
                        pool.wait_ge(added, TOP * (t - GRING + 1))
                    for k in range(TOP):
                        nc.gpsimd.indirect_dma_start(rows[:, t % GRING, k, :], None, g.sorted_y,
                                                     bass.IndirectOffsetOnAxis(g.at[:, k, t:t + 1], 0)
                                                     ).then_inc(gathered[t % GRING], 16)

        @block.tensor
        def _(pe):
            for t in range(TILES + 1):
                if by_feature and t < TILES:
                    if t >= 2:
                        pe.wait_ge(x_ready, t - 1)
                    for c in range(KC):
                        mm = pe.transpose(pr[t % 2][:, c * P:(c + 1) * P], g.XT[:, c, t * P:(t + 1) * P], g.ident[:])
                    mm.then_inc(turned, 1)
                if t and out is None:
                    m = t - 1
                    pe.wait_ge(xq_ready if quantise else x_ready, m + 1)
                    if m >= 2:
                        pe.wait_ge(lo_ready, m - 1)
                    for c in range(KC):
                        cols = slice(c * P, (c + 1) * P)
                        mm = pe.transpose(pt[m % 2][:, c, :], xq[:, m % 2, cols] if quantise else g.X[:, m, cols],
                                          g.ident[:])
                    mm.then_inc(x_turned, 1)

        @block.vector
        def _(dve):
            own = Chain(dve, dve_chain)
            nc.vector.memset(eps[:], EPS).then_inc(eps_ready, 1)

            def low_part(m):
                dve.wait_ge(hi_ready, m + 1)
                cols = slice(m * P, (m + 1) * P)
                nc.vector.tensor_tensor(g.XL[:, :, cols], pt[m % 2][:], g.XH[:, :, cols].bitcast(F32),
                                        ALU.subtract).then_inc(lo_ready, 1)

            def quantised(m):
                dve.wait_ge(x_ready, m + 1)
                own.step(nc.vector.tensor_reduce(amax[:, m, :], g.X[:, m, :].rearrange("p (c k) -> p c k", k=P), AX.X,
                                                 ALU.max, apply_absolute_value=True))
                own.settle()
                own.step(nc.vector.tensor_scalar(scale[:, m, :], amax[:, m, :], 1.0 / FP8_MAX, 1e-12, ALU.mult, ALU.add))
                own.settle()
                own.step(nc.vector.reciprocal(inv[:, m, :], scale[:, m, :]))
                own.settle()
                if m >= 2:
                    dve.wait_ge(x_turned, m - 1)
                for c in range(KC):
                    cols = slice(c * P, (c + 1) * P)
                    ins = nc.vector.tensor_scalar(xq[:, m % 2, cols], g.X[:, m, cols], inv[:, m, c:c + 1],
                                                  scale[:, m, c:c + 1], ALU.mult, ALU.mult)
                    if c < KC - 1:
                        own.step(ins)
                ins.then_inc(xq_ready, 1)

            def source(t):
                return pr[t % 2][:] if by_feature else g.Y[:, t, :]

            for t in range(TILES + 2):
                if t < TILES:
                    if by_feature:
                        dve.wait_ge(turned, t + 1)
                    if gather:
                        dve.wait_ge(gathered[t % GRING], 16 * TOP * (t // GRING + 1))
                        for k in range(TOP):
                            nc.vector.scalar_tensor_tensor(out=g.Y[:, t, :], in0=rows[:, t % GRING, k, :],
                                                           scalar=g.weight[:, k, t:t + 1], in1=g.Y[:, t, :],
                                                           op0=ALU.mult, op1=ALU.add).then_inc(added, 1)
                            dve.wait_ge(added, TOP * t + k + 1)
                    own.step(nc.vector.bn_stats(stats[:, t, :], source(t)))
                    own.settle()
                    nc.vector.bn_aggr(mv[:, t, :], stats[:, t, :]).then_inc(var_ready, 1)
                if 1 <= t <= TILES:
                    m = t - 1
                    dve.wait_ge(std_ready, m + 1)
                    own.step(nc.vector.reciprocal(rstd[:, m:m + 1], std[:, m:m + 1]))
                    own.settle()
                    nc.vector.tensor_scalar(g.X[:, m, :], source(m), mv[:, m, 0:1], rstd[:, m:m + 1], ALU.subtract,
                                            ALU.mult).then_inc(x_ready, 1)
                    if quantise:
                        quantised(m)
                if t >= 2 and out is None:
                    low_part(t - 2)

        @block.scalar
        def _(act):
            act.wait_ge(eps_ready, 1)
            for t in range(TILES + 2):
                if t < TILES:
                    act.wait_ge(var_ready, t + 1)
                    nc.scalar.activation(std[:, t:t + 1], mv[:, t, 1:2], ACT.Sqrt, bias=eps[:, 0:1]).then_inc(std_ready, 1)
                if quantise and 1 <= t <= TILES:
                    act.wait_ge(x_ready, t)
                    nc.scalar.activation(g.Y[:, t - 1, :], g.X[:, t - 1, :], ACT.Copy).then_inc(y_copied, 1)
                if t >= 2 and out is None:
                    m = t - 2
                    act.wait_ge(x_turned, m + 1)
                    nc.scalar.activation(g.XH[:, :, m * P:(m + 1) * P], pt[m % 2][:], ACT.Copy).then_inc(hi_ready, 1)

        @block.sync
        def _(sp):
            if out is not None:
                rows = out.rearrange("(t p) d -> p t d", p=P)
                for t in range(0, TILES, 2):
                    sp.wait_ge(x_ready, t + 2)
                    sp.dma_start(rows[:, t:t + 2, :], g.X[:, t:t + 2, :]).then_inc(stored, 16)
                sp.wait_ge(stored, 16 * TILES // 2)


def route(nc, a, g):
    with ExitStack() as ctx:
        sb, ps, sem = scoped(nc, ctx, "route")
        rw = sb("rw", [P, KC, EXPERTS])
        rh = sb("rh", [P, KC, EXPERTS], F32R)
        rl = sb("rl", [P, KC, EXPERTS], F32R)
        rb = sb("rb", [P, EXPERTS])
        rbias = sb("rbias", [P, EXPERTS])
        order = sb("order", [P, EXPERTS])
        b3 = sb("b3", [MLPS, DIM])
        full = [P, TILES, EXPERTS]
        grouped = [P, TILES, GROUPS]
        lg, lg2, ex, pr_, sc = (sb(n, full) for n in ("lg", "lg2", "ex", "pr", "sc"))
        ms, ms2, ms3, eq, key, e1, e2, esum = (sb(n, full) for n in ("ms", "ms2", "ms3", "eq", "key", "e1", "e2", "es"))
        gm, gm2, geq, gkey, g1, g2, keep, low = (sb(n, grouped) for n in
                                                 ("gm", "gm2", "geq", "gkey", "g1", "g2", "keep", "low"))
        one, two, three_ = (sb(n, [P, TILES]) for n in ("one", "two", "three"))
        gT = sb("gT", [MLPS, TOK])
        upper, ones = sb("upper", [P, P]), sb("ones", [P, P])
        steps, before, tile_no = sb("steps", [P, TILES]), sb("before", [P, EXPERTS, EXPERTS]), sb("tile_no", [P, SORTED])
        count, held, start, end = (sb(n, [P, EXPERTS]) for n in ("count", "held", "start", "end"))
        over, early = sb("over", [P, EXPERTS, TILES]), sb("early", [P, EXPERTS, EXPERTS])
        past, owner = sb("past", [1, SORTED, EXPERTS]), sb("owner", [1, SORTED])
        place, chosen = sb("place", full), sb("chosen", full)
        at = sb("at", [P, TOP, TILES])
        pl = ps("pl", full)
        pg = [ps(f"pg{k}", [P, NB]) for k in range(2)]
        py = [ps(f"py{k}", [P, DIM]) for k in range(2)]
        rank, total = ps("rank", full), ps("total", [P, EXPERTS])
        consts, picked, ranked = sem("consts"), sem("picked"), sem("ranked")
        loaded, logits, exped, gated = sem("loaded"), sem("logits"), sem("exped"), sem("gated")
        turned, copied, y_ready, y_added = sem("turned"), sem("copied"), sem("y_ready"), sem("y_added")
        dve_chain, split = sem("dve_chain"), sem("split")
        block = ctx.enter_context(nc.Block())

        @block.sync
        def _(sp):
            sp.dma_start(rw[:], a["router_w"].rearrange("(c p) e -> p c e", p=P)).then_inc(loaded, 16)
            sp.dma_start(rb[:], a["router_b"].partition_broadcast(P)).then_inc(loaded, 16)
            sp.dma_start(rbias[:], a["router_bias"].partition_broadcast(P)).then_inc(loaded, 16)
            sp.dma_start(order[:], a["order"].partition_broadcast(P)).then_inc(loaded, 16)
            sp.dma_start(b3[:], a["b3"]).then_inc(loaded, 16)
            sp.dma_start(steps[:], a["steps"].partition_broadcast(P)).then_inc(loaded, 16)
            sp.dma_start(before[:], a["before"].partition_broadcast(P)).then_inc(loaded, 16)
            sp.dma_start(tile_no[:], a["tile_no"].partition_broadcast(P)).then_inc(loaded, 16)
            for s in range(2):
                sp.dma_start(g.raw[s][:], a["w123"][EXPERTS + s]).then_inc(g.shared_in[s], 16)

        @block.gpsimd
        def _(pool):
            nc.gpsimd.memset(ones[:], 1.0).then_inc(consts, 1)
            pool.wait_ge(consts, 1)
            nc.gpsimd.affine_select(out=upper[:], in_=ones[:], compare_op=ALU.is_gt, fill=0.0, base=0,
                                    pattern=[[1, P]], channel_multiplier=-1).then_inc(consts, 1)
            for s in range(2):
                pool.wait_ge(g.shared_in[s], 16)
                nc.gpsimd.tensor_scalar(g.wh[s][:], g.raw[s][:, 0:WN], 1.0, 0.0, ALU.mult, ALU.add).then_inc(consts, 1)
                pool.wait_ge(consts, 3 + s)
                nc.gpsimd.tensor_tensor(g.wl[s][:], g.raw[s][:, 0:WN], g.wh[s][:].bitcast(F32),
                                        ALU.subtract).then_inc(g.shared_split, 1)

        @block.tensor
        def _(pe):
            pe.wait_ge(split, 2)
            for t in range(TILES):
                cols = slice(t * P, (t + 1) * P)
                for c in range(KC):
                    for x in (g.XH, g.XL):
                        for w in (rh, rl):
                            first = c == 0 and x is g.XH and w is rh
                            last = c == KC - 1 and x is g.XL and w is rl
                            mm = pe.matmul(pl[:, t, :], x[:, c, cols], w[:, c, :], start=first, stop=last)
            mm.then_inc(logits, 1)
            pe.wait_ge(consts, 2)
            pe.wait_ge(picked, 1)
            pe.matmul(rank[:], upper[:], esum[:], start=True, stop=False)
            for t in range(TILES):
                if t < TILES - 1:
                    pe.matmul(rank[:, t + 1:, :], ones[:],
                              esum[:, t, :].unsqueeze(1).to_broadcast([P, TILES - 1 - t, EXPERTS]), start=False,
                              stop=(t == TILES - 2))
                mm = pe.matmul(total[:], ones[:], esum[:, t, :], start=(t == 0), stop=(t == TILES - 1))
            mm.then_inc(ranked, 1)
            pe.wait_ge(gated, 1)
            for b in range(BLOCKS):
                if b >= 2:
                    pe.wait_ge(copied, b - 1)
                for j in range(PER_BLOCK):
                    t = b * PER_BLOCK + j
                    mm = pe.transpose(pg[b % 2][0:MLPS, j * P:(j + 1) * P], g.gate[:, :, t], g.ident[:])
                mm.then_inc(turned, 1)
            for t in range(TILES):
                pe.wait_ge(copied, t // PER_BLOCK + 1)
                if t >= 2:
                    pe.wait_ge(y_added, t - 1)
                pe.matmul(py[t % 2][:], gT[:, t * P:(t + 1) * P], b3[:], start=True, stop=True).then_inc(y_ready, 1)

        @block.scalar
        def _(act):
            act.wait_ge(dve_chain, 1 + 3)
            nc.scalar.activation(ex[:], lg2[:], ACT.Exp).then_inc(exped, 1)
            for b in range(BLOCKS):
                act.wait_ge(turned, b + 1)
                nc.scalar.activation(gT[:, b * NB:(b + 1) * NB], pg[b % 2][0:MLPS, :], ACT.Copy).then_inc(copied, 1)

        @block.vector
        def _(dve):
            own = Chain(dve, dve_chain)

            def along(x, n):
                return x.unsqueeze(2).to_broadcast([P, TILES, n])

            def do(ins):
                own.step(ins)
                own.settle()

            def pick(sel, v, n, eq_, key_):
                do(nc.vector.tensor_reduce(one[:], v, AX.X, ALU.max))
                do(nc.vector.tensor_tensor(eq_, v, along(one[:], n), ALU.is_equal))
                do(nc.vector.tensor_tensor(key_, eq_, order[:, 0:n].unsqueeze(1).to_broadcast([P, TILES, n]), ALU.mult))
                do(nc.vector.tensor_reduce(two[:], key_, AX.X, ALU.max))
                do(nc.vector.tensor_tensor(sel, key_, along(two[:], n), ALU.is_equal))

            def by_group(x):
                return x[:].rearrange("p t (g k) -> p (t g) k", g=GROUPS)

            def per_group(x):
                return x[:].rearrange("p t g -> p (t g)").unsqueeze(2).to_broadcast([P, TILES * GROUPS, EXPERTS // GROUPS])

            dve.wait_ge(loaded, 128)
            own.step(nc.vector.memset(g.gate[:, EXPERTS:MLPS, :], 1.0))
            nc.vector.tensor_copy(rh[:], rw[:]).then_inc(split, 1)
            dve.wait_ge(split, 1)
            nc.vector.tensor_tensor(rl[:], rw[:], rh[:].bitcast(F32), ALU.subtract).then_inc(split, 1)
            dve.wait_ge(logits, 1)
            do(nc.vector.tensor_tensor(lg[:], pl[:], rb[:].unsqueeze(1).to_broadcast(full), ALU.add))
            do(nc.vector.tensor_reduce(three_[:], lg[:], AX.X, ALU.max))
            do(nc.vector.tensor_tensor(lg2[:], lg[:], along(three_[:], EXPERTS), ALU.subtract))
            dve.wait_ge(exped, 1)
            do(nc.vector.tensor_reduce(one[:], ex[:], AX.X, ALU.add))
            do(nc.vector.reciprocal(two[:], one[:]))
            do(nc.vector.tensor_tensor(pr_[:], ex[:], along(two[:], EXPERTS), ALU.mult))
            do(nc.vector.tensor_tensor(sc[:], pr_[:], rbias[:].unsqueeze(1).to_broadcast(full), ALU.add))
            do(nc.vector.tensor_reduce(gm[:].rearrange("p t g -> p (t g)"), by_group(sc), AX.X, ALU.max))
            pick(g1[:], gm[:], GROUPS, geq[:], gkey[:])
            do(nc.vector.scalar_tensor_tensor(out=gm2[:], in0=g1[:], scalar=-BIG, in1=gm[:], op0=ALU.mult, op1=ALU.add))
            pick(g2[:], gm2[:], GROUPS, geq[:], gkey[:])
            do(nc.vector.tensor_tensor(keep[:], g1[:], g2[:], ALU.add))
            do(nc.vector.tensor_scalar(low[:], keep[:], -1.0, BIG, ALU.add, ALU.mult))
            do(nc.vector.tensor_tensor(by_group(ms), by_group(sc), per_group(keep), ALU.mult))
            do(nc.vector.tensor_tensor(by_group(ms2), by_group(ms), per_group(low), ALU.add))
            pick(e1[:], ms2[:], EXPERTS, eq[:], key[:])
            do(nc.vector.scalar_tensor_tensor(out=ms3[:], in0=e1[:], scalar=-BIG / 2, in1=ms2[:], op0=ALU.mult,
                                              op1=ALU.add))
            do(nc.vector.tensor_scalar(ms3[:], ms3[:], -BIG, None, ALU.max))
            pick(e2[:], ms3[:], EXPERTS, eq[:], key[:])
            nc.vector.tensor_tensor(esum[:], e1[:], e2[:], ALU.add).then_inc(picked, 1)
            dve.wait_ge(picked, 1)
            nc.vector.tensor_tensor(g.gate[:, 0:EXPERTS, :].rearrange("p e t -> p t e"), esum[:], sc[:],
                                    ALU.mult).then_inc(gated, 1)
            for k, e in enumerate((e1, e2)):
                do(nc.vector.tensor_tensor(chosen[:], e[:], sc[:], ALU.mult))
                do(nc.vector.tensor_reduce(g.weight[:, k, :], chosen[:], AX.X, ALU.add))
            dve.wait_ge(ranked, 1)
            do(nc.vector.tensor_copy(count[:], total[:]))
            do(nc.vector.tensor_tensor(over[:], count[:].unsqueeze(2).to_broadcast([P, EXPERTS, TILES]),
                                       steps[:].unsqueeze(1).to_broadcast([P, EXPERTS, TILES]), ALU.is_gt))
            do(nc.vector.tensor_reduce(held[:], over[:], AX.X, ALU.add))
            do(nc.vector.tensor_tensor(early[:], before[:], held[:].unsqueeze(1).to_broadcast([P, EXPERTS, EXPERTS]),
                                       ALU.mult))
            do(nc.vector.tensor_reduce(start[:], early[:], AX.X, ALU.add))
            do(nc.vector.tensor_tensor(end[:], start[:], held[:], ALU.add))
            do(nc.vector.tensor_scalar(start[:], start[:], float(P), None, ALU.mult))
            do(nc.vector.tensor_tensor(place[:], rank[:], start[:].unsqueeze(1).to_broadcast(full), ALU.add))
            for k, e in enumerate((e1, e2)):
                do(nc.vector.tensor_tensor(chosen[:], e[:], place[:], ALU.mult))
                do(nc.vector.tensor_reduce(at[:, k, :], chosen[:], AX.X, ALU.add))
            do(nc.vector.tensor_copy(g.at[:], at[:]))
            do(nc.vector.tensor_tensor(past[:], end[0:1].unsqueeze(1).to_broadcast([1, SORTED, EXPERTS]),
                                       tile_no[0:1].unsqueeze(2).to_broadcast([1, SORTED, EXPERTS]), ALU.is_le))
            do(nc.vector.tensor_reduce(owner[:], past[:], AX.X, ALU.add))
            do(nc.vector.tensor_scalar(g.owner[:], owner[:], EXPERTS - 1.0, None, ALU.min))
            for t in range(TILES):
                dve.wait_ge(y_ready, t + 1)
                nc.vector.tensor_tensor(g.Y[:, t, :], py[t % 2][:], g.X[:, t, :], ALU.add).then_inc(y_added, 1)


def shared_mlp(nc, a, g):
    with ExitStack() as ctx:
        sb, ps, sem = scoped(nc, ctx, "moe")
        silu = sb("silu", [P, 2, NB])
        h = sb("h", [P, 2, NB])
        hh = sb("hh", [P, 2, NB], F32R)
        hl = sb("hl", [P, 2, NB], F32R)
        pg = [ps(f"pg{k}", [P, NB]) for k in range(2)]
        pu = [ps(f"pu{k}", [P, NB]) for k in range(2)]
        py = [ps(f"py{k}", [P, DIM]) for k in range(PER_BLOCK)]
        scattered = sem("scattered")
        g_ready, u_ready, s_ready, hh_ready = sem("g_ready"), sem("u_ready"), sem("s_ready"), sem("hh_ready")
        h_ready, hl_ready, y_ready, y_added = sem("h_ready"), sem("hl_ready"), sem("y_ready"), sem("y_added")
        STEPS = 2 * BLOCKS
        block = ctx.enter_context(nc.Block())

        @block.gpsimd
        def _(pool):
            for t in range(TILES):
                for k in range(TOP):
                    nc.gpsimd.indirect_dma_start(g.sorted_x, bass.IndirectOffsetOnAxis(g.at[:, k, t:t + 1], 0),
                                                 g.X[:, t, :], None).then_inc(scattered, 16)
            pool.wait_ge(scattered, 16 * TOP * TILES)

        @block.tensor
        def _(pe):
            def up(q):
                e, tb = q // BLOCKS, q % BLOCKS
                cols = slice(tb * NB, (tb + 1) * NB)
                pe.wait_ge(g.shared_split, e + 1)
                if q >= 2:
                    pe.wait_ge(h_ready, q - 1)
                for out, at, ready in ((pg, 0, g_ready), (pu, KC * INTER, u_ready)):
                    for c in range(KC):
                        w = slice(at + c * INTER, at + (c + 1) * INTER)
                        mm = three(pe, out[q % 2][:], g.wh[e][:, w], g.wl[e][:, w], g.XH[:, c, cols],
                                   g.XL[:, c, cols], c == 0, c == KC - 1)
                    mm.then_inc(ready, 1)

            def down(q):
                e = q // BLOCKS
                pe.wait_ge(hl_ready, q + 1)
                for j in range(PER_BLOCK):
                    cols = slice(j * P, (j + 1) * P)
                    if q:
                        pe.wait_ge(y_added, PER_BLOCK * (q - 1) + j + 1)
                    three(pe, py[j][:], hh[:, q % 2, cols], hl[:, q % 2, cols], g.wh[e][:, WUP:], g.wl[e][:, WUP:],
                          True, True).then_inc(y_ready, 1)

            for q in range(STEPS):
                up(q)
                if q:
                    down(q - 1)
            down(STEPS - 1)

        @block.scalar
        def _(act):
            for q in range(STEPS):
                act.wait_ge(g_ready, q + 1)
                if q >= 2:
                    act.wait_ge(h_ready, q - 1)
                nc.scalar.activation(silu[:, q % 2, :], pg[q % 2][:], ACT.Silu,
                                     bias=g.raw[q // BLOCKS][:, WN:WN + 1]).then_inc(s_ready, 1)
                act.wait_ge(h_ready, q + 1)
                if q >= 2:
                    act.wait_ge(y_ready, PER_BLOCK * (q - 1))
                nc.scalar.activation(hh[:, q % 2, :], h[:, q % 2, :], ACT.Copy).then_inc(hh_ready, 1)

        @block.vector
        def _(dve):
            def hidden(q):
                dve.wait_ge(u_ready, q + 1)
                dve.wait_ge(s_ready, q + 1)
                if q >= 2:
                    dve.wait_ge(hl_ready, q - 1)
                nc.vector.scalar_tensor_tensor(out=h[:, q % 2, :], in0=pu[q % 2][:], scalar=g.raw[q // BLOCKS][:, WN + 1:WN + 2],
                                               in1=silu[:, q % 2, :], op0=ALU.add, op1=ALU.mult).then_inc(h_ready, 1)
                dve.wait_ge(hh_ready, q + 1)
                nc.vector.tensor_tensor(hl[:, q % 2, :], h[:, q % 2, :], hh[:, q % 2, :].bitcast(F32),
                                        ALU.subtract).then_inc(hl_ready, 1)

            def add(q):
                for j in range(PER_BLOCK):
                    t = PER_BLOCK * (q % BLOCKS) + j
                    dve.wait_ge(y_ready, PER_BLOCK * q + j + 1)
                    if q >= BLOCKS:
                        dve.wait_ge(y_added, PER_BLOCK * (q - BLOCKS) + j + 1)
                    nc.vector.tensor_tensor(g.Y[:, t, :], py[j][:], g.Y[:, t, :], ALU.add).then_inc(y_added, 1)

            for q in range(STEPS):
                hidden(q)
                if q:
                    add(q - 1)
            add(STEPS - 1)


def sorted_experts(nc, a, g):
    with ExitStack() as ctx:
        sb, ps, sem = scoped(nc, ctx, "exp")
        raw = g.raw + [sb(f"raw{k}", [P, WN + 2]) for k in range(2, TURN)]
        x = [sb(f"x{k}", [P, DIM]) for k in range(TURN)]
        xh = [sb(f"xh{k}", [P, KC, P], F32R) for k in range(2)]
        xl = [sb(f"xl{k}", [P, KC, P], F32R) for k in range(2)]
        silu, h = ([sb(f"{n}{k}", [P, P]) for k in range(2)] for n in ("silu", "h"))
        hh, hl = ([sb(f"{n}{k}", [P, P], F32R) for k in range(2)] for n in ("hh", "hl"))
        y = [sb(f"y{k}", [P, DIM]) for k in range(2)]
        pt = [ps(f"pt{k}", [P, KC, P]) for k in range(2)]
        pgu = [[ps(f"p{n}{k}", [P, NB]) for n in "gu"] for k in range(2)]
        py = [ps(f"py{k}", [P, DIM]) for k in range(2)]
        x_in, w_in = [sem(f"x_in{k}") for k in range(TURN)], [sem(f"w_in{k}") for k in range(TURN)]
        up_hi, down_hi, xh_ready, g_ready = sem("up_hi"), sem("down_hi"), sem("xh_ready"), sem("g_ready")
        s_ready, hh_ready, hl_ready = sem("s_ready"), sem("hh_ready"), sem("hl_ready")
        y_stored = [sem(f"y_stored{k}") for k in range(2)]
        x_turned, xl_ready, u_ready, h_ready = sem("x_turned"), sem("xl_ready"), sem("u_ready"), sem("h_ready")
        up_lo, down_lo, y_ready, y_copied = sem("up_lo"), sem("down_lo"), sem("y_ready"), sem("y_copied")
        AHEAD = TURN
        block = ctx.enter_context(nc.Block())

        def steps(eng, stages):
            for n in range(TURN):
                for lag, do in stages:
                    if n >= lag:
                        do(n - lag, n - lag)
            with eng.Fori(1, SORTED // TURN) as i:
                for n in range(TURN):
                    for lag, do in stages:
                        do(i * TURN + (n - lag), (n - lag) % TURN)
            for n in range(max(lag for lag, _ in stages)):
                for lag, do in stages:
                    if n < lag:
                        do(SORTED + n - lag, (n - lag) % TURN)

        @block.sync
        def _(sp):
            def load_x(j, s):
                sp.wait_ge(x_turned, j - TURN + 1 + AHEAD)
                sp.dma_start(x[s][:].unsqueeze(1), g.sorted_x.rearrange("(t p) d -> p t d", p=P)[:, bass.ds(j, 1), :]
                             ).then_inc(x_in[s], 16)

            def load_w(j, s):
                sp.wait_ge(up_lo, j - TURN + 1 + AHEAD)
                sp.wait_ge(down_lo, j - TURN + 1 + AHEAD)
                sp.wait_ge(h_ready, j - TURN + 1 + AHEAD)
                e = nc.values_load(g.owner[0:1, bass.ds(j, 1)], engines=(mybir.EngineType.SP,), min_val=0,
                                   max_val=EXPERTS - 1)
                sp.dma_start(raw[s][:].unsqueeze(1), a["w123"][bass.ds(e, 1)].rearrange("e p w -> p e w")
                             ).then_inc(w_in[s], 16)

            def store_y(j, s):
                sp.wait_ge(y_copied, j + 1 + AHEAD)
                sp.dma_start(g.sorted_y.rearrange("(t p) d -> p t d", p=P)[:, bass.ds(j, 1), :], y[s % 2][:].unsqueeze(1)
                             ).then_inc(y_stored[s % 2], 16)

            for k in range(2):
                sp.sem_inc(y_stored[k], 16)
            steps(sp, [(0, load_x), (0, load_w), (TURN, store_y)])
            for k in range(2):
                sp.wait_ge(y_stored[k], 16 * SORTED // 2 + 16)

        @block.gpsimd
        def _(pool):
            pool.sem_inc(down_lo, AHEAD)

            def up_weights_hi(j, s):
                pool.wait_ge(w_in[s], (j - s) * (16 // TURN) + 16)
                wait_apart(pool, u_ready, j - 1 + AHEAD)
                nc.gpsimd.tensor_scalar(g.wh[s % 2][:, 0:WUP], raw[s][:, 0:WUP], 1.0, 0.0, ALU.mult,
                                        ALU.add).then_inc(up_hi, 1)

            def down_weights_lo(j, s):
                pool.wait_ge(down_hi, j + 1)
                wait_apart(pool, y_ready, j - 1 + AHEAD)
                nc.gpsimd.tensor_tensor(g.wl[s % 2][:, WUP:WN], raw[s][:, WUP:WN], g.wh[s % 2][:, WUP:WN].bitcast(F32),
                                        ALU.subtract).then_inc(down_lo, 1)

            steps(pool, [(0, up_weights_hi), (1, down_weights_lo)])

        @block.tensor
        def _(pe):
            pe.sem_inc(x_turned, AHEAD)
            pe.sem_inc(u_ready, AHEAD)
            pe.sem_inc(y_ready, AHEAD)

            def turn(j, s):
                pe.wait_ge(x_in[s], (j - s) * (16 // TURN) + 16)
                pe.wait_ge(xl_ready, j - 1 + AHEAD)
                for c in range(KC):
                    mm = pe.transpose(pt[s % 2][:, c, :], x[s][:, c * P:(c + 1) * P], g.ident[:])
                mm.then_inc(x_turned, 1)

            def up(j, s):
                k = s % 2
                pe.wait_ge(xl_ready, j + 1 + AHEAD)
                pe.wait_ge(up_lo, j + 1 + AHEAD)
                pe.wait_ge(h_ready, j - 1 + AHEAD)
                for n, ready in ((0, g_ready), (1, u_ready)):
                    for c in range(KC):
                        w = slice((n * KC + c) * INTER, (n * KC + c + 1) * INTER)
                        mm = three(pe, pgu[k][n][:, 0:P], g.wh[k][:, w], g.wl[k][:, w], xh[k][:, c, :], xl[k][:, c, :],
                                   c == 0, c == KC - 1)
                    mm.then_inc(ready, 1)

            def down(j, s):
                k = s % 2
                pe.wait_ge(hl_ready, j + 1)
                pe.wait_ge(down_lo, j + 1 + AHEAD)
                pe.wait_ge(y_copied, j - 1 + AHEAD)
                three(pe, py[k][:], hh[k][:], hl[k][:], g.wh[k][:, WUP:WN], g.wl[k][:, WUP:WN], True,
                      True).then_inc(y_ready, 1)

            steps(pe, [(0, turn), (1, up), (2, down)])

        @block.scalar
        def _(act):
            act.sem_inc(y_copied, AHEAD)

            def y_copy(j, s):
                act.wait_ge(y_ready, j + 1 + AHEAD)
                wait_apart(act, y_stored[s % 2], (j - s % 2) * 8 + 16)
                nc.scalar.activation(y[s % 2][:], py[s % 2][:], ACT.Copy).then_inc(y_copied, 1)

            def x_hi(j, s):
                act.wait_ge(x_turned, j + 1 + AHEAD)
                act.wait_ge(u_ready, j - 1 + AHEAD)
                nc.scalar.activation(xh[s % 2][:], pt[s % 2][:], ACT.Copy).then_inc(xh_ready, 1)

            def down_weights_hi(j, s):
                act.wait_ge(w_in[s], (j - s) * (16 // TURN) + 16)
                act.wait_ge(y_ready, j - 1 + AHEAD)
                nc.scalar.activation(g.wh[s % 2][:, WUP:WN], raw[s][:, WUP:WN], ACT.Copy).then_inc(down_hi, 1)

            def gate(j, s):
                act.wait_ge(g_ready, j + 1)
                act.wait_ge(h_ready, j - 1 + AHEAD)
                nc.scalar.activation(silu[s % 2][:], pgu[s % 2][0][:, 0:P], ACT.Silu,
                                     bias=raw[s][:, WN:WN + 1]).then_inc(s_ready, 1)

            def h_hi(j, s):
                act.wait_ge(h_ready, j + 1 + AHEAD)
                act.wait_ge(y_ready, j - 1 + AHEAD)
                nc.scalar.activation(hh[s % 2][:], h[s % 2][:], ACT.Copy).then_inc(hh_ready, 1)

            steps(act, [(3, y_copy), (0, x_hi), (1, down_weights_hi), (1, gate), (1, h_hi)])

        @block.vector
        def _(dve):
            dve.sem_inc(xl_ready, AHEAD)
            dve.sem_inc(up_lo, AHEAD)
            dve.sem_inc(h_ready, AHEAD)

            def x_lo(j, s):
                dve.wait_ge(xh_ready, j + 1)
                nc.vector.tensor_tensor(xl[s % 2][:], pt[s % 2][:], xh[s % 2][:].bitcast(F32),
                                        ALU.subtract).then_inc(xl_ready, 1)

            def up_weights_lo(j, s):
                dve.wait_ge(up_hi, j + 1)
                nc.vector.tensor_tensor(g.wl[s % 2][:, 0:WUP], raw[s][:, 0:WUP], g.wh[s % 2][:, 0:WUP].bitcast(F32),
                                        ALU.subtract).then_inc(up_lo, 1)

            def hidden(j, s):
                dve.wait_ge(u_ready, j + 1 + AHEAD)
                dve.wait_ge(s_ready, j + 1)
                nc.vector.scalar_tensor_tensor(out=h[s % 2][:], in0=pgu[s % 2][1][:, 0:P], scalar=raw[s][:, WN + 1:WN + 2],
                                               in1=silu[s % 2][:], op0=ALU.add, op1=ALU.mult).then_inc(h_ready, 1)

            def h_lo(j, s):
                dve.wait_ge(hh_ready, j + 1)
                nc.vector.tensor_tensor(hl[s % 2][:], h[s % 2][:], hh[s % 2][:].bitcast(F32),
                                        ALU.subtract).then_inc(hl_ready, 1)

            steps(dve, [(0, x_lo), (0, up_weights_lo), (1, hidden), (1, h_lo)])


def project(nc, a, g):
    with ExitStack() as ctx:
        sb, ps, sem = scoped(nc, ctx, "proj")
        raw = [g.sums[:, k * KC * DIM:(k + 1) * KC * DIM] for k in range(3)]
        wh = [sb(f"wh{k}", [P, KC * DIM], F32R) for k in range(3)]
        wl = [sb(f"wl{k}", [P, KC * DIM], F32R) for k in range(3)]
        hi = sb("hi", [P, 2, NB], F32R)
        lo = sb("lo", [P, 2, NB], F32R)
        v = sb("v", [P, 2, HEADS, VPAD])
        po = [ps(f"po{k}", [P, NB]) for k in range(4)]
        w_in = [sem(f"w_in{k}") for k in range(3)]
        w_hi, w_split, pads, product = sem("w_hi"), sem("w_split"), sem("pads"), sem("product")
        w_first, hi_ready, lo_ready, v_ready = sem("w_first"), sem("hi_ready"), sem("lo_ready"), sem("v_ready")
        stored, v_stored = [sem("stored0"), sem("stored1")], [sem("v_stored0"), sem("v_stored1")]
        QK = 2 * KC * BLOCKS
        block = ctx.enter_context(nc.Block())

        @block.sync
        def _(sp):
            for k in range(3):
                sp.dma_start(raw[k].rearrange("p (c e) -> p c e", c=KC),
                             a["wqkvT"][k].rearrange("(c p) e -> p c e", p=P)).then_inc(w_in[k], 16)
            for q in range(QK):
                which, unit = q // (KC * BLOCKS), (q % BLOCKS) * KC + (q // BLOCKS) % KC
                sp.wait_ge(hi_ready, q + 1)
                sp.dma_start(g.qk_dram[which, 0, unit], hi[:, q % 2, :].bitcast(F32)).then_inc(stored[q % 2], 16)
                sp.wait_ge(lo_ready, q + 1)
                sp.dma_start(g.qk_dram[which, 1, unit], lo[:, q % 2, :].bitcast(F32)).then_inc(stored[q % 2], 16)
            for t in range(TILES):
                sp.wait_ge(v_ready, t + 1)
                sp.dma_start(g.v_dram[t], v[:, t % 2].rearrange("p h d -> p (h d)")).then_inc(v_stored[t % 2], 16)
            for k in range(2):
                sp.wait_ge(stored[k], 16 * QK)
                sp.wait_ge(v_stored[k], 16 * TILES // 2)

        @block.gpsimd
        def _(pool):
            nc.gpsimd.memset(v[:], 0.0).then_inc(pads, 1)
            pool.wait_ge(pads, 1)
            nc.gpsimd.memset(v[:, :, :, DK:DK + 1], 1.0).then_inc(pads, 1)
            for k in (1, 2):
                pool.wait_ge(w_in[k], 16)
                nc.gpsimd.tensor_scalar(wh[k][:], raw[k], 1.0, 0.0, ALU.mult, ALU.add).then_inc(w_hi, 1)
                pool.wait_ge(w_hi, k)
                nc.gpsimd.tensor_tensor(wl[k][:], raw[k], wh[k][:].bitcast(F32), ALU.subtract).then_inc(w_split, 1)

        @block.tensor
        def _(pe):
            def bank_free(n):
                if n >= QK + 4:
                    pe.wait_ge(v_ready, n - QK - 3)
                elif n >= 4:
                    pe.wait_ge(lo_ready, n - 3)

            for q in range(QK):
                which, c_out, b = q // (KC * BLOCKS), (q // BLOCKS) % KC, q % BLOCKS
                if q == 0:
                    pe.wait_ge(w_first, 2)
                if q == QK // 2:
                    pe.wait_ge(w_split, 1)
                bank_free(q)
                for c in range(KC):
                    w = slice(c * DIM + c_out * P, c * DIM + (c_out + 1) * P)
                    mm = three(pe, po[q % 4][:], wh[which][:, w], wl[which][:, w], g.XH[:, c, b * NB:(b + 1) * NB],
                               g.XL[:, c, b * NB:(b + 1) * NB], c == 0, c == KC - 1)
                mm.then_inc(product, 1)
            pe.wait_ge(w_split, 2)
            for t in range(TILES):
                bank_free(QK + t)
                for c in range(KC):
                    w = slice(c * DIM, (c + 1) * DIM)
                    cols = slice(t * P, (t + 1) * P)
                    mm = three(pe, po[t % 4][:], g.XH[:, c, cols], g.XL[:, c, cols], wh[2][:, w], wl[2][:, w],
                               c == 0, c == KC - 1)
                mm.then_inc(product, 1)

        @block.scalar
        def _(act):
            act.wait_ge(w_in[0], 16)
            nc.scalar.activation(wh[0][:], raw[0], ACT.Copy).then_inc(w_first, 1)
            for q in range(QK):
                act.wait_ge(product, q + 1)
                if q >= 2:
                    act.wait_ge(stored[q % 2], 32 * (q // 2))
                nc.scalar.activation(hi[:, q % 2, :], po[q % 4][:], ACT.Copy).then_inc(hi_ready, 1)
            act.wait_ge(pads, 2)
            for t in range(TILES):
                act.wait_ge(product, QK + t + 1)
                if t >= 2:
                    act.wait_ge(v_stored[t % 2], 16 * (t // 2))
                nc.scalar.activation(v[:, t % 2, :, 0:DK], po[t % 4][:].rearrange("p (h d) -> p h d", d=DK),
                                     ACT.Copy).then_inc(v_ready, 1)

        @block.vector
        def _(dve):
            dve.wait_ge(w_first, 1)
            nc.vector.tensor_tensor(wl[0][:], raw[0], wh[0][:].bitcast(F32), ALU.subtract).then_inc(w_first, 1)
            for q in range(QK):
                dve.wait_ge(hi_ready, q + 1)
                nc.vector.tensor_tensor(lo[:, q % 2, :], po[q % 4][:], hi[:, q % 2, :].bitcast(F32),
                                        ALU.subtract).then_inc(lo_ready, 1)


def attend(nc, a, g):
    with ExitStack() as ctx:
        sb, ps, sem = scoped(nc, ctx, "att")
        SET = 4
        SETS = HEADS // SET
        RING = 4
        STEPS = 4
        LEAD = 7
        PER_B = SETS * STEPS
        MROW = 96
        qs = [sb(f"qs{k}", [P, SET, NB], F32R) for k in range(RING)]
        ks = [sb(f"ks{k}", [P, SET, NB], F32R) for k in range(RING)]
        v = [sb(f"v{k}", [P, STEPS, SET * VPAD]) for k in range(RING)]
        prob = [sb(f"prob{k}", [P, SET, NB]) for k in range(2)]
        top = [sb(f"top{k}", [P, STEPS, SET]) for k in range(2)]
        mh = [sb(f"mh{k}", [SET, NB], F32R) for k in range(2)]
        ml = [sb(f"ml{k}", [SET, NB], F32R) for k in range(2)]
        o_sb = [sb(f"o_sb{k}", [P, NB]) for k in range(2)]
        rec = sb("rec", [P, STEPS, SET])
        p_first = [ps(f"first{k}", [P, NB]) for k in range(2)]
        p_second = ps("second", [P, SET, NB])
        p_out = ps("out", [P, NB])
        p_turn = ps("turn", [P, NB])
        loaded = [sem(f"loaded{k}") for k in range(RING)]
        v_in = [sem(f"v_in{k}") for k in range(RING)]
        m_in = [sem(f"m_in{k}") for k in range(RING)]
        q_pads, k_pads, first_ready, second_ready, max_turned = sem("q_pads"), sem("k_pads"), sem("first_ready"), sem("second_ready"), sem("max_turned")
        mh_ready, ml_ready, dve_chain = sem("mh_ready"), sem("ml_ready"), sem("dve_chain")
        exp_done, exp_0 = sem("exp_done"), 2
        pv_done, pv_0 = sem("pv_done"), RING * STEPS
        max_done, max_0 = sem("max_done"), 2
        turned_m, turned_0 = sem("turned_m"), 2
        o_copied, copied_0 = sem("o_copied"), 1
        o_turned, o_turned_0 = sem("o_turned"), 2
        o_done, o_done_0 = sem("o_done"), 2
        block = ctx.enter_context(nc.Block())

        def load(sp, b, w):
            slot = w % RING
            sp.wait_ge(pv_done, PER_B * b + STEPS * (w - RING) + STEPS + pv_0)
            unit, half = b * KC + w // 2, w % 2
            for dst, which, parts in ((qs, 0, (0, 0, 1, 1)), (ks, 1, (0, 1, 0, 1))):
                for r, part in enumerate(parts):
                    src = g.qk_dram[which, part, bass.ds(unit, 1), half * SET * DK:(half + 1) * SET * DK, :]
                    sp.dma_start(dst[slot][r * DK:(r + 1) * DK, :, :].bitcast(F32),
                                 src.rearrange("u (h d) t -> d (u h) t", d=DK)).then_inc(loaded[slot], 16)
            cols = slice(SET * VPAD * (w % SETS), SET * VPAD * (w % SETS + 1))
            sp.dma_start(v[slot][:], g.v_dram[bass.ds((b + w // SETS) * STEPS, STEPS), :, cols].rearrange("t p c -> p t c")
                         ).then_inc(v_in[slot], 16)

        def load_max(sp, b, w):
            sp.wait_ge(ml_ready, SETS * b + w + 1)
            for r, src in ((0, mh), (1, ml)):
                rows = slice(MROW + r * SET, MROW + (r + 1) * SET)
                sp.dma_start(qs[w % RING][rows, :, :].bitcast(F32),
                             src[w % 2][:].bitcast(F32).unsqueeze(1).to_broadcast([SET, SET, NB])
                             ).then_inc(m_in[w % RING], 16)

        @block.sync
        def _(sp):
            for w in range(3):
                load(sp, 0, w)
            sp.wait_ge(q_pads, RING)
            load_max(sp, 0, 0)

            def batch(b, last):
                for s in range(SETS):
                    if not (last and s + 3 >= SETS):
                        load(sp, b, s + 3)
                    if not (last and s + 1 >= SETS):
                        load_max(sp, b, s + 1)

            with sp.Fori(0, BATCH - 1) as b:
                batch(b, False)
            batch(BATCH - 1, True)

        @block.gpsimd
        def _(pool):
            for k in range(RING):
                nc.gpsimd.memset(ks[k][64:P, :, :].bitcast(F32), 0.0).then_inc(k_pads, 1)
                pool.wait_ge(k_pads, 3 * k + 1)
                rows = ks[k][MROW:MROW + 2 * SET, :, :]
                for part in range(2):
                    nc.gpsimd.affine_select(out=rows, in_=rows.bitcast(F32), compare_op=ALU.not_equal, fill=1.0, base=-part * SET,
                                            pattern=[[-1, SET], [0, NB]], channel_multiplier=1).then_inc(k_pads, 1)
                    pool.wait_ge(k_pads, 3 * k + 2 + part)

        @block.tensor
        def _(pe):
            pe.sem_inc(pv_done, pv_0)
            pe.sem_inc(turned_m, turned_0)
            pe.sem_inc(o_turned, o_turned_0)

            def first(b, step, item):
                w, n = step // STEPS, (step % STEPS) * 4 + item
                head, qt = n // 4, n % 4
                if n == 0:
                    if isinstance(b, int) and b == 0 and w < RING:
                        pe.wait_ge(q_pads, w + 1)
                        pe.wait_ge(k_pads, 3 * w + 3)
                    pe.wait_ge(loaded[w % RING], 128 * (SETS // RING) * b + 128 * (w // RING + 1))
                m = 4 * step + item
                pe.wait_ge(max_done, 4 * PER_B * b + m - 1 + max_0)
                pe.matmul(p_first[m % 2][:], qs[w % RING][0:MROW, head, qt * P:(qt + 1) * P],
                          ks[w % RING][0:MROW, head, :], start=True, stop=True).then_inc(first_ready, 1)

            def turn_max(b, w):
                pe.wait_ge(max_done, 4 * PER_B * b + 4 * STEPS * (w + 1) + max_0)
                if not (isinstance(b, int) and b == 0 and w == 0):
                    pe.wait_ge(o_done, SETS * b + w - 2 + o_done_0)
                for qt in range(4):
                    mm = pe.transpose(p_turn[0:SET, qt * P:(qt + 1) * P], top[w % 2][:, qt, :], g.ident[:])
                mm.then_inc(turned_m, 1)

            def second(b, step, pair):
                s, kt = step // STEPS, step % STEPS
                if kt == 0 and pair == 0:
                    pe.wait_ge(m_in[s % RING], 32 * (SETS // RING) * b + 32 * (s // RING + 1))
                pe.wait_ge(exp_done, 2 * (PER_B * b + step - 1) + pair + 1 + exp_0)
                for j in range(2 * pair, 2 * pair + 2):
                    mm = pe.matmul(p_second[:, j, :], ks[s % RING][:, j, kt * P:(kt + 1) * P], qs[s % RING][:, j, :],
                                   start=True, stop=True)
                mm.then_inc(second_ready, 1)

            def weigh(b, step):
                s, kt = step // STEPS, step % STEPS
                if kt == 0:
                    pe.wait_ge(v_in[s % RING], 16 * (SETS // RING) * b + 16 * (s // RING + 1))
                    pe.wait_ge(o_copied, SETS * b + s + copied_0)
                pe.wait_ge(exp_done, 2 * (PER_B * b + step) + 2 + exp_0)
                for j in range(SET):
                    mm = pe.matmul(p_out[VPAD * j:VPAD * (j + 1), :], v[s % RING][:, kt, VPAD * j:VPAD * (j + 1)],
                                   prob[step % 2][:, j, :], start=(kt == 0), stop=(kt == STEPS - 1))
                mm.then_inc(pv_done, 1)

            def turn_out(b, s, maxima):
                pe.wait_ge(o_copied, SETS * b + s + 1 + copied_0)
                if maxima:
                    pe.wait_ge(ml_ready, SETS * b + s + 3)
                else:
                    pe.wait_ge(o_done, SETS * b + s + o_done_0)
                for qt in range(4):
                    mm = pe.transpose(p_turn[:, qt * P:(qt + 1) * P], o_sb[s % 2][:, qt * P:(qt + 1) * P], g.ident[:])
                mm.then_inc(o_turned, 1)

            for step in range(LEAD):
                for item in range(4):
                    first(0, step, item)
                if step == STEPS:
                    turn_max(0, 0)

            def batch(b, begin, last):
                for step in range(PER_B):
                    ahead = not (last and step + LEAD >= PER_B)
                    s, kt = step // STEPS, step % STEPS
                    second(b, step, 0)
                    if ahead:
                        first(b, step + LEAD, 0)
                    second(b, step, 1)
                    if ahead:
                        first(b, step + LEAD, 1)
                    if not (begin and step == 0):
                        weigh(b, step - 1)
                    if ahead:
                        first(b, step + LEAD, 2)
                        first(b, step + LEAD, 3)
                    maxima = not (last and s + 1 >= SETS)
                    if kt == 1 and maxima:
                        turn_max(b, s + 1)
                    if kt == 2 and not (begin and s == 0):
                        turn_out(b, s - 1, maxima)

            batch(0, True, False)
            with pe.Fori(1, BATCH - 1) as b:
                batch(b, False, False)
            batch(BATCH - 1, False, True)
            weigh(BATCH - 1, PER_B - 1)
            turn_out(BATCH - 1, SETS - 1, False)

        @block.scalar
        def _(act):
            act.sem_inc(exp_done, exp_0)
            act.sem_inc(o_copied, copied_0)

            def exps(b, step, pair):
                act.wait_ge(second_ready, 2 * (PER_B * b + step) + pair + 1)
                act.wait_ge(pv_done, PER_B * b + step - 1 + pv_0)
                js = slice(2 * pair, 2 * pair + 2)
                nc.scalar.activation(prob[step % 2][:, js, :], p_second[:, js, :], ACT.Exp,
                                     scale=DK ** -0.5).then_inc(exp_done, 1)

            def high_max(b, w):
                act.wait_ge(turned_m, SETS * b + w + 1 + turned_0)
                nc.scalar.activation(mh[w % 2][:], p_turn[0:SET, :], ACT.Copy, scale=-1.0).then_inc(mh_ready, 1)

            def copy_out(b, s):
                act.wait_ge(pv_done, PER_B * b + STEPS * (s + 1) + pv_0)
                act.wait_ge(o_turned, SETS * b + s - 1 + o_turned_0)
                nc.scalar.activation(o_sb[s % 2][:], p_out[:], ACT.Copy).then_inc(o_copied, 1)

            high_max(0, 0)

            def batch(b, begin, last):
                for step in range(PER_B):
                    s, kt = step // STEPS, step % STEPS
                    exps(b, step, 0)
                    if kt == 2 and not (last and s + 1 >= SETS):
                        high_max(b, s + 1)
                    exps(b, step, 1)
                    if kt == 0 and not (begin and s == 0):
                        copy_out(b, s - 1)

            batch(0, True, False)
            with act.Fori(1, BATCH - 1) as b:
                batch(b, False, False)
            batch(BATCH - 1, False, True)
            copy_out(BATCH - 1, SETS - 1)

        @block.vector
        def _(dve):
            dve.sem_inc(max_done, max_0)
            dve.sem_inc(o_done, o_done_0)
            for k in range(RING):
                nc.vector.memset(qs[k][64:P, :, :].bitcast(F32), 0.0).then_inc(q_pads, 1)

            def maximum(b, step, item):
                w, n = step // STEPS, (step % STEPS) * 4 + item
                head, qt = n // 4, n % 4
                m = 4 * step + item
                if n == 0:
                    dve.wait_ge(turned_m, SETS * b + w - 1 + turned_0)
                dve.wait_ge(first_ready, 4 * PER_B * b + m + 1)
                nc.vector.tensor_reduce(top[w % 2][:, qt, head:head + 1], p_first[m % 2][:], AX.X,
                                        ALU.max).then_inc(max_done, 1)

            def low_max(b, w):
                dve.wait_ge(mh_ready, SETS * b + w + 1)
                nc.vector.scalar_tensor_tensor(out=ml[w % 2][:], in0=p_turn[0:SET, :], scalar=-1.0,
                                               in1=mh[w % 2][:].bitcast(F32), op0=ALU.mult,
                                               op1=ALU.subtract).then_inc(ml_ready, 1)

            def divide(b, s):
                dve.wait_ge(o_turned, SETS * b + s + 1 + o_turned_0)
                o = p_turn[:].rearrange("p (t h d) -> p t h d", t=STEPS, h=SET)
                nc.vector.reciprocal(rec[:].unsqueeze(3), o[:, :, :, DK:DK + 1]).then_inc(dve_chain, 1)
                dve.wait_ge(dve_chain, SETS * b + s + 1)
                tile = (b + s // SETS) * PER_BLOCK
                at = (s % SETS) * SET * DK
                dst = g.Y[:, bass.ds(tile, PER_BLOCK), at:at + SET * DK].rearrange("p t (h d) -> p t h d", d=DK)
                nc.vector.tensor_tensor(dst, o[:, :, :, 0:DK], rec[:].unsqueeze(3).to_broadcast([P, STEPS, SET, DK]),
                                        ALU.mult).then_inc(o_done, 1)

            for step in range(LEAD):
                for item in range(4):
                    maximum(0, step, item)
                if step == STEPS:
                    low_max(0, 0)

            def batch(b, begin, last):
                for step in range(PER_B):
                    s, kt = step // STEPS, step % STEPS
                    ahead = not (last and step + LEAD >= PER_B)
                    for item in range(4):
                        if ahead:
                            maximum(b, step + LEAD, item)
                        if item == 1 and kt == 2 and not (last and s + 1 >= SETS):
                            low_max(b, s + 1)
                        if item == 1 and kt == 3 and not (begin and s == 0):
                            divide(b, s - 1)

            batch(0, True, False)
            with dve.Fori(1, BATCH - 1) as b:
                batch(b, False, False)
            batch(BATCH - 1, False, True)
            divide(BATCH - 1, SETS - 1)


def attention_out(nc, a, g):
    with ExitStack() as ctx:
        sb, ps, sem = scoped(nc, ctx, "wo")
        raw = sb("raw", [P, KC * DIM])
        wh = sb("wh", [P, KC * DIM], F32R)
        wl = sb("wl", [P, KC * DIM], F32R)
        th = sb("th", [P, 2, KC, P], F32R)
        tl = sb("tl", [P, 2, KC, P], F32R)
        pt = [ps(f"pt{k}", [P, KC, P]) for k in range(2)]
        po = [ps(f"po{k}", [P, DIM]) for k in range(2)]
        w_in, w_split = sem("w_in"), sem("w_split")
        turned, hi_ready, lo_ready, product, added = (sem("turned"), sem("hi_ready"), sem("lo_ready"), sem("product"),
                                                      sem("added"))
        block = ctx.enter_context(nc.Block())

        @block.sync
        def _(sp):
            sp.dma_start(raw[:].rearrange("p (c e) -> p c e", c=KC),
                         a["woT"].rearrange("(c p) e -> p c e", p=P)).then_inc(w_in, 16)

        @block.tensor
        def _(pe):
            for t in range(TILES + 1):
                if t < TILES:
                    if t >= 2:
                        pe.wait_ge(lo_ready, t - 1)
                    for c in range(KC):
                        mm = pe.transpose(pt[t % 2][:, c, :], g.Y[:, t, c * P:(c + 1) * P], g.ident[:])
                    mm.then_inc(turned, 1)
                if t:
                    m = t - 1
                    if m == 0:
                        pe.wait_ge(w_split, 2)
                    if m >= 2:
                        pe.wait_ge(added, m - 1)
                    pe.wait_ge(lo_ready, m + 1)
                    for c in range(KC):
                        w = slice(c * DIM, (c + 1) * DIM)
                        mm = three(pe, po[m % 2][:], th[:, m % 2, c, :], tl[:, m % 2, c, :], wh[:, w], wl[:, w],
                                   c == 0, c == KC - 1)
                    mm.then_inc(product, 1)

        @block.scalar
        def _(act):
            act.wait_ge(w_in, 16)
            nc.scalar.activation(wh[:], raw[:], ACT.Copy).then_inc(w_split, 1)
            for t in range(TILES):
                act.wait_ge(turned, t + 1)
                if t >= 2:
                    act.wait_ge(product, t - 1)
                nc.scalar.activation(th[:, t % 2], pt[t % 2][:], ACT.Copy).then_inc(hi_ready, 1)

        @block.vector
        def _(dve):
            dve.wait_ge(w_split, 1)
            nc.vector.tensor_tensor(wl[:], raw[:], wh[:].bitcast(F32), ALU.subtract).then_inc(w_split, 1)
            for t in range(TILES + 1):
                if t < TILES:
                    dve.wait_ge(hi_ready, t + 1)
                    nc.vector.tensor_tensor(tl[:, t % 2], pt[t % 2][:], th[:, t % 2].bitcast(F32),
                                            ALU.subtract).then_inc(lo_ready, 1)
                if t:
                    m = t - 1
                    dve.wait_ge(product, m + 1)
                    nc.vector.tensor_tensor(g.Y[:, m, :], po[m % 2][:], g.X[:, m, :], ALU.add).then_inc(added, 1)


def quantised_mlp(nc, a, g):
    with ExitStack() as ctx:
        sb, ps, sem = scoped(nc, ctx, "ffn")
        PAIR = 2 * P
        W13 = KC * 2 * PAIR
        WN = W13 + 2 * DIM
        scales = sb("scales", [P, FPAIRS, WN // P])
        raw = sb("raw", [P, WN])
        wh = [sb(f"wh{s}", [P, WN], F32R) for s in range(2)]
        wl = [sb(f"wl{s}", [P, WN], F32R) for s in range(2)]
        silu = sb("silu", [P, 2, PAIR])
        h = sb("h", [P, PAIR])
        hq = sb("hq", [P, 2, PAIR])
        amax = sb("amax", [P, 2])
        scale = sb("scale", [P, 2])
        inv = sb("inv", [P, 2])
        hh = sb("hh", [P, 2, 2, P], F32R)
        hl = sb("hl", [P, 2, 2, P], F32R)
        pg = [ps(f"pg{k}", [P, 2 * PAIR]) for k in range(2)]
        pt = [ps(f"pt{k}", [P, 2, P]) for k in range(2)]
        py = [ps(f"py{k}", [P, DIM]) for k in range(2)]
        w_in, sc_in, pool_chain, dve_chain = sem("w_in"), sem("sc_in"), sem("pool_chain"), sem("dve_chain")
        g_ready, s_ready, hh_ready = sem("g_ready"), sem("s_ready"), sem("hh_ready")
        split_ready, split_0 = sem("split_ready"), 1
        u_used, used_0 = sem("u_used"), 2
        turned, turned_0 = sem("turned"), 2
        hq_ready, hq_0 = sem("hq_ready"), 2
        hl_ready, hl_0 = sem("hl_ready"), 2
        y_ready, y_0 = sem("y_ready"), 2 * TILES
        y_added, added_0 = sem("y_added"), TILES
        block = ctx.enter_context(nc.Block())

        def pairs(eng, body):
            with eng.Fori(0, FPAIRS // 2) as i:
                for s in range(2):
                    body(2 * i + s, s)
            body(FPAIRS - 1, 0)

        @block.sync
        def _(sp):
            sp.dma_start(scales[:], a["scales"].partition_broadcast(P)).then_inc(sc_in, 16)

            def fetch(p, s):
                sp.wait_ge(split_ready, p + split_0)
                sp.dma_start(raw[:], a["w132"][p]).then_inc(w_in, 16)

            pairs(sp, fetch)

        @block.gpsimd
        def _(pool):
            pool.sem_inc(split_ready, split_0)
            pool.wait_ge(sc_in, 16)

            def split(p, s):
                wait_apart(pool, w_in, 16 * p + 16)
                blocks = raw[:].rearrange("p (n k) -> p n k", k=P)
                sc = scales[:, bass.ds(p, 1), :].rearrange("p a n -> p (a n)").unsqueeze(2).to_broadcast([P, WN // P, P])
                nc.gpsimd.tensor_tensor(blocks, blocks, sc, ALU.mult).then_inc(pool_chain, 1)
                pool.wait_ge(pool_chain, 2 * p + 1)
                wait_apart(pool, y_ready, (p - 1) * TILES + y_0)
                nc.gpsimd.tensor_scalar(wh[s][:], raw[:], 1.0, 0.0, ALU.mult, ALU.add).then_inc(pool_chain, 1)
                pool.wait_ge(pool_chain, 2 * p + 2)
                nc.gpsimd.tensor_tensor(wl[s][:], raw[:], wh[s][:].bitcast(F32), ALU.subtract).then_inc(split_ready, 1)

            pairs(pool, split)

        @block.tensor
        def _(pe):
            pe.sem_inc(y_ready, y_0)
            pe.sem_inc(turned, turned_0)

            def pair(p, s):
                def up(t):
                    pe.wait_ge(u_used, TILES * p + t - 1 + used_0)
                    for c in range(KC):
                        w = slice(c * 2 * PAIR, (c + 1) * 2 * PAIR)
                        cols = slice(t * P, (t + 1) * P)
                        mm = three(pe, pg[t % 2][:], g.XH[:, c, cols], g.XL[:, c, cols], wh[s][:, w], wl[s][:, w],
                                   c == 0, c == KC - 1)
                    mm.then_inc(g_ready, 1)

                def turn(t):
                    pe.wait_ge(hq_ready, TILES * p + t + 1 + hq_0)
                    pe.wait_ge(hl_ready, TILES * p + t - 1 + hl_0)
                    for i in range(2):
                        mm = pe.transpose(pt[t % 2][:, i, :], hq[:, t % 2, i * P:(i + 1) * P], g.ident[:])
                    mm.then_inc(turned, 1)

                def down(t):
                    pe.wait_ge(hl_ready, TILES * p + t + 1 + hl_0)
                    pe.wait_ge(y_added, TILES * p + t - 1 + added_0)
                    for i in range(2):
                        w = slice(W13 + i * DIM, W13 + (i + 1) * DIM)
                        mm = three(pe, py[t % 2][:], hh[:, t % 2, i, :], hl[:, t % 2, i, :], wh[s][:, w], wl[s][:, w],
                                   i == 0, i == 1)
                    mm.then_inc(y_ready, 1)

                pe.wait_ge(split_ready, p + 1 + split_0)
                for t in range(TILES + 2):
                    if t < TILES:
                        up(t)
                    if 1 <= t <= TILES:
                        turn(t - 1)
                    if t >= 2:
                        down(t - 2)

            pairs(pe, pair)

        @block.scalar
        def _(act):
            def pair(p, s):
                for t in range(TILES + 1):
                    if t < TILES:
                        act.wait_ge(g_ready, TILES * p + t + 1)
                        act.wait_ge(u_used, TILES * p + t - 1 + used_0)
                        nc.scalar.activation(silu[:, t % 2, :], pg[t % 2][:, 0:PAIR], ACT.Silu).then_inc(s_ready, 1)
                    if t:
                        m = t - 1
                        act.wait_ge(turned, TILES * p + m + 1 + turned_0)
                        act.wait_ge(y_ready, TILES * p + m - 1 + y_0)
                        nc.scalar.activation(hh[:, m % 2], pt[m % 2][:], ACT.Copy).then_inc(hh_ready, 1)

            pairs(act, pair)

        @block.vector
        def _(dve):
            own = Chain(dve, dve_chain)
            dve.sem_inc(u_used, used_0)
            dve.sem_inc(hq_ready, hq_0)
            dve.sem_inc(hl_ready, hl_0)
            dve.sem_inc(y_added, added_0)
            PER_TILE = 4

            def pair(p, s):
                def hidden(t):
                    n = TILES * p + t
                    own.base, own.n = PER_TILE * n, 0
                    dve.wait_ge(s_ready, n + 1)
                    dve.wait_ge(hq_ready, n + hq_0)
                    nc.vector.tensor_tensor(h[:], pg[t % 2][:, PAIR:2 * PAIR], silu[:, t % 2, :],
                                            ALU.mult).then_inc(u_used, 1)
                    dve.wait_ge(u_used, n + 1 + used_0)
                    own.step(nc.vector.tensor_reduce(amax[:], h[:].rearrange("p (i k) -> p i k", k=P), AX.X, ALU.max,
                                                     apply_absolute_value=True))
                    own.settle()
                    own.step(nc.vector.tensor_scalar(scale[:], amax[:], 1.0 / FP8_MAX, 1e-12, ALU.mult, ALU.add))
                    own.settle()
                    own.step(nc.vector.reciprocal(inv[:], scale[:]))
                    own.settle()
                    dve.wait_ge(turned, n - 1 + turned_0)
                    own.step(nc.vector.tensor_scalar(hq[:, t % 2, 0:P], h[:, 0:P], inv[:, 0:1], scale[:, 0:1],
                                                     ALU.mult, ALU.mult))
                    nc.vector.tensor_scalar(hq[:, t % 2, P:PAIR], h[:, P:PAIR], inv[:, 1:2], scale[:, 1:2],
                                            ALU.mult, ALU.mult).then_inc(hq_ready, 1)

                def low(t):
                    dve.wait_ge(hh_ready, TILES * p + t + 1)
                    nc.vector.tensor_tensor(hl[:, t % 2], pt[t % 2][:], hh[:, t % 2].bitcast(F32),
                                            ALU.subtract).then_inc(hl_ready, 1)

                def add(t):
                    dve.wait_ge(y_ready, TILES * p + t + 1 + y_0)
                    dve.wait_ge(y_added, TILES * (p - 1) + t + 1 + added_0)
                    nc.vector.tensor_tensor(g.Y[:, t, :], py[t % 2][:], g.Y[:, t, :], ALU.add).then_inc(y_added, 1)

                for t in range(TILES + 2):
                    if t < TILES:
                        hidden(t)
                    if 1 <= t <= TILES:
                        low(t - 1)
                    if t >= 2:
                        add(t - 2)

            pairs(dve, pair)


class Shared:
    pass


def program(nc, a, out):
    g = Shared()
    g.brow_dram = nc.dram_tensor("brow_dram", [STATE, BATCH, NB], F32, kind="Internal").ap()
    g.qk_dram = nc.dram_tensor("qk_dram", [2, 2, UNITS, P, NB], F32, kind="Internal").ap()
    g.v_dram = nc.dram_tensor("v_dram", [TILES, P, HEADS * VPAD], F32, kind="Internal").ap()
    g.sorted_x = nc.dram_tensor("sorted_x", [SORTED * P, DIM], F32, kind="Internal").ap()
    g.sorted_y = nc.dram_tensor("sorted_y", [SORTED * P, DIM], F32, kind="Internal").ap()
    with ExitStack() as ctx:
        sb, _, sem = scoped(nc, ctx, "all")
        g.ident = sb("ident", [P, P])
        g.gate = sb("gate", [P, MLPS, TILES])
        g.weight, g.at = sb("weight", [P, TOP, TILES]), sb("at", [P, TOP, TILES], mybir.dt.int32)
        g.owner = sb("owner", [1, SORTED], mybir.dt.int32)
        sums = sb("sums", [P, KC * TOK])
        g.sums = sums
        g.XT = sums[:].rearrange("p (c t) -> p c t", c=KC)
        g.Y = sums[:].rearrange("p (t d) -> p t d", t=TILES)
        g.X = sb("X", [P, TILES, DIM])
        with ExitStack() as ssm:
            sb, _, _ = scoped(nc, ssm, "ssm")
            g.sel = sb("sel", [STATE, STATE, P])
            g.A = sb("A", [P, KC, STATE])
            g.D1 = sb("D1", [P, KC])
            g.DT = sb("DT", [P, KC, TOK])
            g.U = sb("U", [P, KC, TOK])
            g.CT = sb("CT", [STATE, TOK])
            ssm_inputs(nc, a, g)
            ssm_scan(nc, a, g)
        with ExitStack() as later:
            sb, _, _ = scoped(nc, later, "later")
            g.XH = sb("XH", [P, KC, TOK], F32R)
            g.XL = sb("XL", [P, KC, TOK], F32R)
            normalise(nc, g, "ln1", True)
            with ExitStack() as moe:
                sb, _, sem = scoped(nc, moe, "mlps")
                g.raw = [sb(f"raw{s}", [P, WN + 2]) for s in range(2)]
                g.wh = [sb(f"wh{s}", [P, WN], F32R) for s in range(2)]
                g.wl = [sb(f"wl{s}", [P, WN], F32R) for s in range(2)]
                g.shared_in, g.shared_split = [sem("shared_in0"), sem("shared_in1")], sem("shared_split")
                route(nc, a, g)
                shared_mlp(nc, a, g)
                sorted_experts(nc, a, g)
            normalise(nc, g, "ln2", False, gather=True)
            project(nc, a, g)
        attend(nc, a, g)
        attention_out(nc, a, g)
        with ExitStack() as later:
            sb, _, _ = scoped(nc, later, "last")
            g.XH = sb("XH", [P, KC, TOK], F32R)
            g.XL = sb("XL", [P, KC, TOK], F32R)
            normalise(nc, g, "ln3", False, quantise=True)
            quantised_mlp(nc, a, g)
        normalise(nc, g, "ln4", False, out)


def laid_out(x):
    import numpy as np

    def dense(v):
        return np.ascontiguousarray(v)

    def columns(v):
        return dense(v.reshape(-1, P).T)

    def halves(w):
        return w.reshape(DIM, 2, INTER).transpose(1, 0, 2)

    def folded(w):
        return w.reshape(MLPS, KC, P, INTER).transpose(0, 2, 1, 3).reshape(MLPS, P, KC * INTER)

    def by_pair(w):
        return w.T.reshape(KC, P, FPAIRS, 2 * P)

    w1 = np.concatenate([x["L0_ffn_ew1"], halves(x["L0_ffn_sw1"])])
    w2 = np.concatenate([x["L0_ffn_ew2"], halves(x["L0_ffn_sw2"])])
    w3 = np.concatenate([x["L0_ffn_ew3"], x["L0_ffn_sw3"].reshape(2, INTER, DIM)])
    b1 = np.concatenate([x["L0_ffn_eb1"], x["L0_ffn_sb1"].reshape(2, INTER)])
    b2 = np.concatenate([x["L0_ffn_eb2"], x["L0_ffn_sb2"].reshape(2, INTER)])
    b3 = np.concatenate([x["L0_ffn_eb3"], x["L0_ffn_sb3"].reshape(1, DIM), np.zeros((1, DIM), np.float32)])
    w13 = np.stack([by_pair(x["L1_ffn_w1"]), by_pair(x["L1_ffn_w3"])], 3)
    w13 = w13.transpose(2, 1, 0, 3, 4).reshape(FPAIRS, P, KC * 4 * P)
    down = x["L1_ffn_w2"].T.reshape(FPAIRS, 2, P, DIM).transpose(0, 2, 1, 3).reshape(FPAIRS, P, 2 * DIM)
    s1, s3 = (x[n].reshape(FPAIRS, 2, KC) for n in ("L1_ffn_w1_scale", "L1_ffn_w3_scale"))
    s13 = np.stack([s1, s3], 1).transpose(0, 3, 1, 2).reshape(FPAIRS, 4 * KC)
    s2 = x["L1_ffn_w2_scale"].T.reshape(FPAIRS, 2 * KC)
    return {
        "xT": dense(x["L0_attn_x"].reshape(TOK, DIM).T),
        "xprojT": dense(x["L0_attn_x_proj_w"].T),
        "dtprojT": dense(x["L0_attn_dt_proj_w"].T),
        "dtb": columns(x["L0_attn_dt_proj_b"]),
        "alog": dense(x["L0_attn_A_log"]),
        "dcoef": columns(x["L0_attn_D"]),
        "router_w": dense(x["L0_ffn_router_w"]),
        "router_b": dense(x["L0_ffn_router_b"]),
        "router_bias": dense(x["L0_ffn_router_bias"]),
        "order": np.arange(EXPERTS, 0, -1, dtype=np.float32),
        "steps": np.arange(TILES, dtype=np.float32) * P,
        "before": np.tri(EXPERTS, k=-1, dtype=np.float32),
        "tile_no": np.arange(SORTED, dtype=np.float32),
        "w123": dense(np.concatenate([folded(w1), folded(w2), w3, b1[:, :, None], b2[:, :, None]], axis=2)),
        "b3": b3,
        "wqkvT": dense(np.stack([x[f"L1_attn_w_{n}"].T for n in "qkv"])),
        "woT": dense(x["L1_attn_w_o"].T),
        "w132": dense(np.concatenate([w13, down], axis=2)),
        "scales": dense(np.concatenate([s13, s2], axis=1)),
    }


def kernel(**inputs):
    import numpy as np
    import concourse.bacc as bacc
    from concourse.bass_utils import run_bass_kernel_spmd

    nc = bacc.Bacc("TRN2", target_bir_lowering=False, num_devices=1)
    arrays = laid_out({n: np.asarray(v) for n, v in inputs.items()})
    aps = {n: nc.dram_tensor(f"in_{n}", v.shape, mybir.dt.from_np(v.dtype), kind="ExternalInput").ap()
           for n, v in arrays.items()}
    out = nc.dram_tensor("out_x", (TOK, DIM), F32, kind="ExternalOutput").ap()
    program(nc, aps, out)
    result = run_bass_kernel_spmd(nc, [{f"in_{n}": v for n, v in arrays.items()}], core_ids=[0])
    return result.results[0]["out_x"].reshape(BATCH, SEQ, DIM)
```

```python
from contextlib import ExitStack


import numpy as np

import concourse.bass as bass
from concourse import mybir

F32 = mybir.dt.float32
F32R = mybir.dt.float32r
ALU = mybir.AluOpType
ACT = mybir.ActivationFunctionType
AX = mybir.AxisListType

P = 128
BATCH, SEQ, DIM = 4, 512, 512
TOK = BATCH * SEQ
KC = DIM // P
TILES = TOK // P
NB = 512
BLOCKS = TOK // NB
PER_BLOCK = NB // P
STATE, RANK = 16, 16
EXPERTS, GROUPS, INTER = 16, 4, 128
MLPS = EXPERTS + 2
TOP = 2
TURN = 4
SORTED = -(-(TOP * TILES + EXPERTS - 1) // TURN) * TURN
WUP = 2 * KC * INTER
WN = WUP + DIM
HEADS, DK = 32, 16
GHEADS = P // DK
UNITS = BATCH * KC
VPAD = 32
FFN_INTER = 1792
FBLOCKS = FFN_INTER // P
FPAIRS = FBLOCKS // 2
EPS = 1e-5
FP8_MAX = 448.0
BIG = 3.0e38


class Chain:

    def __init__(self, eng, sem):
        self.eng, self.sem, self.base, self.n = eng, sem, 0, 0

    def step(self, ins):
        ins.then_inc(self.sem, 1)
        self.n += 1

    def settle(self):
        self.eng.wait_ge(self.sem, self.base + self.n)

    def enter(self, i, per):
        self.start, self.per = self.base + self.n, per
        self.base, self.n = self.start + i * per, 0

    def leave(self, times):
        assert self.n == self.per, (self.n, self.per)
        self.base, self.n = self.start + times * self.per, 0


def clear(nc, sems):
    numbers = sorted(s.num for s in sems)
    with nc.Block() as block:
        @block.gpsimd
        def _(pool):
            first = numbers[0]
            for n, after in zip(numbers, numbers[1:] + [None]):
                if after != n + 1:
                    pool.sem_clear(range(first, n + 1))
                    first = after


def scoped(nc, ctx, tag, reused=False):
    sems = []
    if reused:
        ctx.callback(clear, nc, sems)

    def sb(name, shape, dt=F32):
        return ctx.enter_context(nc.sbuf_tensor(f"{tag}_{name}", shape, dt))

    def ps(name, shape):
        return ctx.enter_context(nc.psum_tensor(f"{tag}_{name}", shape, F32))

    def sem(name):
        sems.append(ctx.enter_context(nc.semaphore(f"{tag}_{name}")))
        return sems[-1]

    return sb, ps, sem


def wait_apart(eng, sem, value):
    eng.wait_ge(sem, value)
    eng.nop(nofuse=True)


class Ahead:

    def __init__(self, nc, ctx, tag):
        sb, _, sem = scoped(nc, ctx, tag)
        self.raw = sb("raw", [P, KC * DIM])
        self.hi, self.lo = sb("hi", [P, KC * DIM], F32R), sb("lo", [P, KC * DIM], F32R)
        self.landed, self.hi_ready, self.lo_ready = sem("landed"), sem("hi_ready"), sem("lo_ready")

    def load(self, sp, src):
        sp.dma_start(self.raw[:].rearrange("p (c e) -> p c e", c=KC),
                     src.rearrange("(c p) e -> p c e", p=P)).then_inc(self.landed, 16)

    def split(self, pool):
        pool.wait_ge(self.landed, 16)
        pool.tensor_scalar(self.hi[:], self.raw[:], 1.0, 0.0, ALU.mult, ALU.add).then_inc(self.hi_ready, 1)
        pool.wait_ge(self.hi_ready, 1)
        pool.tensor_tensor(self.lo[:], self.raw[:], self.hi[:].bitcast(F32), ALU.subtract).then_inc(self.lo_ready, 1)


def three(pe, out, lh, ll, rh, rl, first, last):
    pe.matmul(out, lh, rh, start=first, stop=False)
    pe.matmul(out, lh, rl, start=False, stop=False)
    return pe.matmul(out, ll, rh, start=False, stop=last)


def ssm_inputs(nc, a, g):
    with ExitStack() as ctx:
        sb, ps, sem = scoped(nc, ctx, "pre", reused=True)
        GAP = 32
        wx = sb("wx", [P, KC, 2 * GAP + STATE])
        wdt = sb("wdt", [RANK, DIM])
        dtb = sb("dtb", [P, KC])
        alog = sb("alog", [P, KC, STATE])
        dtin = sb("dtin", [RANK, 2, NB])
        brow = sb("brow", [STATE, 2, NB])
        zero = sb("zero", [P, DIM])
        e, ln = (sb(n, [P, 2, KC, NB]) for n in ("e", "ln"))
        pos = g.X[:].rearrange("p (b c) t -> p b c t", c=KC)
        rest = sb("rest", [P, KC, NB])
        rows = [ps(f"rows{k}", [P, NB]) for k in range(2)]
        pz = [ps(f"pz{k}", [P, NB]) for k in range(4)]
        gaps, loaded, x_in = sem("gaps"), sem("loaded"), [sem(f"x_in{b}") for b in range(BATCH)]
        rows_ready, rows_copied, z_ready, mag_ready = sem("rows_ready"), sem("rows_copied"), sem("z_ready"), sem("mag_ready")
        pos_ready, e_ready, ln_ready, a_ready = sem("pos_ready"), sem("e_ready"), sem("ln_ready"), sem("a_ready")
        d1_ready, rounded, sum_ready, rest_ready = sem("d1_ready"), sem("rounded"), sem("sum_ready"), sem("rest_ready")
        dt_ready, consts, u_ready = sem("dt_ready"), sem("consts"), sem("u_ready")
        masked = sem("masked")
        zeroed, cleared, b_stored = sem("zeroed"), sem("cleared"), [sem("b_stored0"), sem("b_stored1")]
        CLEARS = SORTED // BATCH
        block = ctx.enter_context(nc.Block())

        @block.sync
        def _(sp):
            sp.dma_start(wdt[:], a["dtprojT"]).then_inc(loaded, 16)
            sp.dma_start(dtb[:], a["dtb"]).then_inc(loaded, 16)
            sp.wait_ge(gaps, 1)
            for k in range(3):
                sp.dma_start(wx[:, :, k * GAP:k * GAP + STATE],
                             a["xprojT"].rearrange("(c p) r -> p c r", p=P)[:, :, k * STATE:(k + 1) * STATE]).then_inc(loaded, 16)
            for b in range(BATCH):
                sp.dma_start(g.XT[:, :, b * NB:(b + 1) * NB],
                             a["xT"].rearrange("(c p) t -> p c t", p=P)[:, :, b * NB:(b + 1) * NB]).then_inc(x_in[b], 16)
                if b == 0:
                    sp.dma_start(alog[:], a["alog"].rearrange("(c p) n -> p c n", p=P)).then_inc(loaded, 16)
                    sp.dma_start(g.D1[:], a["dcoef"]).then_inc(loaded, 16)
            sp.wait_ge(zeroed, 1)
            for b in range(BATCH):
                at = g.sorted_x.rearrange("(t p) d -> p t d", p=P)[:, b * CLEARS:(b + 1) * CLEARS, :]
                sp.dma_start(at, zero[:].unsqueeze(1).to_broadcast([P, CLEARS, DIM])).then_inc(cleared, 16)
                sp.wait_ge(rows_copied, 3 * b + 2)
                sp.dma_start(g.brow_dram[:, b, :], brow[:, b % 2, :]).then_inc(b_stored[b % 2], 16)
            for s in range(2):
                sp.wait_ge(b_stored[s], 16 * BATCH // 2)
            sp.wait_ge(cleared, 16 * BATCH)

        @block.tensor
        def _(pe):
            def project_rows(b):
                pe.wait_ge(x_in[b], 16)
                if b >= 2:
                    pe.wait_ge(rows_copied, 3 * (b - 1))
                for c in range(KC):
                    mm = pe.matmul(rows[b % 2][0:2 * GAP + STATE, :], wx[:, c, :], g.XT[:, c, b * NB:(b + 1) * NB],
                                   start=(c == 0), stop=(c == KC - 1))
                mm.then_inc(rows_ready, 1)

            pe.wait_ge(loaded, 112)
            project_rows(0)
            for b in range(BATCH):
                if b + 1 < BATCH:
                    project_rows(b + 1)
                pe.wait_ge(rows_copied, 3 * b + 1)
                for c in range(KC):
                    i = b * KC + c
                    if b:
                        pe.wait_ge(pos_ready, i - KC + 1)
                    pe.matmul(pz[c][:], wdt[:, c * P:(c + 1) * P], dtin[:, b % 2, :], start=True,
                              stop=True).then_inc(z_ready, 1)

        @block.scalar
        def _(act):
            act.wait_ge(loaded, 112)
            nc.scalar.activation(g.A[:], alog[:], ACT.Exp).then_inc(a_ready, 1)

            def copy_rows(b):
                act.wait_ge(rows_ready, b + 1)
                if b >= 2:
                    act.wait_ge(z_ready, KC * (b - 1))
                nc.scalar.activation(dtin[:, b % 2, :], rows[b % 2][0:RANK, :], ACT.Copy).then_inc(rows_copied, 1)
                if b >= 2:
                    act.wait_ge(b_stored[b % 2], 16 * (b // 2))
                nc.scalar.activation(brow[:, b % 2, :], rows[b % 2][GAP:GAP + STATE, :], ACT.Copy).then_inc(rows_copied, 1)
                nc.scalar.activation(g.CT[:, b * NB:(b + 1) * NB], rows[b % 2][2 * GAP:2 * GAP + STATE, :],
                                     ACT.Copy).then_inc(rows_copied, 1)

            copy_rows(0)
            for b in range(BATCH):
                s = b % 2
                if b >= 2:
                    act.wait_ge(sum_ready, b - 1)
                for c in range(KC):
                    act.wait_ge(z_ready, b * KC + c + 1)
                    nc.scalar.activation(e[:, s, c, :], pz[c][:], ACT.Abs, bias=dtb[:, c:c + 1]).then_inc(mag_ready, 1)
                if b + 1 < BATCH:
                    copy_rows(b + 1)
                act.wait_ge(mag_ready, KC * (b + 1))
                nc.scalar.activation(e[:, s], e[:, s], ACT.Exp, scale=-1.0).then_inc(e_ready, 1)
                act.wait_ge(e_ready, b + 1)
                nc.scalar.activation(ln[:, s], e[:, s], ACT.Ln, bias=1.0).then_inc(ln_ready, 1)

        @block.vector
        def _(dve):
            dve.wait_ge(loaded, 112)
            nc.vector.tensor_scalar(g.D1[:], g.D1[:], 1.0, None, ALU.add).then_inc(d1_ready, 1)
            dve.wait_ge(a_ready, 1)
            nc.vector.tensor_scalar(g.A[:], g.A[:], -1.0, None, ALU.mult).then_inc(a_ready, 1)

            def positive(b):
                for c in range(KC):
                    dve.wait_ge(mag_ready, b * KC + c + 1)
                    nc.vector.tensor_scalar(pos[:, b, c, :], pz[c][:], dtb[:, c:c + 1], 0.0, ALU.add,
                                            ALU.max).then_inc(pos_ready, 1)

            positive(0)
            for b in range(BATCH):
                s = b % 2
                dve.wait_ge(e_ready, b + 1)
                if b:
                    dve.wait_ge(dt_ready, b)
                nc.vector.tensor_scalar(rest[:], e[:, s], 1.0, -1.0, ALU.add, ALU.add).then_inc(rounded, 1)
                dve.wait_ge(rounded, b + 1)
                dve.wait_ge(ln_ready, b + 1)
                nc.vector.scalar_tensor_tensor(out=ln[:, s], in0=rest[:], scalar=0.0, in1=ln[:, s], op0=ALU.is_gt,
                                               op1=ALU.mult).then_inc(masked, 1)
                dve.wait_ge(masked, b + 1)
                nc.vector.tensor_tensor(rest[:], e[:, s], rest[:], ALU.subtract).then_inc(rest_ready, 1)
                dve.wait_ge(pos_ready, KC * (b + 1))
                nc.vector.tensor_tensor(pos[:, b], pos[:, b], ln[:, s], ALU.add).then_inc(sum_ready, 1)
                if b + 1 < BATCH:
                    positive(b + 1)

        @block.gpsimd
        def _(pool):
            nc.gpsimd.memset(wx[:], 0.0).then_inc(gaps, 1)
            nc.gpsimd.memset(zero[:], 0.0).then_inc(zeroed, 1)
            nc.gpsimd.memset(g.sel[:], 0.0).then_inc(consts, 1)
            nc.gpsimd.memset(g.ident[:], 0.0).then_inc(consts, 1)
            pool.wait_ge(consts, 2)
            nc.gpsimd.affine_select(out=g.sel[:], in_=g.sel[:], compare_op=ALU.not_equal, fill=1.0, base=0,
                                    pattern=[[-1, STATE], [0, P]], channel_multiplier=1).then_inc(consts, 1)
            nc.gpsimd.affine_select(out=g.ident[:], in_=g.ident[:], compare_op=ALU.not_equal, fill=1.0, base=0,
                                    pattern=[[-1, P]], channel_multiplier=1).then_inc(consts, 1)
            for b in range(BATCH):
                cols = slice(b * NB, (b + 1) * NB)
                pool.wait_ge(sum_ready, b + 1)
                pool.wait_ge(rest_ready, b + 1)
                nc.gpsimd.tensor_tensor(g.DT[:, :, cols], pos[:, b], rest[:], ALU.add).then_inc(dt_ready, 1)
                pool.wait_ge(dt_ready, b + 1)
                nc.gpsimd.tensor_tensor(g.U[:, :, cols], g.DT[:, :, cols], g.XT[:, :, cols], ALU.mult).then_inc(u_ready, 1)


def ssm_scan(nc, a, g):
    with ExitStack() as ctx:
        sb, ps, sem = scoped(nc, ctx, "scan", reused=True)
        RING = 4
        STEPS = STATE * KC
        bbc = sb("bbc", [P, RING, NB])
        dbx = sb("dbx", [P, 2 * KC, NB])
        HRING = 4
        h = sb("h", [P, HRING, NB])
        hc = sb("hc", [P, 2, NB])
        da = ps("da", [P, 2, NB])
        cbc = ps("cbc", [P, 2, NB])
        y = ps("y", [P, KC, NB])
        b_in = [sem(f"b_in{k}") for k in range(RING)]
        dbx_ready, dbx_0 = sem("dbx_ready"), STATE
        h_ready, h_0 = sem("h_ready"), 2 * KC
        hc_ready, hc_0 = sem("hc_ready"), 2 * KC
        y_used_hc, y_used_0 = sem("y_used_hc"), 2
        y_read = sem("y_read")
        da_ready, c_ready = sem("da_ready"), sem("c_ready")
        block = ctx.enter_context(nc.Block())

        @block.sync
        def _(sp):
            with sp.Fori(0, BATCH) as b:
                for n in range(STATE):
                    sp.wait_ge(dbx_ready, b * STEPS + KC * (n - RING + 1) + dbx_0)
                    sp.dma_start(bbc[:, n % RING, :], g.brow_dram[n, b].partition_broadcast(P)).then_inc(b_in[n % RING], 16)

        @block.gpsimd
        def _(pool):
            pool.sem_inc(dbx_ready, dbx_0)
            with pool.Fori(0, BATCH) as b:
                for n in range(STATE):
                    pool.wait_ge(b_in[n % RING], b * (16 * STATE // RING) + 16 * (n // RING + 1))
                    wait_apart(pool, h_ready, b * STEPS + KC * (n - 1) + h_0)
                    for c in range(KC):
                        i = n * KC + c
                        nc.gpsimd.tensor_tensor(dbx[:, i % (2 * KC), :], g.U[:, c, bass.ts(b, NB)], bbc[:, n % RING, :],
                                                ALU.mult).then_inc(dbx_ready, 1)

        @block.scalar
        def _(act):
            with act.Fori(0, BATCH) as b:
                for n in range(STATE):
                    for c in range(KC):
                        i = n * KC + c
                        wait_apart(act, h_ready, b * STEPS + i - 1 + h_0)
                        nc.scalar.activation(da[:, i % 2, :], g.DT[:, c, bass.ts(b, NB)], ACT.Exp,
                                             scale=g.A[:, c, n:n + 1]).then_inc(da_ready, 1)

        @block.vector
        def _(dve):
            dve.sem_inc(h_ready, h_0)
            dve.sem_inc(hc_ready, hc_0)
            dve.sem_inc(y_read, KC)

            def weigh(b, i):
                dve.wait_ge(h_ready, b * STEPS + i + 1 + h_0)
                dve.wait_ge(c_ready, b * STATE + i // KC + 1)
                dve.wait_ge(y_used_hc, b * STEPS + i - 1 + y_used_0)
                nc.vector.tensor_tensor(hc[:, i % 2, :], cbc[:, (i // KC) % 2, :], h[:, i % HRING, :],
                                        ALU.mult).then_inc(hc_ready, 1)

            with dve.Fori(0, BATCH) as b:
                for i in range(STEPS):
                    dve.wait_ge(da_ready, b * STEPS + i + 1)
                    dve.wait_ge(dbx_ready, b * STEPS + i + 1 + dbx_0)
                    dve.wait_ge(hc_ready, b * STEPS + i - HRING + 1 + hc_0)
                    nc.vector.tensor_tensor_scan(h[:, i % HRING, :], da[:, i % 2, :], dbx[:, i % (2 * KC), :], 0.0,
                                                 ALU.mult, ALU.add).then_inc(h_ready, 1)
                    if i:
                        weigh(b, i - 1)
                weigh(b, STEPS - 1)
                for c in range(KC):
                    dve.wait_ge(y_used_hc, b * STEPS + STEPS - KC + c + 1 + y_used_0)
                    xs = g.XT[:, c, bass.ts(b, NB)]
                    nc.vector.scalar_tensor_tensor(out=xs, in0=xs, scalar=g.D1[:, c:c + 1], in1=y[:, c, :],
                                                   op0=ALU.mult, op1=ALU.add).then_inc(y_read, 1)

        @block.tensor
        def _(pe):
            pe.sem_inc(y_used_hc, y_used_0)
            with pe.Fori(0, BATCH) as b:
                for n in range(STATE + 1):
                    if n < STATE:
                        wait_apart(pe, hc_ready, b * STEPS + KC * (n - 1) + hc_0)
                        pe.matmul(cbc[:, n % 2, :], g.sel[:, n, :], g.CT[:, bass.ts(b, NB)], start=True,
                                  stop=True).then_inc(c_ready, 1)
                    if n == 0:
                        continue
                    for c in range(KC):
                        m = n - 1
                        i = m * KC + c
                        if m == 0:
                            pe.wait_ge(y_read, b * KC + c + 1)
                        pe.wait_ge(hc_ready, b * STEPS + i + 1 + hc_0)
                        mm = pe.matmul(y[:, c, :], g.ident[:], hc[:, i % 2, :], start=(m == 0), stop=(m == STATE - 1))
                        mm.then_inc(y_used_hc, 1)


def normalise(nc, g, tag, by_feature, out=None, quantise=False, gather=False, ahead=None):
    with ExitStack() as ctx:
        sb, ps, sem = scoped(nc, ctx, tag, reused=by_feature)
        stats = sb("stats", [P, TILES, 6])
        mv = sb("mv", [P, TILES, 2])
        std = sb("std", [P, TILES])
        rstd = sb("rstd", [P, TILES])
        eps = sb("eps", [P, 1])
        if quantise:
            amax, scale, inv = (sb(n, [P, TILES, KC]) for n in ("amax", "scale", "inv"))
            xq = sb("xq", [P, 2, DIM])
        RING = 4
        pr = [ps(f"pr{k}", [P, DIM]) for k in range(RING)] if by_feature else None
        pt = [ps(f"pt{k}", [P, KC, P]) for k in range(2)] if out is None else None
        x_ready = sem("x_ready")
        if by_feature:
            turned = sem("turned")
        if gather:
            GRING = 4
            rows = sb("rows", [P, GRING, TOP, DIM])
            gathered = [sem(f"gathered{k}") for k in range(GRING)]
        if out is None:
            x_turned, hi_ready, lo_ready = sem("x_turned"), sem("hi_ready"), sem("lo_ready")
        else:
            stored = sem("stored")
        var_ready, std_ready, eps_ready = sem("var_ready"), sem("std_ready"), sem("eps_ready")
        if quantise:
            xq_ready, y_copied, inv_ready = sem("xq_ready"), sem("y_copied"), sem("inv_ready")
            amax_ready, scale_ready = sem("amax_ready"), sem("scale_ready")
        if gather:
            added = sem("added")
        stats_ready, rstd_ready = sem("stats_ready"), sem("rstd_ready")
        LAG = 3 if quantise else 2
        block = ctx.enter_context(nc.Block())

        if gather:
            @block.gpsimd
            def _(pool):
                for t in range(TILES):
                    if t >= GRING:
                        pool.wait_ge(added, TOP * (t - GRING + 1))
                    for k in range(TOP):
                        nc.gpsimd.indirect_dma_start(rows[:, t % GRING, k, :], None, g.sorted_y,
                                                     bass.IndirectOffsetOnAxis(g.at[:, k, t:t + 1], 0)
                                                     ).then_inc(gathered[t % GRING], 16)
                ahead[1](pool)
        elif ahead:
            @block.gpsimd
            def _(pool):
                ahead[1](pool)

        @block.tensor
        def _(pe):
            def turn_in(t):
                if t >= RING:
                    pe.wait_ge(x_ready, t - RING + 1)
                for c in range(KC):
                    mm = pe.transpose(pr[t % RING][:, c * P:(c + 1) * P], g.XT[:, c, t * P:(t + 1) * P], g.ident[:])
                mm.then_inc(turned, 1)

            if by_feature:
                for t in range(RING - 1):
                    turn_in(t)
            for t in range(TILES + 1):
                if by_feature and 0 < t <= TILES - RING + 1:
                    turn_in(t + RING - 2)
                if t and out is None:
                    m = t - 1
                    pe.wait_ge(xq_ready if quantise else x_ready, KC * (m + 1) if quantise else m + 1)
                    if m >= 2:
                        pe.wait_ge(lo_ready, m - 1)
                    for c in range(KC):
                        cols = slice(c * P, (c + 1) * P)
                        mm = pe.transpose(pt[m % 2][:, c, :], xq[:, m % 2, cols] if quantise else g.X[:, m, cols],
                                          g.ident[:])
                    mm.then_inc(x_turned, 1)

        @block.vector
        def _(dve):
            nc.vector.memset(eps[:], EPS).then_inc(eps_ready, 1)

            def source(t):
                return pr[t % RING][:] if by_feature else g.Y[:, t, :]

            def low_part(m):
                dve.wait_ge(hi_ready, m + 1)
                cols = slice(m * P, (m + 1) * P)
                nc.vector.tensor_tensor(g.XL[:, :, cols], pt[m % 2][:], g.XH[:, :, cols].bitcast(F32),
                                        ALU.subtract).then_inc(lo_ready, 1)

            def largest(m):
                dve.wait_ge(x_ready, m + 1)
                nc.vector.tensor_reduce(amax[:, m, :], g.X[:, m, :].rearrange("p (c k) -> p c k", k=P), AX.X,
                                        ALU.max, apply_absolute_value=True).then_inc(amax_ready, 1)

            def block_scale(m):
                dve.wait_ge(amax_ready, m + 1)
                nc.vector.tensor_scalar(scale[:, m, :], amax[:, m, :], 1.0 / FP8_MAX, 1e-12, ALU.mult,
                                        ALU.add).then_inc(scale_ready, 1)

            def inverse(m):
                dve.wait_ge(scale_ready, m + 1)
                nc.vector.reciprocal(inv[:, m, :], scale[:, m, :]).then_inc(inv_ready, 1)

            def quantised(m):
                dve.wait_ge(inv_ready, m + 1)
                if m >= 2:
                    dve.wait_ge(x_turned, m - 1)
                for c in range(KC):
                    cols = slice(c * P, (c + 1) * P)
                    nc.vector.tensor_scalar(xq[:, m % 2, cols], g.X[:, m, cols], inv[:, m, c:c + 1],
                                            scale[:, m, c:c + 1], ALU.mult, ALU.mult).then_inc(xq_ready, 1)

            def add_row(t, k):
                if k == 0:
                    dve.wait_ge(gathered[t % GRING], 16 * TOP * (t // GRING + 1))
                else:
                    dve.wait_ge(added, TOP * t + k)
                nc.vector.scalar_tensor_tensor(out=g.Y[:, t, :], in0=rows[:, t % GRING, k, :],
                                               scalar=g.weight[:, k, t:t + 1], in1=g.Y[:, t, :],
                                               op0=ALU.mult, op1=ALU.add).then_inc(added, 1)

            def stats_of(t):
                if by_feature:
                    dve.wait_ge(turned, t + 1)
                if gather:
                    dve.wait_ge(added, TOP * (t + 1))
                nc.vector.bn_stats(stats[:, t, :], source(t)).then_inc(stats_ready, 1)

            def variance(t):
                dve.wait_ge(stats_ready, t + 1)
                nc.vector.bn_aggr(mv[:, t, :], stats[:, t, :]).then_inc(var_ready, 1)

            def inverse_std(m):
                dve.wait_ge(std_ready, m + 1)
                nc.vector.reciprocal(rstd[:, m:m + 1], std[:, m:m + 1]).then_inc(rstd_ready, 1)

            def centre(m):
                dve.wait_ge(rstd_ready, m + 1)
                nc.vector.tensor_scalar(g.X[:, m, :], source(m), mv[:, m, 0:1], rstd[:, m:m + 1], ALU.subtract,
                                        ALU.mult).then_inc(x_ready, 1)

            stages = [(0, stats_of), (1, inverse_std), (0, variance), (1, centre)]
            if gather:
                stages = [(0, lambda t: add_row(t, 0)), (1, inverse_std), (1, centre), (0, lambda t: add_row(t, 1)),
                          (0, stats_of), (LAG, low_part), (0, variance)]
            elif quantise:
                stages = [(0, stats_of), (2, block_scale), (1, inverse_std), (0, variance), (2, inverse), (1, centre),
                          (2, quantised), (1, largest), (LAG, low_part)]
            elif out is None:
                stages.append((LAG, low_part))
            for t in range(TILES + LAG):
                for lag, stage in stages:
                    if 0 <= t - lag < TILES:
                        stage(t - lag)

        @block.scalar
        def _(act):
            act.wait_ge(eps_ready, 1)
            for t in range(TILES + LAG):
                if t >= LAG and out is None:
                    m = t - LAG
                    act.wait_ge(x_turned, m + 1)
                    nc.scalar.activation(g.XH[:, :, m * P:(m + 1) * P], pt[m % 2][:], ACT.Copy).then_inc(hi_ready, 1)
                if t < TILES:
                    act.wait_ge(var_ready, t + 1)
                    nc.scalar.activation(std[:, t:t + 1], mv[:, t, 1:2], ACT.Sqrt, bias=eps[:, 0:1]).then_inc(std_ready, 1)
                if quantise and 1 <= t <= TILES:
                    act.wait_ge(x_ready, t)
                    nc.scalar.activation(g.Y[:, t - 1, :], g.X[:, t - 1, :], ACT.Copy).then_inc(y_copied, 1)

        @block.sync
        def _(sp):
            if ahead:
                ahead[0](sp)
            if out is not None:
                rows = out.rearrange("(t p) d -> p t d", p=P)
                for t in range(0, TILES, 2):
                    sp.wait_ge(x_ready, t + 2)
                    sp.dma_start(rows[:, t:t + 2, :], g.X[:, t:t + 2, :]).then_inc(stored, 16)
                sp.wait_ge(stored, 16 * TILES // 2)


def route_and_share(nc, a, g):
    with ExitStack() as ctx:
        sb, ps, sem = scoped(nc, ctx, "route", reused=True)
        QUARTER = P // BLOCKS
        rpad = sb("rpad", [P, KC, QUARTER])
        lgT = sb("lgT", [P, NB])
        rb = sb("rb", [P, EXPERTS])
        rbias = sb("rbias", [P, EXPERTS])
        order = sb("order", [P, EXPERTS])
        b3 = sb("b3", [P, DIM])
        taken = 0

        def spare(shape):
            nonlocal taken
            n = int(np.prod(shape[1:]))
            flat = g.sums[0:shape[0], taken:taken + n]
            taken += n
            names = [f"a{k}" for k in range(len(shape) - 1)]
            return flat.rearrange(f"p ({' '.join(names)}) -> p {' '.join(names)}", **dict(zip(names, shape[1:])))

        full = [P, TILES, EXPERTS]
        grouped = [P, TILES, GROUPS]
        lg, lg2, ex, pr_, sc = (spare(full) for _ in ("lg", "lg2", "ex", "pr", "sc"))
        ms, ms2, ms3, eq, key, e1, e2, esum = (spare(full) for _ in ("ms", "ms2", "ms3", "eq", "key", "e1", "e2", "es"))
        gm, gm2, geq, gkey, g1, g2, keep, low = (spare(grouped) for _ in
                                                 ("gm", "gm2", "geq", "gkey", "g1", "g2", "keep", "low"))
        one, two, three_ = (sb(n, [P, TILES]) for n in ("one", "two", "three"))
        gT = sb("gT", [P, TOK])
        upper, ones = sb("upper", [P, P]), sb("ones", [P, P])
        steps, before, tile_no = spare([P, TILES]), spare([P, EXPERTS, EXPERTS]), spare([P, SORTED])
        held, start, end = (sb(n, [P, EXPERTS]) for n in ("held", "start", "end"))
        by_expert = [P, EXPERTS, TILES]
        inner, until, at_row = spare(by_expert), spare(by_expert), spare(by_expert)
        over, early = spare([P, EXPERTS, TILES]), spare([P, EXPERTS, EXPERTS])
        past, owner = spare([1, SORTED, EXPERTS]), spare([1, SORTED])
        place, chosen = spare(full), spare(full)
        at = spare([P, TOP, TILES])
        silu = sb("silu", [P, 2, NB])
        h = sb("h", [P, 2, NB])
        hh = sb("hh", [P, 2, NB], F32R)
        hl = sb("hl", [P, 2, NB], F32R)
        pg = [ps(f"pg{k}", [P, NB]) for k in range(2)]
        pu = [ps(f"pu{k}", [P, NB]) for k in range(2)]
        py = [ps(f"py{k}", [P, DIM]) for k in range(PER_BLOCK)]
        plT, pl = py[0][:], py[1][:].rearrange("p (t b e) -> p t b e", b=BLOCKS, e=QUARTER)
        rank, total = (py[2][:, k * EXPERTS * TILES:(k + 1) * EXPERTS * TILES].rearrange("p (e t) -> p e t", t=TILES)
                       for k in range(2))
        loaded, consts, pads = sem("loaded"), sem("consts"), sem("pads")
        logits_T, copied_T, logits, exped = sem("logits_T"), sem("copied_T"), sem("logits"), sem("exped")
        picked, ranked, gated, placed = sem("picked"), sem("ranked"), sem("gated"), sem("placed")
        turned, gate_ready, dve_chain, scattered = sem("turned"), sem("gate_ready"), sem("dve_chain"), sem("scattered")
        g_ready, u_ready, s_ready, hh_ready = sem("g_ready"), sem("u_ready"), sem("s_ready"), sem("hh_ready")
        h_ready, hl_ready, y_ready, y_added = sem("h_ready"), sem("hl_ready"), sem("y_ready"), sem("y_added")
        STEPS = 2 * BLOCKS
        block = ctx.enter_context(nc.Block())

        @block.sync
        def _(sp):
            sp.wait_ge(pads, 2)
            sp.dma_start(rpad[:, :, 0:EXPERTS], a["router_w"].rearrange("(c p) e -> p c e", p=P)).then_inc(loaded, 16)
            sp.dma_start(rb[:], a["router_b"].partition_broadcast(P)).then_inc(loaded, 16)
            sp.dma_start(rbias[:], a["router_bias"].partition_broadcast(P)).then_inc(loaded, 16)
            sp.dma_start(order[:], a["order"].partition_broadcast(P)).then_inc(loaded, 16)
            sp.dma_start(b3[0:MLPS, :], a["b3"]).then_inc(loaded, 16)
            sp.dma_start(inner[:], a["inner"].partition_broadcast(P)).then_inc(loaded, 16)
            sp.dma_start(steps[:], a["steps"].partition_broadcast(P)).then_inc(loaded, 16)
            sp.dma_start(before[:], a["before"].partition_broadcast(P)).then_inc(loaded, 16)
            sp.dma_start(tile_no[:], a["tile_no"].partition_broadcast(P)).then_inc(loaded, 16)
            for s in range(2):
                sp.dma_start(g.raw[s][:], a["w123"][EXPERTS + s]).then_inc(g.shared_in[s], 16)

        @block.gpsimd
        def _(pool):
            nc.gpsimd.memset(rpad[:], 0.0).then_inc(pads, 1)
            nc.gpsimd.memset(b3[:], 0.0).then_inc(pads, 1)
            nc.gpsimd.memset(ones[:], 1.0).then_inc(consts, 1)
            pool.wait_ge(consts, 1)
            nc.gpsimd.affine_select(out=upper[:], in_=ones[:], compare_op=ALU.is_gt, fill=0.0, base=0,
                                    pattern=[[1, P]], channel_multiplier=-1).then_inc(consts, 1)
            for s in range(2):
                pool.wait_ge(g.shared_in[s], 16)
                nc.gpsimd.tensor_scalar(g.wh[s][:], g.raw[s][:, 0:WN], 1.0, 0.0, ALU.mult, ALU.add).then_inc(consts, 1)
                pool.wait_ge(consts, 3 + s)
                nc.gpsimd.tensor_tensor(g.wl[s][:], g.raw[s][:, 0:WN], g.wh[s][:].bitcast(F32),
                                        ALU.subtract).then_inc(g.shared_split, 1)
            nc.gpsimd.memset(gT[:], 0.0).then_inc(pads, 1)
            pool.wait_ge(placed, 1)
            for t in range(TILES):
                for k in range(TOP):
                    nc.gpsimd.indirect_dma_start(g.sorted_x, bass.IndirectOffsetOnAxis(g.at[:, k, t:t + 1], 0),
                                                 g.X[:, t, :], None).then_inc(scattered, 16)
            pool.wait_ge(scattered, 16 * TOP * TILES)

        @block.tensor
        def _(pe):
            def up(q):
                e, tb = q // BLOCKS, q % BLOCKS
                cols = slice(tb * NB, (tb + 1) * NB)
                pe.wait_ge(g.shared_split, e + 1)
                if q >= 2:
                    pe.wait_ge(h_ready, q - 1)
                for out, at, ready in ((pg, 0, g_ready), (pu, KC * INTER, u_ready)):
                    for c in range(KC):
                        w = slice(at + c * INTER, at + (c + 1) * INTER)
                        mm = three(pe, out[q % 2][:], g.wh[e][:, w], g.wl[e][:, w], g.XH[:, c, cols],
                                   g.XL[:, c, cols], c == 0, c == KC - 1)
                    mm.then_inc(ready, 1)

            def down(q):
                e = q // BLOCKS
                pe.wait_ge(hl_ready, q + 1)
                for j in range(PER_BLOCK):
                    cols = slice(j * P, (j + 1) * P)
                    if q:
                        pe.wait_ge(y_added, PER_BLOCK * (q - 1) + j + 1)
                    if e == 0:
                        t = PER_BLOCK * q + j
                        pe.matmul(py[j][:], gT[:, t * P:(t + 1) * P], b3[:], start=True, stop=False)
                    three(pe, py[j][:], hh[:, q % 2, cols], hl[:, q % 2, cols], g.wh[e][:, WUP:], g.wl[e][:, WUP:],
                          e == 1, True).then_inc(y_ready, 1)

            pe.wait_ge(loaded, 144)
            for n in range(2 * KC):
                c, x = n // 2, (g.XH, g.XL)[n % 2]
                for b in range(BLOCKS):
                    mm = pe.matmul(plT[b * QUARTER:(b + 1) * QUARTER, :], rpad[:, c, :],
                                   x[:, c, b * NB:(b + 1) * NB].bitcast(F32), start=(n == 0), stop=(n == 2 * KC - 1))
            mm.then_inc(logits_T, 1)
            up(0)
            pe.wait_ge(copied_T, 1)
            for j in range(PER_BLOCK):
                mm = pe.transpose(py[1][:, j * P:(j + 1) * P], lgT[:, j * P:(j + 1) * P], g.ident[:])
            mm.then_inc(logits, 1)
            up(1)
            pe.wait_ge(consts, 2)
            pe.wait_ge(picked, 1)
            pe.matmul(rank, upper[:], esum[:].rearrange("p t e -> p e t"), start=True, stop=True)
            pe.matmul(total, ones[:], esum[:].rearrange("p t e -> p e t"), start=True, stop=True).then_inc(ranked, 1)
            pe.wait_ge(gated, 1)
            for b in range(BLOCKS):
                if b == 2:
                    pe.wait_ge(placed, 1)
                for j in range(PER_BLOCK):
                    t = b * PER_BLOCK + j
                    mm = pe.transpose(py[b][0:MLPS, j * P:(j + 1) * P], g.gate[:, :, t], g.ident[:])
                mm.then_inc(turned, 1)
            pe.wait_ge(gate_ready, BLOCKS)
            for q in range(STEPS):
                if q >= 2:
                    up(q)
                if q:
                    down(q - 1)
            down(STEPS - 1)

        @block.scalar
        def _(act):
            act.wait_ge(logits_T, 1)
            nc.scalar.activation(lgT[:], plT, ACT.Copy).then_inc(copied_T, 1)
            act.wait_ge(dve_chain, 1 + BLOCKS + 2)
            nc.scalar.activation(ex[:], lg2[:], ACT.Exp).then_inc(exped, 1)
            act.wait_ge(pads, 3)
            for b in range(BLOCKS):
                act.wait_ge(turned, b + 1)
                nc.scalar.activation(gT[0:MLPS, b * NB:(b + 1) * NB], py[b][0:MLPS, :], ACT.Copy).then_inc(gate_ready, 1)
            for q in range(STEPS):
                act.wait_ge(g_ready, q + 1)
                if q >= 2:
                    act.wait_ge(h_ready, q - 1)
                nc.scalar.activation(silu[:, q % 2, :], pg[q % 2][:], ACT.Silu,
                                     bias=g.raw[q // BLOCKS][:, WN:WN + 1]).then_inc(s_ready, 1)
                act.wait_ge(h_ready, q + 1)
                if q >= 2:
                    act.wait_ge(y_ready, PER_BLOCK * (q - 1))
                nc.scalar.activation(hh[:, q % 2, :], h[:, q % 2, :], ACT.Copy).then_inc(hh_ready, 1)

        @block.vector
        def _(dve):
            own = Chain(dve, dve_chain)

            def along(x, n):
                return x.unsqueeze(2).to_broadcast([P, TILES, n])

            def do(ins):
                own.step(ins)
                own.settle()

            def pick(sel, v, n, eq_, key_):
                do(nc.vector.tensor_reduce(one[:], v, AX.X, ALU.max))
                do(nc.vector.tensor_tensor(eq_, v, along(one[:], n), ALU.is_equal))
                do(nc.vector.tensor_tensor(key_, eq_, order[:, 0:n].unsqueeze(1).to_broadcast([P, TILES, n]), ALU.mult))
                do(nc.vector.tensor_reduce(two[:], key_, AX.X, ALU.max))
                do(nc.vector.tensor_tensor(sel, key_, along(two[:], n), ALU.is_equal))

            def by_group(x):
                return x[:].rearrange("p t (g k) -> p (t g) k", g=GROUPS)

            def per_group(x):
                return x[:].rearrange("p t g -> p (t g)").unsqueeze(2).to_broadcast([P, TILES * GROUPS, EXPERTS // GROUPS])

            dve.wait_ge(loaded, 144)
            own.step(nc.vector.memset(g.gate[:, EXPERTS:MLPS, :], 1.0))
            dve.wait_ge(logits, 1)
            for b in range(BLOCKS):
                ins = nc.vector.tensor_tensor(lg[:, b * PER_BLOCK:(b + 1) * PER_BLOCK, :], pl[:, :, b, 0:EXPERTS],
                                              rb[:].unsqueeze(1).to_broadcast([P, PER_BLOCK, EXPERTS]), ALU.add)
                if b < BLOCKS - 1:
                    own.step(ins)
            do(ins)
            do(nc.vector.tensor_reduce(three_[:], lg[:], AX.X, ALU.max))
            do(nc.vector.tensor_tensor(lg2[:], lg[:], along(three_[:], EXPERTS), ALU.subtract))
            dve.wait_ge(exped, 1)
            do(nc.vector.tensor_reduce(one[:], ex[:], AX.X, ALU.add))
            do(nc.vector.reciprocal(two[:], one[:]))
            do(nc.vector.tensor_tensor(pr_[:], ex[:], along(two[:], EXPERTS), ALU.mult))
            do(nc.vector.tensor_tensor(sc[:], pr_[:], rbias[:].unsqueeze(1).to_broadcast(full), ALU.add))
            do(nc.vector.tensor_reduce(gm[:].rearrange("p t g -> p (t g)"), by_group(sc), AX.X, ALU.max))
            pick(g1[:], gm[:], GROUPS, geq[:], gkey[:])
            do(nc.vector.scalar_tensor_tensor(out=gm2[:], in0=g1[:], scalar=-BIG, in1=gm[:], op0=ALU.mult, op1=ALU.add))
            pick(g2[:], gm2[:], GROUPS, geq[:], gkey[:])
            do(nc.vector.tensor_tensor(keep[:], g1[:], g2[:], ALU.add))
            do(nc.vector.tensor_scalar(low[:], keep[:], -1.0, BIG, ALU.add, ALU.mult))
            do(nc.vector.tensor_tensor(by_group(ms), by_group(sc), per_group(keep), ALU.mult))
            do(nc.vector.tensor_tensor(by_group(ms2), by_group(ms), per_group(low), ALU.add))
            pick(e1[:], ms2[:], EXPERTS, eq[:], key[:])
            do(nc.vector.scalar_tensor_tensor(out=ms3[:], in0=e1[:], scalar=-BIG / 2, in1=ms2[:], op0=ALU.mult,
                                              op1=ALU.add))
            do(nc.vector.tensor_scalar(ms3[:], ms3[:], -BIG, None, ALU.max))
            pick(e2[:], ms3[:], EXPERTS, eq[:], key[:])
            nc.vector.tensor_tensor(esum[:], e1[:], e2[:], ALU.add).then_inc(picked, 1)
            dve.wait_ge(picked, 1)
            nc.vector.tensor_tensor(g.gate[:, 0:EXPERTS, :].rearrange("p e t -> p t e"), esum[:], sc[:],
                                    ALU.mult).then_inc(gated, 1)
            for k, e in enumerate((e1, e2)):
                do(nc.vector.tensor_tensor(chosen[:], e[:], sc[:], ALU.mult))
                do(nc.vector.tensor_reduce(g.weight[:, k, :], chosen[:], AX.X, ALU.add))
            dve.wait_ge(ranked, 1)
            do(nc.vector.tensor_tensor_scan(until[:].rearrange("p e t -> p (e t)"), inner[:].rearrange("p e t -> p (e t)"),
                                            total.rearrange("p e t -> p (e t)"), 0.0, ALU.mult, ALU.add))
            do(nc.vector.tensor_tensor(at_row[:], until[:], total, ALU.subtract))
            do(nc.vector.tensor_tensor(at_row[:], at_row[:], rank, ALU.add))
            do(nc.vector.tensor_tensor(over[:], until[:, :, TILES - 1].unsqueeze(2).to_broadcast([P, EXPERTS, TILES]),
                                       steps[:].unsqueeze(1).to_broadcast([P, EXPERTS, TILES]), ALU.is_gt))
            do(nc.vector.tensor_reduce(held[:], over[:], AX.X, ALU.add))
            do(nc.vector.tensor_tensor(early[:], before[:], held[:].unsqueeze(1).to_broadcast([P, EXPERTS, EXPERTS]),
                                       ALU.mult))
            do(nc.vector.tensor_reduce(start[:], early[:], AX.X, ALU.add))
            do(nc.vector.tensor_tensor(end[:], start[:], held[:], ALU.add))
            do(nc.vector.tensor_scalar(start[:], start[:], float(P), None, ALU.mult))
            do(nc.vector.tensor_tensor(place[:], at_row[:].rearrange("p e t -> p t e"), start[:].unsqueeze(1).to_broadcast(full), ALU.add))
            for k, e in enumerate((e1, e2)):
                do(nc.vector.tensor_tensor(chosen[:], e[:], place[:], ALU.mult))
                do(nc.vector.tensor_reduce(at[:, k, :], chosen[:], AX.X, ALU.add))
            own.settle()
            nc.vector.tensor_copy(g.at[:], at[:]).then_inc(placed, 1)
            do(nc.vector.tensor_tensor(past[:], end[0:1].unsqueeze(1).to_broadcast([1, SORTED, EXPERTS]),
                                       tile_no[0:1].unsqueeze(2).to_broadcast([1, SORTED, EXPERTS]), ALU.is_le))
            do(nc.vector.tensor_reduce(owner[:], past[:], AX.X, ALU.add))
            do(nc.vector.tensor_scalar(g.owner[:], owner[:], EXPERTS - 1.0, None, ALU.min))

            def hidden(q):
                dve.wait_ge(u_ready, q + 1)
                dve.wait_ge(s_ready, q + 1)
                if q >= 2:
                    dve.wait_ge(hl_ready, q - 1)
                nc.vector.scalar_tensor_tensor(out=h[:, q % 2, :], in0=pu[q % 2][:], scalar=g.raw[q // BLOCKS][:, WN + 1:WN + 2],
                                               in1=silu[:, q % 2, :], op0=ALU.add, op1=ALU.mult).then_inc(h_ready, 1)
                dve.wait_ge(hh_ready, q + 1)
                nc.vector.tensor_tensor(hl[:, q % 2, :], h[:, q % 2, :], hh[:, q % 2, :].bitcast(F32),
                                        ALU.subtract).then_inc(hl_ready, 1)

            def add(q):
                for j in range(PER_BLOCK):
                    t = PER_BLOCK * (q % BLOCKS) + j
                    dve.wait_ge(y_ready, PER_BLOCK * q + j + 1)
                    if q >= BLOCKS:
                        dve.wait_ge(y_added, PER_BLOCK * (q - BLOCKS) + j + 1)
                    base = g.X if q < BLOCKS else g.Y
                    nc.vector.tensor_tensor(g.Y[:, t, :], py[j][:], base[:, t, :], ALU.add).then_inc(y_added, 1)

            for q in range(STEPS):
                hidden(q)
                if q:
                    add(q - 1)
            add(STEPS - 1)


def sorted_experts(nc, a, g):
    with ExitStack() as ctx:
        sb, ps, sem = scoped(nc, ctx, "exp", reused=True)
        raw = g.raw + [sb(f"raw{k}", [P, WN + 2]) for k in range(2, TURN)]
        x = [sb(f"x{k}", [P, DIM]) for k in range(TURN)]
        xh = [sb(f"xh{k}", [P, KC, P], F32R) for k in range(2)]
        xl = [sb(f"xl{k}", [P, KC, P], F32R) for k in range(2)]
        silu, h = ([sb(f"{n}{k}", [P, P]) for k in range(2)] for n in ("silu", "h"))
        hh, hl = ([sb(f"{n}{k}", [P, P], F32R) for k in range(2)] for n in ("hh", "hl"))
        y = [sb(f"y{k}", [P, DIM]) for k in range(2)]
        pt = [ps(f"pt{k}", [P, KC, P]) for k in range(2)]
        pgu = [[ps(f"p{n}{k}", [P, NB]) for n in "gu"] for k in range(2)]
        py = [ps(f"py{k}", [P, DIM]) for k in range(2)]
        x_in, w_in = [sem(f"x_in{k}") for k in range(TURN)], [sem(f"w_in{k}") for k in range(TURN)]
        up_hi, down_hi, xh_ready, g_ready = sem("up_hi"), sem("down_hi"), sem("xh_ready"), sem("g_ready")
        s_ready, hh_ready, hl_ready = sem("s_ready"), sem("hh_ready"), sem("hl_ready")
        y_stored = [sem(f"y_stored{k}") for k in range(2)]
        x_turned, xl_ready, u_ready, h_ready = sem("x_turned"), sem("xl_ready"), sem("u_ready"), sem("h_ready")
        up_lo, down_lo, y_ready, y_copied = sem("up_lo"), sem("down_lo"), sem("y_ready"), sem("y_copied")
        AHEAD = TURN
        block = ctx.enter_context(nc.Block())

        def steps(eng, stages):
            for n in range(TURN):
                for lag, do in stages:
                    if n >= lag:
                        do(n - lag, n - lag)
            with eng.Fori(1, SORTED // TURN) as i:
                for n in range(TURN):
                    for lag, do in stages:
                        do(i * TURN + (n - lag), (n - lag) % TURN)
            for n in range(max(lag for lag, _ in stages)):
                for lag, do in stages:
                    if n < lag:
                        do(SORTED + n - lag, (n - lag) % TURN)

        @block.sync
        def _(sp):
            def load_x(j, s):
                sp.wait_ge(x_turned, j - TURN + 1 + AHEAD)
                sp.dma_start(x[s][:].unsqueeze(1), g.sorted_x.rearrange("(t p) d -> p t d", p=P)[:, bass.ds(j, 1), :]
                             ).then_inc(x_in[s], 16)

            def load_w(j, s):
                sp.wait_ge(up_lo, j - TURN + 1 + AHEAD)
                sp.wait_ge(down_lo, j - TURN + 1 + AHEAD)
                sp.wait_ge(h_ready, j - TURN + 1 + AHEAD)
                e = nc.values_load(g.owner[0:1, bass.ds(j, 1)], engines=(mybir.EngineType.SP,), min_val=0,
                                   max_val=EXPERTS - 1)
                sp.dma_start(raw[s][:].unsqueeze(1), a["w123"][bass.ds(e, 1)].rearrange("e p w -> p e w")
                             ).then_inc(w_in[s], 16)

            def store_y(j, s):
                sp.wait_ge(y_copied, j + 1 + AHEAD)
                sp.dma_start(g.sorted_y.rearrange("(t p) d -> p t d", p=P)[:, bass.ds(j, 1), :], y[s % 2][:].unsqueeze(1)
                             ).then_inc(y_stored[s % 2], 16)

            for k in range(2):
                sp.sem_inc(y_stored[k], 16)
            steps(sp, [(0, load_x), (0, load_w), (TURN, store_y)])
            for k in range(2):
                sp.wait_ge(y_stored[k], 16 * SORTED // 2 + 16)

        @block.gpsimd
        def _(pool):
            pool.sem_inc(down_lo, AHEAD)

            def up_weights_hi(j, s):
                pool.wait_ge(w_in[s], (j - s) * (16 // TURN) + 16)
                wait_apart(pool, u_ready, j - 1 + AHEAD)
                nc.gpsimd.tensor_scalar(g.wh[s % 2][:, 0:WUP], raw[s][:, 0:WUP], 1.0, 0.0, ALU.mult,
                                        ALU.add).then_inc(up_hi, 1)

            def down_weights_lo(j, s):
                pool.wait_ge(down_hi, j + 1)
                wait_apart(pool, y_ready, j - 1 + AHEAD)
                nc.gpsimd.tensor_tensor(g.wl[s % 2][:, WUP:WN], raw[s][:, WUP:WN], g.wh[s % 2][:, WUP:WN].bitcast(F32),
                                        ALU.subtract).then_inc(down_lo, 1)

            steps(pool, [(0, up_weights_hi), (1, down_weights_lo)])

        @block.tensor
        def _(pe):
            pe.sem_inc(x_turned, AHEAD)
            pe.sem_inc(u_ready, AHEAD)
            pe.sem_inc(y_ready, AHEAD)

            def turn(j, s):
                pe.wait_ge(x_in[s], (j - s) * (16 // TURN) + 16)
                pe.wait_ge(xl_ready, j - 1 + AHEAD)
                for c in range(KC):
                    mm = pe.transpose(pt[s % 2][:, c, :], x[s][:, c * P:(c + 1) * P], g.ident[:])
                mm.then_inc(x_turned, 1)

            def up(j, s):
                k = s % 2
                pe.wait_ge(xl_ready, j + 1 + AHEAD)
                pe.wait_ge(up_lo, j + 1 + AHEAD)
                pe.wait_ge(h_ready, j - 1 + AHEAD)
                for n, ready in ((0, g_ready), (1, u_ready)):
                    for c in range(KC):
                        w = slice((n * KC + c) * INTER, (n * KC + c + 1) * INTER)
                        mm = three(pe, pgu[k][n][:, 0:P], g.wh[k][:, w], g.wl[k][:, w], xh[k][:, c, :], xl[k][:, c, :],
                                   c == 0, c == KC - 1)
                    mm.then_inc(ready, 1)

            def down(j, s):
                k = s % 2
                pe.wait_ge(hl_ready, j + 1)
                pe.wait_ge(down_lo, j + 1 + AHEAD)
                pe.wait_ge(y_copied, j - 1 + AHEAD)
                three(pe, py[k][:], hh[k][:], hl[k][:], g.wh[k][:, WUP:WN], g.wl[k][:, WUP:WN], True,
                      True).then_inc(y_ready, 1)

            steps(pe, [(0, turn), (1, up), (2, down)])

        @block.scalar
        def _(act):
            act.sem_inc(y_copied, AHEAD)

            def y_copy(j, s):
                act.wait_ge(y_ready, j + 1 + AHEAD)
                wait_apart(act, y_stored[s % 2], (j - s % 2) * 8 + 16)
                nc.scalar.activation(y[s % 2][:], py[s % 2][:], ACT.Copy).then_inc(y_copied, 1)

            def x_hi(j, s):
                act.wait_ge(x_turned, j + 1 + AHEAD)
                act.wait_ge(u_ready, j - 1 + AHEAD)
                nc.scalar.activation(xh[s % 2][:], pt[s % 2][:], ACT.Copy).then_inc(xh_ready, 1)

            def down_weights_hi(j, s):
                act.wait_ge(w_in[s], (j - s) * (16 // TURN) + 16)
                act.wait_ge(y_ready, j - 1 + AHEAD)
                nc.scalar.activation(g.wh[s % 2][:, WUP:WN], raw[s][:, WUP:WN], ACT.Copy).then_inc(down_hi, 1)

            def gate(j, s):
                act.wait_ge(g_ready, j + 1)
                act.wait_ge(h_ready, j - 1 + AHEAD)
                nc.scalar.activation(silu[s % 2][:], pgu[s % 2][0][:, 0:P], ACT.Silu,
                                     bias=raw[s][:, WN:WN + 1]).then_inc(s_ready, 1)

            def h_hi(j, s):
                act.wait_ge(h_ready, j + 1 + AHEAD)
                act.wait_ge(y_ready, j - 1 + AHEAD)
                nc.scalar.activation(hh[s % 2][:], h[s % 2][:], ACT.Copy).then_inc(hh_ready, 1)

            steps(act, [(3, y_copy), (0, x_hi), (1, down_weights_hi), (1, gate), (1, h_hi)])

        @block.vector
        def _(dve):
            dve.sem_inc(xl_ready, AHEAD)
            dve.sem_inc(up_lo, AHEAD)
            dve.sem_inc(h_ready, AHEAD)

            def x_lo(j, s):
                dve.wait_ge(xh_ready, j + 1)
                nc.vector.tensor_tensor(xl[s % 2][:], pt[s % 2][:], xh[s % 2][:].bitcast(F32),
                                        ALU.subtract).then_inc(xl_ready, 1)

            def up_weights_lo(j, s):
                dve.wait_ge(up_hi, j + 1)
                nc.vector.tensor_tensor(g.wl[s % 2][:, 0:WUP], raw[s][:, 0:WUP], g.wh[s % 2][:, 0:WUP].bitcast(F32),
                                        ALU.subtract).then_inc(up_lo, 1)

            def hidden(j, s):
                dve.wait_ge(u_ready, j + 1 + AHEAD)
                dve.wait_ge(s_ready, j + 1)
                nc.vector.scalar_tensor_tensor(out=h[s % 2][:], in0=pgu[s % 2][1][:, 0:P], scalar=raw[s][:, WN + 1:WN + 2],
                                               in1=silu[s % 2][:], op0=ALU.add, op1=ALU.mult).then_inc(h_ready, 1)

            def h_lo(j, s):
                dve.wait_ge(hh_ready, j + 1)
                nc.vector.tensor_tensor(hl[s % 2][:], h[s % 2][:], hh[s % 2][:].bitcast(F32),
                                        ALU.subtract).then_inc(hl_ready, 1)

            steps(dve, [(0, x_lo), (0, up_weights_lo), (1, hidden), (1, h_lo)])


def project(nc, a, g):
    with ExitStack() as ctx:
        sb, ps, sem = scoped(nc, ctx, "proj")
        raw = [g.sums[:, k * KC * DIM:(k + 1) * KC * DIM] for k in range(3)]
        wh = [g.wq.hi] + [sb(f"wh{k}", [P, KC * DIM], F32R) for k in (1, 2)]
        wl = [g.wq.lo] + [sb(f"wl{k}", [P, KC * DIM], F32R) for k in (1, 2)]
        hi = sb("hi", [P, 2, NB], F32R)
        lo = sb("lo", [P, 2, NB], F32R)
        v = sb("v", [P, 2, HEADS, VPAD])
        po = [ps(f"po{k}", [P, NB]) for k in range(4)]
        w_in = [sem(f"w_in{k}") for k in range(3)]
        w_hi, w_split, pads, product = sem("w_hi"), sem("w_split"), sem("pads"), sem("product")
        hi_ready, lo_ready, v_ready = sem("hi_ready"), sem("lo_ready"), sem("v_ready")
        stored, v_stored = [sem("stored0"), sem("stored1")], [sem("v_stored0"), sem("v_stored1")]
        QK = 2 * KC * BLOCKS
        block = ctx.enter_context(nc.Block())

        @block.sync
        def _(sp):
            for k in (1, 2):
                sp.dma_start(raw[k].rearrange("p (c e) -> p c e", c=KC),
                             a["wqkvT"][k].rearrange("(c p) e -> p c e", p=P)).then_inc(w_in[k], 16)
            for q in range(QK):
                which, unit = q // (KC * BLOCKS), (q % BLOCKS) * KC + (q // BLOCKS) % KC
                sp.wait_ge(hi_ready, q + 1)
                sp.dma_start(g.qk_dram[which, 0, unit], hi[:, q % 2, :].bitcast(F32)).then_inc(stored[q % 2], 16)
                sp.wait_ge(lo_ready, q + 1)
                sp.dma_start(g.qk_dram[which, 1, unit], lo[:, q % 2, :].bitcast(F32)).then_inc(stored[q % 2], 16)
            for t in range(TILES):
                sp.wait_ge(v_ready, t + 1)
                sp.dma_start(g.v_dram[t], v[:, t % 2].rearrange("p h d -> p (h d)")).then_inc(v_stored[t % 2], 16)
            for k in range(2):
                sp.wait_ge(stored[k], 16 * QK)
                sp.wait_ge(v_stored[k], 16 * TILES // 2)

        @block.gpsimd
        def _(pool):
            nc.gpsimd.memset(v[:], 0.0).then_inc(pads, 1)
            pool.wait_ge(pads, 1)
            nc.gpsimd.memset(v[:, :, :, DK:DK + 1], 1.0).then_inc(pads, 1)
            for k in (1, 2):
                pool.wait_ge(w_in[k], 16)
                nc.gpsimd.tensor_scalar(wh[k][:], raw[k], 1.0, 0.0, ALU.mult, ALU.add).then_inc(w_hi, 1)
                pool.wait_ge(w_hi, k)
                nc.gpsimd.tensor_tensor(wl[k][:], raw[k], wh[k][:].bitcast(F32), ALU.subtract).then_inc(w_split, 1)

        @block.tensor
        def _(pe):
            def bank_free(n):
                if n >= QK + 4:
                    pe.wait_ge(v_ready, n - QK - 3)
                elif n >= 4:
                    pe.wait_ge(lo_ready, n - 3)

            for q in range(QK):
                which, c_out, b = q // (KC * BLOCKS), (q // BLOCKS) % KC, q % BLOCKS
                if q == QK // 2:
                    pe.wait_ge(w_split, 1)
                bank_free(q)
                for c in range(KC):
                    w = slice(c * DIM + c_out * P, c * DIM + (c_out + 1) * P)
                    mm = three(pe, po[q % 4][:], wh[which][:, w], wl[which][:, w], g.XH[:, c, b * NB:(b + 1) * NB],
                               g.XL[:, c, b * NB:(b + 1) * NB], c == 0, c == KC - 1)
                mm.then_inc(product, 1)
            pe.wait_ge(w_split, 2)
            for t in range(TILES):
                bank_free(QK + t)
                for c in range(KC):
                    w = slice(c * DIM, (c + 1) * DIM)
                    cols = slice(t * P, (t + 1) * P)
                    mm = three(pe, po[t % 4][:], g.XH[:, c, cols], g.XL[:, c, cols], wh[2][:, w], wl[2][:, w],
                               c == 0, c == KC - 1)
                mm.then_inc(product, 1)

        @block.scalar
        def _(act):
            for q in range(QK):
                act.wait_ge(product, q + 1)
                if q >= 2:
                    act.wait_ge(stored[q % 2], 32 * (q // 2))
                nc.scalar.activation(hi[:, q % 2, :], po[q % 4][:], ACT.Copy).then_inc(hi_ready, 1)
            act.wait_ge(pads, 2)
            for t in range(TILES):
                act.wait_ge(product, QK + t + 1)
                if t >= 2:
                    act.wait_ge(v_stored[t % 2], 16 * (t // 2))
                nc.scalar.activation(v[:, t % 2, :, 0:DK], po[t % 4][:].rearrange("p (h d) -> p h d", d=DK),
                                     ACT.Copy).then_inc(v_ready, 1)

        @block.vector
        def _(dve):
            for q in range(QK):
                dve.wait_ge(hi_ready, q + 1)
                nc.vector.tensor_tensor(lo[:, q % 2, :], po[q % 4][:], hi[:, q % 2, :].bitcast(F32),
                                        ALU.subtract).then_inc(lo_ready, 1)


def attend(nc, a, g):
    with ExitStack() as ctx:
        sb, ps, sem = scoped(nc, ctx, "att")
        SET = 4
        SETS = HEADS // SET
        RING = 4
        STEPS = 4
        LEAD = 7
        PER_B = SETS * STEPS
        MROW = 96
        qs = [sb(f"qs{k}", [P, SET, NB], F32R) for k in range(RING)]
        ks = [sb(f"ks{k}", [P, SET, NB], F32R) for k in range(RING)]
        v = [sb(f"v{k}", [P, STEPS, SET * VPAD]) for k in range(RING)]
        prob = [sb(f"prob{k}", [P, SET, NB]) for k in range(2)]
        top = [sb(f"top{k}", [P, STEPS, SET]) for k in range(2)]
        mh = [sb(f"mh{k}", [SET, NB], F32R) for k in range(2)]
        ml = [sb(f"ml{k}", [SET, NB], F32R) for k in range(2)]
        o_sb = [sb(f"o_sb{k}", [P, NB]) for k in range(2)]
        rec = sb("rec", [P, STEPS, SET])
        p_first = [ps(f"first{k}", [P, NB]) for k in range(2)]
        p_second = ps("second", [P, SET, NB])
        p_out = ps("out", [P, NB])
        p_turn = ps("turn", [P, NB])
        loaded = [sem(f"loaded{k}") for k in range(RING)]
        v_in = [sem(f"v_in{k}") for k in range(RING)]
        m_in = [sem(f"m_in{k}") for k in range(RING)]
        q_pads, k_pads, first_ready, second_ready, max_turned = sem("q_pads"), sem("k_pads"), sem("first_ready"), sem("second_ready"), sem("max_turned")
        mh_ready, ml_ready, dve_chain = sem("mh_ready"), sem("ml_ready"), sem("dve_chain")
        exp_done, exp_0 = sem("exp_done"), 2
        pv_done, pv_0 = sem("pv_done"), RING * STEPS
        max_done, max_0 = sem("max_done"), 2
        turned_m, turned_0 = sem("turned_m"), 2
        o_copied, copied_0 = sem("o_copied"), 1
        o_turned, o_turned_0 = sem("o_turned"), 2
        o_done, o_done_0 = sem("o_done"), 2
        block = ctx.enter_context(nc.Block())

        def load(sp, b, w):
            slot = w % RING
            sp.wait_ge(pv_done, PER_B * b + STEPS * (w - RING) + STEPS + pv_0)
            unit, half = b * KC + w // 2, w % 2
            for dst, which, parts in ((qs, 0, (0, 0, 1, 1)), (ks, 1, (0, 1, 0, 1))):
                for r, part in enumerate(parts):
                    src = g.qk_dram[which, part, bass.ds(unit, 1), half * SET * DK:(half + 1) * SET * DK, :]
                    sp.dma_start(dst[slot][r * DK:(r + 1) * DK, :, :].bitcast(F32),
                                 src.rearrange("u (h d) t -> d (u h) t", d=DK)).then_inc(loaded[slot], 16)
            cols = slice(SET * VPAD * (w % SETS), SET * VPAD * (w % SETS + 1))
            sp.dma_start(v[slot][:], g.v_dram[bass.ds((b + w // SETS) * STEPS, STEPS), :, cols].rearrange("t p c -> p t c")
                         ).then_inc(v_in[slot], 16)

        def load_max(sp, b, w):
            sp.wait_ge(ml_ready, SETS * b + w + 1)
            for r, src in ((0, mh), (1, ml)):
                rows = slice(MROW + r * SET, MROW + (r + 1) * SET)
                sp.dma_start(qs[w % RING][rows, :, :].bitcast(F32),
                             src[w % 2][:].bitcast(F32).unsqueeze(1).to_broadcast([SET, SET, NB])
                             ).then_inc(m_in[w % RING], 16)

        @block.sync
        def _(sp):
            for w in range(3):
                load(sp, 0, w)
            sp.wait_ge(q_pads, 1)
            load_max(sp, 0, 0)

            def batch(b, last):
                for s in range(SETS):
                    if not (last and s + 3 >= SETS):
                        load(sp, b, s + 3)
                    if not (last and s + 1 >= SETS):
                        load_max(sp, b, s + 1)

            g.wo.load(sp, a["woT"])
            with sp.Fori(0, BATCH - 1) as b:
                batch(b, False)
            batch(BATCH - 1, True)

        @block.gpsimd
        def _(pool):
            for k in range(RING):
                nc.gpsimd.memset(ks[k][64:P, :, :].bitcast(F32), 0.0).then_inc(k_pads, 1)
                pool.wait_ge(k_pads, 3 * k + 1)
                rows = ks[k][MROW:MROW + 2 * SET, :, :]
                for part in range(2):
                    nc.gpsimd.affine_select(out=rows, in_=rows.bitcast(F32), compare_op=ALU.not_equal, fill=1.0, base=-part * SET,
                                            pattern=[[-1, SET], [0, NB]], channel_multiplier=1).then_inc(k_pads, 1)
                    pool.wait_ge(k_pads, 3 * k + 2 + part)
            g.wo.split(pool)

        @block.tensor
        def _(pe):
            pe.sem_inc(pv_done, pv_0)
            pe.sem_inc(turned_m, turned_0)
            pe.sem_inc(o_turned, o_turned_0)

            def first(b, step, item):
                w, n = step // STEPS, (step % STEPS) * 4 + item
                head, qt = n // 4, n % 4
                if n == 0:
                    if isinstance(b, int) and b == 0 and w < RING:
                        pe.wait_ge(q_pads, w + 1)
                        pe.wait_ge(k_pads, 3 * w + 3)
                    pe.wait_ge(loaded[w % RING], 128 * (SETS // RING) * b + 128 * (w // RING + 1))
                m = 4 * step + item
                pe.wait_ge(max_done, 4 * PER_B * b + m - 1 + max_0)
                pe.matmul(p_first[m % 2][:], qs[w % RING][0:MROW, head, qt * P:(qt + 1) * P],
                          ks[w % RING][0:MROW, head, :], start=True, stop=True).then_inc(first_ready, 1)

            def turn_max(b, w):
                pe.wait_ge(max_done, 4 * PER_B * b + 4 * STEPS * (w + 1) + max_0)
                if not (isinstance(b, int) and b == 0 and w == 0):
                    pe.wait_ge(o_done, SETS * b + w - 2 + o_done_0)
                for qt in range(4):
                    mm = pe.transpose(p_turn[0:SET, qt * P:(qt + 1) * P], top[w % 2][:, qt, :], g.ident[:])
                mm.then_inc(turned_m, 1)

            def second(b, step, pair):
                s, kt = step // STEPS, step % STEPS
                if kt == 0 and pair == 0:
                    pe.wait_ge(m_in[s % RING], 32 * (SETS // RING) * b + 32 * (s // RING + 1))
                pe.wait_ge(exp_done, 2 * (PER_B * b + step - 1) + pair + 1 + exp_0)
                for j in range(2 * pair, 2 * pair + 2):
                    mm = pe.matmul(p_second[:, j, :], ks[s % RING][:, j, kt * P:(kt + 1) * P], qs[s % RING][:, j, :],
                                   start=True, stop=True)
                mm.then_inc(second_ready, 1)

            def weigh(b, step):
                s, kt = step // STEPS, step % STEPS
                if kt == 0:
                    pe.wait_ge(v_in[s % RING], 16 * (SETS // RING) * b + 16 * (s // RING + 1))
                    pe.wait_ge(o_copied, SETS * b + s + copied_0)
                pe.wait_ge(exp_done, 2 * (PER_B * b + step) + 2 + exp_0)
                for j in range(SET):
                    mm = pe.matmul(p_out[VPAD * j:VPAD * (j + 1), :], v[s % RING][:, kt, VPAD * j:VPAD * (j + 1)],
                                   prob[step % 2][:, j, :], start=(kt == 0), stop=(kt == STEPS - 1))
                mm.then_inc(pv_done, 1)

            def turn_out(b, s, maxima):
                pe.wait_ge(o_copied, SETS * b + s + 1 + copied_0)
                if maxima:
                    pe.wait_ge(ml_ready, SETS * b + s + 3)
                else:
                    pe.wait_ge(o_done, SETS * b + s + o_done_0)
                for qt in range(4):
                    mm = pe.transpose(p_turn[:, qt * P:(qt + 1) * P], o_sb[s % 2][:, qt * P:(qt + 1) * P], g.ident[:])
                mm.then_inc(o_turned, 1)

            for step in range(LEAD):
                for item in range(4):
                    first(0, step, item)
                if step == STEPS:
                    turn_max(0, 0)

            def batch(b, begin, last):
                for step in range(PER_B):
                    ahead = not (last and step + LEAD >= PER_B)
                    s, kt = step // STEPS, step % STEPS
                    second(b, step, 0)
                    if ahead:
                        first(b, step + LEAD, 0)
                    second(b, step, 1)
                    if ahead:
                        first(b, step + LEAD, 1)
                    if not (begin and step == 0):
                        weigh(b, step - 1)
                    if ahead:
                        first(b, step + LEAD, 2)
                        first(b, step + LEAD, 3)
                    maxima = not (last and s + 1 >= SETS)
                    if kt == 1 and maxima:
                        turn_max(b, s + 1)
                    if kt == 2 and not (begin and s == 0):
                        turn_out(b, s - 1, maxima)

            batch(0, True, False)
            with pe.Fori(1, BATCH - 1) as b:
                batch(b, False, False)
            batch(BATCH - 1, False, True)
            weigh(BATCH - 1, PER_B - 1)
            turn_out(BATCH - 1, SETS - 1, False)

        @block.scalar
        def _(act):
            act.sem_inc(exp_done, exp_0)
            act.sem_inc(o_copied, copied_0)

            def exps(b, step, pair):
                act.wait_ge(second_ready, 2 * (PER_B * b + step) + pair + 1)
                act.wait_ge(pv_done, PER_B * b + step - 1 + pv_0)
                js = slice(2 * pair, 2 * pair + 2)
                nc.scalar.activation(prob[step % 2][:, js, :], p_second[:, js, :], ACT.Exp,
                                     scale=DK ** -0.5).then_inc(exp_done, 1)

            def high_max(b, w):
                act.wait_ge(turned_m, SETS * b + w + 1 + turned_0)
                nc.scalar.activation(mh[w % 2][:], p_turn[0:SET, :], ACT.Copy, scale=-1.0).then_inc(mh_ready, 1)

            def copy_out(b, s):
                act.wait_ge(pv_done, PER_B * b + STEPS * (s + 1) + pv_0)
                act.wait_ge(o_turned, SETS * b + s - 1 + o_turned_0)
                nc.scalar.activation(o_sb[s % 2][:], p_out[:], ACT.Copy).then_inc(o_copied, 1)

            high_max(0, 0)

            def batch(b, begin, last):
                for step in range(PER_B):
                    s, kt = step // STEPS, step % STEPS
                    exps(b, step, 0)
                    if kt == 2 and not (last and s + 1 >= SETS):
                        high_max(b, s + 1)
                    exps(b, step, 1)
                    if kt == 0 and not (begin and s == 0):
                        copy_out(b, s - 1)

            batch(0, True, False)
            with act.Fori(1, BATCH - 1) as b:
                batch(b, False, False)
            batch(BATCH - 1, False, True)
            copy_out(BATCH - 1, SETS - 1)

        @block.vector
        def _(dve):
            dve.sem_inc(max_done, max_0)
            dve.sem_inc(o_done, o_done_0)

            def maximum(b, step, item):
                w, n = step // STEPS, (step % STEPS) * 4 + item
                head, qt = n // 4, n % 4
                m = 4 * step + item
                if n == 0:
                    dve.wait_ge(turned_m, SETS * b + w - 1 + turned_0)
                dve.wait_ge(first_ready, 4 * PER_B * b + m + 1)
                nc.vector.tensor_reduce(top[w % 2][:, qt, head:head + 1], p_first[m % 2][:], AX.X,
                                        ALU.max).then_inc(max_done, 1)

            def low_max(b, w):
                dve.wait_ge(mh_ready, SETS * b + w + 1)
                nc.vector.scalar_tensor_tensor(out=ml[w % 2][:], in0=p_turn[0:SET, :], scalar=-1.0,
                                               in1=mh[w % 2][:].bitcast(F32), op0=ALU.mult,
                                               op1=ALU.subtract).then_inc(ml_ready, 1)

            def divide(b, s):
                dve.wait_ge(o_turned, SETS * b + s + 1 + o_turned_0)
                o = p_turn[:].rearrange("p (t h d) -> p t h d", t=STEPS, h=SET)
                nc.vector.reciprocal(rec[:].unsqueeze(3), o[:, :, :, DK:DK + 1]).then_inc(dve_chain, 1)
                dve.wait_ge(dve_chain, SETS * b + s + 1)
                tile = (b + s // SETS) * PER_BLOCK
                at = (s % SETS) * SET * DK
                dst = g.Y[:, bass.ds(tile, PER_BLOCK), at:at + SET * DK].rearrange("p t (h d) -> p t h d", d=DK)
                nc.vector.tensor_tensor(dst, o[:, :, :, 0:DK], rec[:].unsqueeze(3).to_broadcast([P, STEPS, SET, DK]),
                                        ALU.mult).then_inc(o_done, 1)

            for step in range(LEAD):
                if step < RING:
                    nc.vector.memset(qs[step][64:P, :, :].bitcast(F32), 0.0).then_inc(q_pads, 1)
                for item in range(4):
                    maximum(0, step, item)
                if step == STEPS:
                    low_max(0, 0)

            def batch(b, begin, last):
                for step in range(PER_B):
                    s, kt = step // STEPS, step % STEPS
                    ahead = not (last and step + LEAD >= PER_B)
                    for item in range(4):
                        if ahead:
                            maximum(b, step + LEAD, item)
                        if item == 1 and kt == 2 and not (last and s + 1 >= SETS):
                            low_max(b, s + 1)
                        if item == 1 and kt == 3 and not (begin and s == 0):
                            divide(b, s - 1)

            batch(0, True, False)
            with dve.Fori(1, BATCH - 1) as b:
                batch(b, False, False)
            batch(BATCH - 1, False, True)
            divide(BATCH - 1, SETS - 1)


def attention_out(nc, a, g):
    with ExitStack() as ctx:
        sb, ps, sem = scoped(nc, ctx, "wo")
        wh, wl = g.wo.hi, g.wo.lo
        th = sb("th", [P, 2, KC, P], F32R)
        tl = sb("tl", [P, 2, KC, P], F32R)
        pt = [ps(f"pt{k}", [P, KC, P]) for k in range(2)]
        po = [ps(f"po{k}", [P, DIM]) for k in range(2)]
        turned, hi_ready, lo_ready, product, added = (sem("turned"), sem("hi_ready"), sem("lo_ready"), sem("product"),
                                                      sem("added"))
        block = ctx.enter_context(nc.Block())

        @block.tensor
        def _(pe):
            for t in range(TILES + 1):
                if t < TILES:
                    if t >= 2:
                        pe.wait_ge(lo_ready, t - 1)
                    for c in range(KC):
                        mm = pe.transpose(pt[t % 2][:, c, :], g.Y[:, t, c * P:(c + 1) * P], g.ident[:])
                    mm.then_inc(turned, 1)
                if t:
                    m = t - 1
                    if m >= 2:
                        pe.wait_ge(added, m - 1)
                    pe.wait_ge(lo_ready, m + 1)
                    for c in range(KC):
                        w = slice(c * DIM, (c + 1) * DIM)
                        mm = three(pe, po[m % 2][:], th[:, m % 2, c, :], tl[:, m % 2, c, :], wh[:, w], wl[:, w],
                                   c == 0, c == KC - 1)
                    mm.then_inc(product, 1)

        @block.scalar
        def _(act):
            for t in range(TILES):
                act.wait_ge(turned, t + 1)
                if t >= 2:
                    act.wait_ge(product, t - 1)
                nc.scalar.activation(th[:, t % 2], pt[t % 2][:], ACT.Copy).then_inc(hi_ready, 1)

        @block.vector
        def _(dve):
            for t in range(TILES + 1):
                if t < TILES:
                    dve.wait_ge(hi_ready, t + 1)
                    nc.vector.tensor_tensor(tl[:, t % 2], pt[t % 2][:], th[:, t % 2].bitcast(F32),
                                            ALU.subtract).then_inc(lo_ready, 1)
                if t:
                    m = t - 1
                    dve.wait_ge(product, m + 1)
                    nc.vector.tensor_tensor(g.Y[:, m, :], po[m % 2][:], g.X[:, m, :], ALU.add).then_inc(added, 1)


class PairWeights:

    PAIR = 2 * P
    W13 = KC * 2 * PAIR
    WN = W13 + 2 * DIM

    def __init__(self, nc, ctx, a):
        sb, _, sem = scoped(nc, ctx, "pairs")
        self.a = a
        self.scales = sb("scales", [P, FPAIRS, self.WN // P])
        self.raw = sb("raw", [P, self.WN])
        self.wh = [sb(f"wh{s}", [P, self.WN], F32R) for s in range(2)]
        self.wl = [sb(f"wl{s}", [P, self.WN], F32R) for s in range(2)]
        self.w_in, self.sc_in, self.chain, self.split_ready = sem("w_in"), sem("sc_in"), sem("chain"), sem("split_ready")

    def first_loads(self, sp):
        sp.dma_start(self.scales[:], self.a["scales"].partition_broadcast(P)).then_inc(self.sc_in, 16)
        self.load(sp, 0)

    def first_split(self, pool):
        pool.wait_ge(self.sc_in, 16)
        self.scale(pool, 0)
        self.split(pool, 0, 0)

    def load(self, sp, p):
        sp.dma_start(self.raw[:], self.a["w132"][p]).then_inc(self.w_in, 16)

    def scale(self, pool, p):
        wait_apart(pool, self.w_in, 16 * p + 16)
        blocks = self.raw[:].rearrange("p (n k) -> p n k", k=P)
        sc = self.scales[:, bass.ds(p, 1), :].rearrange("p a n -> p (a n)").unsqueeze(2).to_broadcast([P, self.WN // P, P])
        pool.tensor_tensor(blocks, blocks, sc, ALU.mult).then_inc(self.chain, 1)
        pool.wait_ge(self.chain, 2 * p + 1)

    def split(self, pool, p, s):
        pool.tensor_scalar(self.wh[s][:], self.raw[:], 1.0, 0.0, ALU.mult, ALU.add).then_inc(self.chain, 1)
        pool.wait_ge(self.chain, 2 * p + 2)
        pool.tensor_tensor(self.wl[s][:], self.raw[:], self.wh[s][:].bitcast(F32), ALU.subtract).then_inc(self.split_ready, 1)


def quantised_mlp(nc, a, g):
    with ExitStack() as ctx:
        sb, ps, sem = scoped(nc, ctx, "ffn")
        f = g.pair_weights
        PAIR, W13, wh, wl = f.PAIR, f.W13, f.wh, f.wl
        silu = sb("silu", [P, 2, PAIR])
        h = sb("h", [P, PAIR])
        hq = sb("hq", [P, 2, PAIR])
        amax = sb("amax", [P, 2])
        scale = sb("scale", [P, 2])
        inv = sb("inv", [P, 2])
        hh = sb("hh", [P, 2, 2, P], F32R)
        hl = sb("hl", [P, 2, 2, P], F32R)
        pg = [ps(f"pg{k}", [P, 2 * PAIR]) for k in range(2)]
        pt = [ps(f"pt{k}", [P, 2, P]) for k in range(2)]
        py = [ps(f"py{k}", [P, DIM]) for k in range(2)]
        dve_chain = sem("dve_chain")
        g_ready, s_ready, hh_ready = sem("g_ready"), sem("s_ready"), sem("hh_ready")
        u_used, used_0 = sem("u_used"), 2
        turned, turned_0 = sem("turned"), 2
        hq_ready, hq_0 = sem("hq_ready"), 2
        hl_ready, hl_0 = sem("hl_ready"), 2
        y_ready, y_0 = sem("y_ready"), 2 * TILES
        y_added, added_0 = sem("y_added"), TILES
        block = ctx.enter_context(nc.Block())

        def pairs(eng, body):
            with eng.Fori(0, FPAIRS // 2) as i:
                for s in range(2):
                    body(2 * i + s, s)
            body(FPAIRS - 1, 0)

        def after_first(eng, body):
            with eng.Fori(0, FPAIRS // 2) as i:
                for s in range(2):
                    body(2 * i + 1 + s, (1 + s) % 2)

        @block.sync
        def _(sp):
            def fetch(p, s):
                sp.wait_ge(f.split_ready, p)
                f.load(sp, p)

            after_first(sp, fetch)

        @block.gpsimd
        def _(pool):
            def split(p, s):
                f.scale(pool, p)
                wait_apart(pool, y_ready, (p - 1) * TILES + y_0)
                f.split(pool, p, s)

            after_first(pool, split)

        @block.tensor
        def _(pe):
            pe.sem_inc(y_ready, y_0)
            pe.sem_inc(turned, turned_0)

            def pair(p, s):
                def up(t):
                    pe.wait_ge(u_used, TILES * p + t - 1 + used_0)
                    for c in range(KC):
                        w = slice(c * 2 * PAIR, (c + 1) * 2 * PAIR)
                        cols = slice(t * P, (t + 1) * P)
                        mm = three(pe, pg[t % 2][:], g.XH[:, c, cols], g.XL[:, c, cols], wh[s][:, w], wl[s][:, w],
                                   c == 0, c == KC - 1)
                    mm.then_inc(g_ready, 1)

                def turn(t):
                    pe.wait_ge(hq_ready, TILES * p + t + 1 + hq_0)
                    pe.wait_ge(hl_ready, TILES * p + t - 1 + hl_0)
                    for i in range(2):
                        mm = pe.transpose(pt[t % 2][:, i, :], hq[:, t % 2, i * P:(i + 1) * P], g.ident[:])
                    mm.then_inc(turned, 1)

                def down(t):
                    pe.wait_ge(hl_ready, TILES * p + t + 1 + hl_0)
                    pe.wait_ge(y_added, TILES * p + t - 1 + added_0)
                    for i in range(2):
                        w = slice(W13 + i * DIM, W13 + (i + 1) * DIM)
                        mm = three(pe, py[t % 2][:], hh[:, t % 2, i, :], hl[:, t % 2, i, :], wh[s][:, w], wl[s][:, w],
                                   i == 0, i == 1)
                    mm.then_inc(y_ready, 1)

                pe.wait_ge(f.split_ready, p + 1)
                for t in range(TILES + 2):
                    if t < TILES:
                        up(t)
                    if 1 <= t <= TILES:
                        turn(t - 1)
                    if t >= 2:
                        down(t - 2)

            pairs(pe, pair)

        @block.scalar
        def _(act):
            def pair(p, s):
                for t in range(TILES + 1):
                    if t < TILES:
                        act.wait_ge(g_ready, TILES * p + t + 1)
                        act.wait_ge(u_used, TILES * p + t - 1 + used_0)
                        nc.scalar.activation(silu[:, t % 2, :], pg[t % 2][:, 0:PAIR], ACT.Silu).then_inc(s_ready, 1)
                    if t:
                        m = t - 1
                        act.wait_ge(turned, TILES * p + m + 1 + turned_0)
                        act.wait_ge(y_ready, TILES * p + m - 1 + y_0)
                        nc.scalar.activation(hh[:, m % 2], pt[m % 2][:], ACT.Copy).then_inc(hh_ready, 1)

            pairs(act, pair)

        @block.vector
        def _(dve):
            own = Chain(dve, dve_chain)
            dve.sem_inc(u_used, used_0)
            dve.sem_inc(hq_ready, hq_0)
            dve.sem_inc(hl_ready, hl_0)
            dve.sem_inc(y_added, added_0)
            PER_TILE = 4

            def pair(p, s):
                def hidden(t):
                    n = TILES * p + t
                    own.base, own.n = PER_TILE * n, 0
                    dve.wait_ge(s_ready, n + 1)
                    dve.wait_ge(hq_ready, n + hq_0)
                    nc.vector.tensor_tensor(h[:], pg[t % 2][:, PAIR:2 * PAIR], silu[:, t % 2, :],
                                            ALU.mult).then_inc(u_used, 1)
                    dve.wait_ge(u_used, n + 1 + used_0)
                    own.step(nc.vector.tensor_reduce(amax[:], h[:].rearrange("p (i k) -> p i k", k=P), AX.X, ALU.max,
                                                     apply_absolute_value=True))
                    own.settle()
                    own.step(nc.vector.tensor_scalar(scale[:], amax[:], 1.0 / FP8_MAX, 1e-12, ALU.mult, ALU.add))
                    own.settle()
                    own.step(nc.vector.reciprocal(inv[:], scale[:]))
                    own.settle()
                    dve.wait_ge(turned, n - 1 + turned_0)
                    own.step(nc.vector.tensor_scalar(hq[:, t % 2, 0:P], h[:, 0:P], inv[:, 0:1], scale[:, 0:1],
                                                     ALU.mult, ALU.mult))
                    nc.vector.tensor_scalar(hq[:, t % 2, P:PAIR], h[:, P:PAIR], inv[:, 1:2], scale[:, 1:2],
                                            ALU.mult, ALU.mult).then_inc(hq_ready, 1)

                def low(t):
                    dve.wait_ge(hh_ready, TILES * p + t + 1)
                    nc.vector.tensor_tensor(hl[:, t % 2], pt[t % 2][:], hh[:, t % 2].bitcast(F32),
                                            ALU.subtract).then_inc(hl_ready, 1)

                def add(t):
                    dve.wait_ge(y_ready, TILES * p + t + 1 + y_0)
                    dve.wait_ge(y_added, TILES * (p - 1) + t + 1 + added_0)
                    nc.vector.tensor_tensor(g.Y[:, t, :], py[t % 2][:], g.Y[:, t, :], ALU.add).then_inc(y_added, 1)

                for t in range(TILES + 2):
                    if t < TILES:
                        hidden(t)
                    if 1 <= t <= TILES:
                        low(t - 1)
                    if t >= 2:
                        add(t - 2)

            pairs(dve, pair)


class Shared:
    pass


def program(nc, a, out):
    g = Shared()
    g.brow_dram = nc.dram_tensor("brow_dram", [STATE, BATCH, NB], F32, kind="Internal").ap()
    g.qk_dram = nc.dram_tensor("qk_dram", [2, 2, UNITS, P, NB], F32, kind="Internal").ap()
    g.v_dram = nc.dram_tensor("v_dram", [TILES, P, HEADS * VPAD], F32, kind="Internal").ap()
    g.sorted_x = nc.dram_tensor("sorted_x", [SORTED * P, DIM], F32, kind="Internal").ap()
    g.sorted_y = nc.dram_tensor("sorted_y", [SORTED * P, DIM], F32, kind="Internal").ap()
    with ExitStack() as ctx:
        sb, _, sem = scoped(nc, ctx, "all")
        g.ident = sb("ident", [P, P])
        g.gate = sb("gate", [P, MLPS, TILES])
        g.weight, g.at = sb("weight", [P, TOP, TILES]), sb("at", [P, TOP, TILES], mybir.dt.int32)
        g.owner = sb("owner", [1, SORTED], mybir.dt.int32)
        sums = sb("sums", [P, KC * TOK])
        g.sums = sums
        g.XT = sums[:].rearrange("p (c t) -> p c t", c=KC)
        g.Y = sums[:].rearrange("p (t d) -> p t d", t=TILES)
        g.X = sb("X", [P, TILES, DIM])
        with ExitStack() as ssm:
            sb, _, _ = scoped(nc, ssm, "ssm")
            g.sel = sb("sel", [STATE, STATE, P])
            g.A = sb("A", [P, KC, STATE])
            g.D1 = sb("D1", [P, KC])
            g.DT = sb("DT", [P, KC, TOK])
            g.U = sb("U", [P, KC, TOK])
            g.CT = sb("CT", [STATE, TOK])
            ssm_inputs(nc, a, g)
            ssm_scan(nc, a, g)
        with ExitStack() as later:
            sb, _, _ = scoped(nc, later, "later")
            g.XH = sb("XH", [P, KC, TOK], F32R)
            g.XL = sb("XL", [P, KC, TOK], F32R)
            normalise(nc, g, "ln1", True)
            with ExitStack() as moe:
                sb, _, sem = scoped(nc, moe, "mlps")
                g.raw = [sb(f"raw{s}", [P, WN + 2]) for s in range(2)]
                g.wh = [sb(f"wh{s}", [P, WN], F32R) for s in range(2)]
                g.wl = [sb(f"wl{s}", [P, WN], F32R) for s in range(2)]
                g.shared_in, g.shared_split = [sem("shared_in0"), sem("shared_in1")], sem("shared_split")
                route_and_share(nc, a, g)
                sorted_experts(nc, a, g)
            with ExitStack() as first:
                g.wq = Ahead(nc, first, "wq")
                normalise(nc, g, "ln2", False, gather=True, ahead=(lambda sp: g.wq.load(sp, a["wqkvT"][0]), g.wq.split))
                project(nc, a, g)
        with ExitStack() as last:
            g.wo = Ahead(nc, last, "wo_ahead")
            attend(nc, a, g)
            attention_out(nc, a, g)
        with ExitStack() as later:
            sb, _, _ = scoped(nc, later, "last")
            g.XH = sb("XH", [P, KC, TOK], F32R)
            g.XL = sb("XL", [P, KC, TOK], F32R)
            g.pair_weights = PairWeights(nc, later, a)
            normalise(nc, g, "ln3", False, quantise=True,
                      ahead=(g.pair_weights.first_loads, g.pair_weights.first_split))
            quantised_mlp(nc, a, g)
        normalise(nc, g, "ln4", False, out)


def laid_out(x):
    import numpy as np

    def dense(v):
        return np.ascontiguousarray(v)

    def columns(v):
        return dense(v.reshape(-1, P).T)

    def halves(w):
        return w.reshape(DIM, 2, INTER).transpose(1, 0, 2)

    def folded(w):
        return w.reshape(MLPS, KC, P, INTER).transpose(0, 2, 1, 3).reshape(MLPS, P, KC * INTER)

    def by_pair(w):
        return w.T.reshape(KC, P, FPAIRS, 2 * P)

    w1 = np.concatenate([x["L0_ffn_ew1"], halves(x["L0_ffn_sw1"])])
    w2 = np.concatenate([x["L0_ffn_ew2"], halves(x["L0_ffn_sw2"])])
    w3 = np.concatenate([x["L0_ffn_ew3"], x["L0_ffn_sw3"].reshape(2, INTER, DIM)])
    b1 = np.concatenate([x["L0_ffn_eb1"], x["L0_ffn_sb1"].reshape(2, INTER)])
    b2 = np.concatenate([x["L0_ffn_eb2"], x["L0_ffn_sb2"].reshape(2, INTER)])
    b3 = np.concatenate([x["L0_ffn_eb3"], x["L0_ffn_sb3"].reshape(1, DIM), np.zeros((1, DIM), np.float32)])
    w13 = np.stack([by_pair(x["L1_ffn_w1"]), by_pair(x["L1_ffn_w3"])], 3)
    w13 = w13.transpose(2, 1, 0, 3, 4).reshape(FPAIRS, P, KC * 4 * P)
    down = x["L1_ffn_w2"].T.reshape(FPAIRS, 2, P, DIM).transpose(0, 2, 1, 3).reshape(FPAIRS, P, 2 * DIM)
    s1, s3 = (x[n].reshape(FPAIRS, 2, KC) for n in ("L1_ffn_w1_scale", "L1_ffn_w3_scale"))
    s13 = np.stack([s1, s3], 1).transpose(0, 3, 1, 2).reshape(FPAIRS, 4 * KC)
    s2 = x["L1_ffn_w2_scale"].T.reshape(FPAIRS, 2 * KC)
    return {
        "xT": dense(x["L0_attn_x"].reshape(TOK, DIM).T),
        "xprojT": dense(x["L0_attn_x_proj_w"].T),
        "dtprojT": dense(x["L0_attn_dt_proj_w"].T),
        "dtb": columns(x["L0_attn_dt_proj_b"]),
        "alog": dense(x["L0_attn_A_log"]),
        "dcoef": columns(x["L0_attn_D"]),
        "router_w": dense(x["L0_ffn_router_w"]),
        "router_b": dense(x["L0_ffn_router_b"]),
        "router_bias": dense(x["L0_ffn_router_bias"]),
        "order": np.arange(EXPERTS, 0, -1, dtype=np.float32),
        "inner": np.tile(np.arange(TILES) > 0, EXPERTS).astype(np.float32).reshape(EXPERTS, TILES),
        "steps": np.arange(TILES, dtype=np.float32) * P,
        "before": np.tri(EXPERTS, k=-1, dtype=np.float32),
        "tile_no": np.arange(SORTED, dtype=np.float32),
        "w123": dense(np.concatenate([folded(w1), folded(w2), w3, b1[:, :, None], b2[:, :, None]], axis=2)),
        "b3": b3,
        "wqkvT": dense(np.stack([x[f"L1_attn_w_{n}"].T for n in "qkv"])),
        "woT": dense(x["L1_attn_w_o"].T),
        "w132": dense(np.concatenate([w13, down], axis=2)),
        "scales": dense(np.concatenate([s13, s2], axis=1)),
    }


def kernel(**inputs):
    import numpy as np
    import concourse.bacc as bacc
    from concourse.bass_utils import run_bass_kernel_spmd

    nc = bacc.Bacc("TRN2", target_bir_lowering=False, num_devices=1)
    arrays = laid_out({n: np.asarray(v) for n, v in inputs.items()})
    aps = {n: nc.dram_tensor(f"in_{n}", v.shape, mybir.dt.from_np(v.dtype), kind="ExternalInput").ap()
           for n, v in arrays.items()}
    out = nc.dram_tensor("out_x", (TOK, DIM), F32, kind="ExternalOutput").ap()
    program(nc, aps, out)
    result = run_bass_kernel_spmd(nc, [{f"in_{n}": v for n, v in arrays.items()}], core_ids=[0])
    return result.results[0]["out_x"].reshape(BATCH, SEQ, DIM)
```
